# Optimizing a Trainium2 kernel written in Bass

```python
import numpy as np
import jax
import jax.numpy as jnp

def _softmax(x, axis=-1):
    return jax.nn.softmax(x, axis=axis)

def _gelu(x):
    return jax.nn.gelu(x, approximate=True)

def _silu(x):
    return jax.nn.silu(x)

def _sigmoid(x):
    return jax.nn.sigmoid(x)

def _layernorm(x, axis=-1, eps=1e-05):
    m = jnp.mean(x, axis=axis, keepdims=True)
    v = jnp.var(x, axis=axis, keepdims=True)
    return (x - m) / jnp.sqrt(v + eps)

def _scatter_add(tgt, idx, src, axis=0):
    return tgt.at[idx].add(src)

def _segment_sum(src, seg, n):
    return jax.ops.segment_sum(src, seg, n)
kernel_name = 'mk_gnn_preln_d2_gnn_r8_59654a'

def setup_inputs(seed: int=0):
    np.random.seed(seed)
    _w = jnp.asarray

    def _rec_inputs():
        import jax
        import jax.numpy as jnp
        _gk = jax.random.key(seed)
        x = -0.0005121 + 1.001 * jax.random.normal(jax.random.fold_in(_gk, 1), (6250, 64), jnp.float32)
        src = jax.random.randint(jax.random.fold_in(_gk, 2), (200000,), 0, 6250, jnp.int32)
        dst = jax.random.randint(jax.random.fold_in(_gk, 3), (200000,), 0, 6250, jnp.int32)
        _o = jnp.argsort(dst, stable=True)
        src = src[_o]
        dst = dst[_o]
        edge_attr_8 = jax.random.uniform(jax.random.fold_in(_gk, 12), (200000, 8), jnp.float32, 0.0, 1)
        edge_attr_9 = 0.00031416 + 0.999952 * jax.random.normal(jax.random.fold_in(_gk, 13), (200000, 9), jnp.float32)
        return (x, src, dst, edge_attr_8, edge_attr_9)
    x, src, dst, edge_attr_8, edge_attr_9 = _rec_inputs()

    def _L0_gnn_setup():
        import jax, jax.numpy as jnp
        import numpy as np
        N = 6250
        E = 150000
        D_IN = 64
        D_H = 64
        L = 3
        TAU = 1.0
        EPS = 1e-30
        LN_EPS = 1e-05
        ALPHA = 0.5

        def scatter_logsumexp(src, index, n, tau=TAU, eps=EPS):
            scaled = src.astype(jnp.float32) / tau
            max_val = jax.ops.segment_max(scaled, index, num_segments=n)
            exp_val = jnp.exp(scaled - max_val[index])
            sum_exp = jax.ops.segment_sum(exp_val, index, num_segments=n)
            deg = jnp.bincount(index, length=n)
            has_nbr = (deg > 0)[:, None]
            max_safe = jnp.where(has_nbr, max_val, 0.0)
            out = tau * (max_safe + jnp.log(jnp.maximum(sum_exp, eps)))
            return jnp.where(has_nbr, out, 0.0).astype(src.dtype)

        def layer_norm(h, gamma, beta):
            mu = jnp.mean(h, axis=-1, keepdims=True)
            var = jnp.var(h, axis=-1, keepdims=True)
            return (h - mu) * jax.lax.rsqrt(var + LN_EPS) * gamma + beta
        key = jax.random.key(seed)
        ks = jax.random.split(key, 8)
        x = jax.random.normal(ks[0], (N, D_IN), dtype=jnp.float32)
        edge_src = jax.random.randint(ks[1], (E,), 0, N)
        edge_dst = jax.random.randint(ks[2], (E,), 0, N)
        s_in = 1.0 / np.sqrt(D_IN)
        s_l = 1.0 / np.sqrt(2 * D_H)
        W_in = jax.random.uniform(ks[3], (D_H, D_IN), minval=-s_in, maxval=s_in, dtype=jnp.float32)
        b_in = jax.random.uniform(ks[4], (D_H,), minval=-s_in, maxval=s_in, dtype=jnp.float32)
        W_l = jax.random.uniform(ks[5], (L, D_H, 2 * D_H), minval=-s_l, maxval=s_l, dtype=jnp.float32)
        b_l = jax.random.uniform(ks[6], (L, D_H), minval=-s_l, maxval=s_l, dtype=jnp.float32)
        gamma_l = jnp.ones((L, D_H), dtype=jnp.float32)
        beta_l = jnp.zeros((L, D_H), dtype=jnp.float32)
        return {'x': x, 'edge_src': edge_src, 'edge_dst': edge_dst, 'W_in': W_in, 'b_in': b_in, 'W_l': W_l, 'b_l': b_l, 'gamma_l': gamma_l, 'beta_l': beta_l}
    _L0_gnn_all = _L0_gnn_setup()
    _L0_gnn_in = {k: v for k, v in _L0_gnn_all.items() if k in ('W_in', 'b_in', 'W_l', 'b_l', 'gamma_l', 'beta_l')}
    del _L0_gnn_all

    def _L1_gnn_setup():
        import jax, jax.numpy as jnp
        import numpy as np
        N_NODES = 6250
        N_EDGES = 100000
        NODE_DIM = 64
        SH_DIM = 9
        RADIAL_DIM = 8
        HIDDEN_DIM = 128
        LN_EPS = 1e-05

        def _linear_init(key, fan_in, fan_out):
            kw, kb = jax.random.split(key)
            bound = 1.0 / np.sqrt(fan_in)
            W = jax.random.uniform(kw, (fan_in, fan_out), minval=-bound, maxval=bound, dtype=jnp.float32)
            b = jax.random.uniform(kb, (fan_out,), minval=-bound, maxval=bound, dtype=jnp.float32)
            return (W, b)

        def _layernorm(x, g, b):
            mu = jnp.mean(x, axis=-1, keepdims=True)
            var = jnp.var(x, axis=-1, keepdims=True)
            return (x - mu) * jax.lax.rsqrt(var + LN_EPS) * g + b
        key = jax.random.key(seed)
        ks = jax.random.split(key, 12)
        node_feats = jax.random.normal(ks[0], (N_NODES, NODE_DIM), dtype=jnp.float32)
        edge_index = jax.random.randint(ks[1], (2, N_EDGES), 0, N_NODES, dtype=jnp.int64)
        edge_sh = jax.random.normal(ks[2], (N_EDGES, SH_DIM), dtype=jnp.float32)
        edge_radial = jax.random.uniform(ks[3], (N_EDGES, RADIAL_DIM), dtype=jnp.float32)
        msg_in = NODE_DIM + SH_DIM + RADIAL_DIM
        W1, b1 = _linear_init(ks[4], msg_in, HIDDEN_DIM)
        W2, b2 = _linear_init(ks[5], HIDDEN_DIM, HIDDEN_DIM)
        W3, b3 = _linear_init(ks[6], HIDDEN_DIM, NODE_DIM)
        U1, ub1 = _linear_init(ks[7], 2 * NODE_DIM, HIDDEN_DIM)
        ln1_g = jnp.ones((HIDDEN_DIM,), jnp.float32)
        ln1_b = jnp.zeros((HIDDEN_DIM,), jnp.float32)
        U2, ub2 = _linear_init(ks[8], HIDDEN_DIM, NODE_DIM)
        ln2_g = jnp.ones((NODE_DIM,), jnp.float32)
        ln2_b = jnp.zeros((NODE_DIM,), jnp.float32)
        G, gb = _linear_init(ks[9], 2 * NODE_DIM, NODE_DIM)
        return dict(node_feats=node_feats, edge_index=edge_index, edge_sh=edge_sh, edge_radial=edge_radial, W1=W1, b1=b1, W2=W2, b2=b2, W3=W3, b3=b3, U1=U1, ub1=ub1, ln1_g=ln1_g, ln1_b=ln1_b, U2=U2, ub2=ub2, ln2_g=ln2_g, ln2_b=ln2_b, G=G, gb=gb)
    _L1_gnn_all = _L1_gnn_setup()
    _L1_gnn_in = {k: v for k, v in _L1_gnn_all.items() if k in ('W1', 'b1', 'W2', 'b2', 'W3', 'b3', 'U1', 'ub1', 'ln1_g', 'ln1_b', 'U2', 'ub2', 'ln2_g', 'ln2_b', 'G', 'gb')}
    del _L1_gnn_all
    return {'x': x, 'src': src, 'dst': dst, 'edge_attr_8': edge_attr_8, 'edge_attr_9': edge_attr_9, 'L0_gnn_W_in': _L0_gnn_in['W_in'], 'L0_gnn_b_in': _L0_gnn_in['b_in'], 'L0_gnn_W_l': _L0_gnn_in['W_l'], 'L0_gnn_b_l': _L0_gnn_in['b_l'], 'L0_gnn_gamma_l': _L0_gnn_in['gamma_l'], 'L0_gnn_beta_l': _L0_gnn_in['beta_l'], 'L1_gnn_W1': _L1_gnn_in['W1'], 'L1_gnn_b1': _L1_gnn_in['b1'], 'L1_gnn_W2': _L1_gnn_in['W2'], 'L1_gnn_b2': _L1_gnn_in['b2'], 'L1_gnn_W3': _L1_gnn_in['W3'], 'L1_gnn_b3': _L1_gnn_in['b3'], 'L1_gnn_U1': _L1_gnn_in['U1'], 'L1_gnn_ub1': _L1_gnn_in['ub1'], 'L1_gnn_ln1_g': _L1_gnn_in['ln1_g'], 'L1_gnn_ln1_b': _L1_gnn_in['ln1_b'], 'L1_gnn_U2': _L1_gnn_in['U2'], 'L1_gnn_ub2': _L1_gnn_in['ub2'], 'L1_gnn_ln2_g': _L1_gnn_in['ln2_g'], 'L1_gnn_ln2_b': _L1_gnn_in['ln2_b'], 'L1_gnn_G': _L1_gnn_in['G'], 'L1_gnn_gb': _L1_gnn_in['gb']}

def reference(x, src, dst, edge_attr_8, edge_attr_9, L0_gnn_W_in, L0_gnn_b_in, L0_gnn_W_l, L0_gnn_b_l, L0_gnn_gamma_l, L0_gnn_beta_l, L1_gnn_W1, L1_gnn_b1, L1_gnn_W2, L1_gnn_b2, L1_gnn_W3, L1_gnn_b3, L1_gnn_U1, L1_gnn_ub1, L1_gnn_ln1_g, L1_gnn_ln1_b, L1_gnn_U2, L1_gnn_ub2, L1_gnn_ln2_g, L1_gnn_ln2_b, L1_gnn_G, L1_gnn_gb):
    import jax
    import jax.numpy as jnp

    def _L0_gnn_ref(x, edge_src, edge_dst, W_in, b_in, W_l, b_l, gamma_l, beta_l):
        import jax, jax.numpy as jnp
        import numpy as np
        N = 6250
        E = 150000
        D_IN = 64
        D_H = 64
        L = 3
        TAU = 1.0
        EPS = 1e-30
        LN_EPS = 1e-05
        ALPHA = 0.5

        def scatter_logsumexp(src, index, n, tau=TAU, eps=EPS):
            scaled = src.astype(jnp.float32) / tau
            max_val = jax.ops.segment_max(scaled, index, num_segments=n)
            exp_val = jnp.exp(scaled - max_val[index])
            sum_exp = jax.ops.segment_sum(exp_val, index, num_segments=n)
            deg = jnp.bincount(index, length=n)
            has_nbr = (deg > 0)[:, None]
            max_safe = jnp.where(has_nbr, max_val, 0.0)
            out = tau * (max_safe + jnp.log(jnp.maximum(sum_exp, eps)))
            return jnp.where(has_nbr, out, 0.0).astype(src.dtype)

        def layer_norm(h, gamma, beta):
            mu = jnp.mean(h, axis=-1, keepdims=True)
            var = jnp.var(h, axis=-1, keepdims=True)
            return (h - mu) * jax.lax.rsqrt(var + LN_EPS) * gamma + beta
        h = x @ W_in.T + b_in
        for i in range(L):
            src_feat = h[edge_src]
            agg = scatter_logsumexp(src_feat, edge_dst, N)
            hc = jnp.concatenate([h, agg], axis=-1)
            h_new = hc @ W_l[i].T + b_l[i]
            h_new = jax.nn.relu(layer_norm(h_new, gamma_l[i], beta_l[i]))
            h = ALPHA * h + (1.0 - ALPHA) * h_new
        return h

    def _L1_gnn_ref(node_feats, edge_index, edge_sh, edge_radial, W1, b1, W2, b2, W3, b3, U1, ub1, ln1_g, ln1_b, U2, ub2, ln2_g, ln2_b, G, gb):
        import jax, jax.numpy as jnp
        import numpy as np
        N_NODES = 6250
        N_EDGES = 100000
        NODE_DIM = 64
        SH_DIM = 9
        RADIAL_DIM = 8
        HIDDEN_DIM = 128
        LN_EPS = 1e-05

        def _linear_init(key, fan_in, fan_out):
            kw, kb = jax.random.split(key)
            bound = 1.0 / np.sqrt(fan_in)
            W = jax.random.uniform(kw, (fan_in, fan_out), minval=-bound, maxval=bound, dtype=jnp.float32)
            b = jax.random.uniform(kb, (fan_out,), minval=-bound, maxval=bound, dtype=jnp.float32)
            return (W, b)

        def _layernorm(x, g, b):
            mu = jnp.mean(x, axis=-1, keepdims=True)
            var = jnp.var(x, axis=-1, keepdims=True)
            return (x - mu) * jax.lax.rsqrt(var + LN_EPS) * g + b
        src, dst = (edge_index[0], edge_index[1])
        msg_input = jnp.concatenate([node_feats[src], edge_sh, edge_radial], axis=-1)
        h = jax.nn.silu(msg_input @ W1 + b1)
        h = jax.nn.silu(h @ W2 + b2)
        messages = h @ W3 + b3
        aggregated = jax.ops.segment_sum(messages, dst, num_segments=node_feats.shape[0])
        update_input = jnp.concatenate([node_feats, aggregated], axis=-1)
        gate = jax.nn.sigmoid(update_input @ G + gb)
        u = jax.nn.silu(_layernorm(update_input @ U1 + ub1, ln1_g, ln1_b))
        update = _layernorm(u @ U2 + ub2, ln2_g, ln2_b)
        return node_feats + gate * update
    edge_index = jnp.stack([src, dst])
    h = jnp.maximum(_layernorm(x, axis=-1), 0.0)
    x = x + _L0_gnn_ref(h, src, dst, L0_gnn_W_in, L0_gnn_b_in, L0_gnn_W_l, L0_gnn_b_l, L0_gnn_gamma_l, L0_gnn_beta_l)
    h = jnp.maximum(_layernorm(x, axis=-1), 0.0)
    x = x + _L1_gnn_ref(h, edge_index, edge_attr_9, edge_attr_8, L1_gnn_W1, L1_gnn_b1, L1_gnn_W2, L1_gnn_b2, L1_gnn_W3, L1_gnn_b3, L1_gnn_U1, L1_gnn_ub1, L1_gnn_ln1_g, L1_gnn_ln1_b, L1_gnn_U2, L1_gnn_ub2, L1_gnn_ln2_g, L1_gnn_ln2_b, L1_gnn_G, L1_gnn_gb)
    return x

_drawn_inputs = setup_inputs


def setup_inputs(seed=0):
    import zlib

    import numpy as np

    out = dict(_drawn_inputs(seed))
    spreads = {'L0_gnn_gamma_l': (1.0, 0.2),
     'L0_gnn_beta_l': (0.0, 0.1),
     'L1_gnn_ln1_g': (1.0, 0.2),
     'L1_gnn_ln1_b': (0.0, 0.314),
     'L1_gnn_ln2_g': (1.0, 0.2),
     'L1_gnn_ln2_b': (0.0, 0.281)}
    factors = {'edge_attr_8': 8.0,
     'edge_attr_9': 4.286,
     'L0_gnn_b_in': 7.227,
     'L0_gnn_b_l': 4.424,
     'L1_gnn_b1': 2.959,
     'L1_gnn_ub1': 3.36,
     'L1_gnn_gb': 8.0}
    for name, (base, spread) in spreads.items():
        noise = np.random.default_rng([zlib.crc32(name.encode()), seed]).standard_normal(out[name].shape)
        drawn = base * np.exp(spread * noise) if base else spread * noise
        out[name] = jnp.asarray(drawn.astype(out[name].dtype))
    for name, factor in factors.items():
        out[name] = (out[name] * factor).astype(out[name].dtype)
    return out
```

```python
from contextlib import ExitStack

import concourse.bass as bass
from concourse import mybir

F32 = mybir.dt.float32
I32 = mybir.dt.int32
U32 = mybir.dt.uint32
ALU = mybir.AluOpType
ACT = mybir.ActivationFunctionType
AX = mybir.AxisListType

P = 128
N_NODES, D, HID = 6250, 64, 128
N_EDGES, N_ATTR, LAYERS = 200000, 17, 3
J = -(-N_NODES // P)
NPAD = P * J
GT = 7
NG = J // GT
TB = 4
BE = TB * P
SLOTS = 4
BODY = SLOTS * BE
NB = -(-N_EDGES // BODY)
EPAD = NB * BODY
ET = EPAD // P
LN_EPS = 1e-5
SUM_EPS = 1e-30
BIG = 1e30
DMA = 16

W_COLS, _at = {}, 0
for _name, _rows, _cols in [("w_l", 2 * D, LAYERS * D), ("w_in", D, D), ("W1x", D, HID), ("W1e", N_ATTR, HID),
                            ("W2", HID, HID), ("W3", HID, D), ("U1", 2 * D, HID), ("U2", HID, D), ("G", 2 * D, D),
                            ("b2", HID, 1)]:
    W_COLS[_name] = (_at, _rows, _cols)
    _at += _cols
W_TOTAL = _at
V_COLS, _at = {}, 0
for _name, _cols in [("b_in", D), ("b_l", LAYERS * D), ("gamma", LAYERS * D), ("beta", LAYERS * D), ("b1", HID),
                     ("b3", D), ("ub1", HID), ("ln1_g", HID), ("ln1_b", HID), ("ub2", D), ("ln2_g", D),
                     ("ln2_b", D), ("gb", D)]:
    V_COLS[_name] = (_at, _cols)
    _at += _cols
V_TOTAL = _at


def build(nc, x_in, dst_in, prev_in, first_in, src_in, attr_in, w_in, v_in, out):
    with ExitStack() as ctx:
        def sb(name, shape, dt=F32):
            return ctx.enter_context(nc.sbuf_tensor(name, shape, dt))

        def sem(name):
            return ctx.enter_context(nc.semaphore(name))

        h_tab = nc.dram_tensor("h_tab", (NPAD, D), F32).ap()
        p_tab = nc.dram_tensor("p_tab", (NPAD, HID), F32).ap()
        scan_rows = nc.dram_tensor("scan_rows", (EPAD, P), F32).ap()
        drop_d = nc.dram_tensor("drop_d", (1, EPAD + BODY), F32).ap()
        keep_d = nc.dram_tensor("keep_d", (1, EPAD + BODY), F32).ap()
        ends_d = nc.dram_tensor("ends_d", (1, NPAD + 1), F32).ap()

        weights = sb("weights", [P, W_TOTAL])
        rowvec = sb("rowvec", [P, V_TOTAL])
        ident = sb("ident", [P, P])
        neg_ident = sb("neg_ident", [D, D])
        zero1 = sb("zero1", [1, 1])
        src_all = sb("src_all", [P, ET], I32)
        xres = sb("xres", [P, J, D])
        hbuf = sb("hbuf", [P, J, D])
        ybuf = sb("ybuf", [P, J, D])
        wide = sb("wide", [P, J, P])
        ends = sb("ends", [P, J, P])
        small = [sb(f"small{n}", [P, J]) for n in range(6)]
        mean, var, rstd, end_f, start_f, has = small
        degree = sb("degree", [P, J])
        end_idx = sb("end_idx", [P, J], I32)
        stage = sb("stage", [P, GT, P])
        stageT = sb("stageT", [P, GT * P])
        idx = sb("idx", [P, SLOTS, TB], I32)
        rows = sb("rows", [P, SLOTS, TB, P])
        outrow = sb("outrow", [P, SLOTS, TB, P])
        segmask = sb("segmask", [P, SLOTS, BE])
        scan = sb("scan", [P, BODY + 1])
        top = sb("top", [D, BODY + 1])
        bufA = sb("bufA", [P, SLOTS, BE])
        bufB = sb("bufB", [P, SLOTS, BE])
        attrT = sb("attrT", [N_ATTR, SLOTS, BE])

        ps = ctx.enter_context(nc.psum_tensor("ps", [P, 8, 512], F32))
        xT = [ps[:, k, :] for k in range(SLOTS)]
        back = [ps[:, SLOTS + k, :] for k in range(SLOTS)]

        def W(name):
            a, r, c = W_COLS[name]
            return weights[0:r, a:a + c]

        def V(name, a=0, n=None):
            s, c = V_COLS[name]
            return rowvec[:, s + a:s + a + (c if n is None else n)]

        def edge_list(buf):
            return buf[:, :, :].rearrange("p a b -> p (a b)")[:, 0:ET]

        firsts = rows[:, :, :, :].rearrange("p a b c -> p (a b c)").bitcast(I32)[:, 0:ET]
        dst_tiles = dst_in.rearrange("o (t e) -> (o t) e", e=P)

        loaded = sem("loaded")
        consts = sem("consts")
        ids_ready = sem("ids_ready")
        setup = sem("setup")
        masks_ready, masks_stored = sem("masks_ready"), sem("masks_stored")
        tile_known, tile_fetched = sem("tile_known"), sem("tile_fetched")
        end_known, end_stored, start_loaded, ends_known = (sem(n) for n in (
            "end_known", "end_stored", "start_loaded", "ends_known"))
        h_ready, h_stored, p_ready, p_stored = (sem(n) for n in ("h_ready", "h_stored", "p_ready", "p_stored"))
        y_ready, y_stored = sem("y_ready"), sem("y_stored")
        attr_loaded = [sem(f"attr_loaded{k}") for k in range(SLOTS)]

        class EdgeSems:
            def __init__(self, tag):
                self.idx_ready = sem(tag + "idx_ready")
                self.xt_done = sem(tag + "xt_done")
                self.top_done = sem(tag + "top_done")
                self.diff_done = sem(tag + "diff_done")
                self.fall_done = sem(tag + "fall_done")
                self.shift_done = sem(tag + "shift_done")
                self.decay_done = sem(tag + "decay_done")
                self.term_done = sem(tag + "term_done")
                self.scan_done = sem(tag + "scan_done")
                self.top_carried = sem(tag + "top_carried")
                self.scan_carried = sem(tag + "scan_carried")
                self.back_done = sem(tag + "back_done")
                self.out_ready = sem(tag + "out_ready")
                self.out_free = sem(tag + "out_free")
                self.silu1_done = sem(tag + "silu1_done")
                self.w2_done = sem(tag + "w2_done")
                self.silu2_done = sem(tag + "silu2_done")
                self.ends_fetched = sem(tag + "ends_fetched")
                self.floored = sem(tag + "floored")
                self.ln_done = sem(tag + "ln_done")
                self.gathered = [sem(f"{tag}gathered{k}") for k in range(SLOTS)]
                self.mask_loaded = [sem(f"{tag}mask_loaded{k}") for k in range(SLOTS)]
                self.stored = [sem(f"{tag}stored{k}") for k in range(SLOTS)]

        class NodeSems:
            def __init__(self, tag):
                self.staged = sem(tag + "staged")
                self.turned = sem(tag + "turned")
                self.copied = sem(tag + "copied")
                self.product = sem(tag + "product")
                self.used = sem(tag + "used")

        e0, e1 = EdgeSems("l0_"), EdgeSems("l1_")
        n_in, n_l, n_p, n_s, n_u, n_o = (NodeSems(t) for t in ("nin_", "nl_", "np_", "ns_", "nu_", "no_"))
        LNS = ("in", "l", "p", "u", "o")
        chain = {t: sem("chain_" + t) for t in LNS + ("s",)}
        var_ready = {t: sem("var_ready_" + t) for t in LNS}
        sd_ready = {t: sem("sd_ready_" + t) for t in LNS}
        gate_in, gate_done, u_in, u_done = (sem(n) for n in ("gate_in", "gate_done", "u_in", "u_done"))

        alone = {e: sem("alone_" + e) for e in ("pe", "pool", "dve")}

        block = ctx.enter_context(nc.Block())
        LOADS = 7

        @block.sync
        def _(sp):
            sp.sem_inc(e0.out_free, 1)
            sp.sem_inc(e1.out_free, 1)
            sp.dma_start(edge_list(bufA).bitcast(I32), dst_in.rearrange("o (p e) -> (o p) e", p=P)).then_inc(loaded, DMA)
            sp.dma_start(edge_list(bufB).bitcast(I32), prev_in.rearrange("o (p e) -> (o p) e", p=P)).then_inc(loaded, DMA)
            sp.dma_start(firsts, first_in.partition_broadcast(P)).then_inc(loaded, DMA)
            sp.dma_start(xres[:, :, :], x_in).then_inc(loaded, DMA)
            sp.dma_start(weights[:, :], w_in).then_inc(loaded, DMA)
            sp.dma_start(rowvec[:, :], v_in.partition_broadcast(P)).then_inc(loaded, DMA)
            sp.dma_start(src_all[:, :], src_in).then_inc(loaded, DMA)

            sp.wait_ge(masks_ready, 2)
            for m, buf in ((drop_d, bufA), (keep_d, bufB)):
                t = edge_list(buf)
                sp.dma_start(m[:, 0:EPAD].rearrange("o (p e) -> (o p) e", p=P), t).then_inc(masks_stored, DMA)
                sp.dma_start(m[:, EPAD:EPAD + ET], t[0:1, :]).then_inc(masks_stored, DMA)
                sp.dma_start(m[:, EPAD + ET:EPAD + BODY], t[1:2, 0:BODY - ET]).then_inc(masks_stored, DMA)
            sp.wait_ge(masks_stored, 6 * DMA)
            for k in range(SLOTS):
                sp.dma_start(segmask[0:D, k, :], drop_d[:, k * BE:(k + 1) * BE].partition_broadcast(D))\
                  .then_inc(e0.mask_loaded[k], DMA)

            sp.wait_ge(end_known, 1)
            sp.wait_ge(consts, 5)
            sp.dma_start(ends_d[:, 1:NPAD + 1].rearrange("o (p j) -> (o p) j", p=P), end_f[:, :]).then_inc(end_stored, DMA)
            sp.dma_start(ends_d[:, 0:1], zero1[0:1, 0:1]).then_inc(end_stored, DMA)
            sp.wait_ge(end_stored, 2 * DMA)
            sp.dma_start(start_f[:, :], ends_d[:, 0:NPAD].rearrange("o (p j) -> (o p) j", p=P)).then_inc(start_loaded, DMA)

            def store_h():
                sp.dma_start(h_tab.rearrange("(p j) d -> p (j d)", p=P), hbuf[:, :, :].rearrange("p j d -> p (j d)"))\
                  .then_inc(h_stored, DMA)

            def store_rows(e, c, i):
                for k in range(SLOTS):
                    sp.wait_ge(e.out_ready, SLOTS * c + k + 1 + SLOTS)
                    sp.dma_start(scan_rows[bass.ds(i * BODY + k * BE, BE), :].rearrange("(t p) f -> p t f", p=P),
                                 outrow[:, k, :, :]).then_inc(e.stored[k], DMA)
                for k in range(SLOTS):
                    sp.wait_ge(e.stored[k], DMA * (c + 1))
                sp.sem_inc(e.out_free, 1)

            sp.wait_ge(h_ready, 1)
            store_h()
            with sp.Fori(0, LAYERS) as l:
                with sp.Fori(0, NB) as i:
                    c = l * NB + i
                    for k in range(SLOTS):
                        sp.wait_ge(e0.fall_done, SLOTS * c + k + 1)
                        sp.dma_start(segmask[0:D, k, :],
                                     drop_d[:, bass.ds((i + 1) * BODY + k * BE, BE)].partition_broadcast(D))\
                          .then_inc(e0.mask_loaded[k], DMA)
                    store_rows(e0, c, i)
                sp.wait_ge(h_ready, l + 2)
                store_h()

            for k in range(SLOTS):
                sp.wait_ge(e0.mask_loaded[k], DMA * (LAYERS * NB + 1))
                sp.dma_start(segmask[:, k, :], keep_d[:, k * BE:(k + 1) * BE].partition_broadcast(P))\
                  .then_inc(e1.mask_loaded[k], DMA)
                sp.dma_start(attrT[:, k, :], attr_in[:, k * BE:(k + 1) * BE]).then_inc(attr_loaded[k], DMA)
            sp.wait_ge(p_ready, 1)
            sp.dma_start(p_tab.rearrange("(p j) d -> p (j d)", p=P), wide[:, :, :].rearrange("p j d -> p (j d)"))\
              .then_inc(p_stored, DMA)
            with sp.Fori(0, NB) as i:
                for k in range(SLOTS):
                    sp.wait_ge(e1.xt_done, SLOTS * i + k + 1 + SLOTS)
                    sp.dma_start(attrT[:, k, :], attr_in[:, bass.ds((i + 1) * BODY + k * BE, BE)])\
                      .then_inc(attr_loaded[k], DMA)
                for k in range(SLOTS):
                    sp.wait_ge(e1.scan_done, SLOTS * i + k + 1 + SLOTS)
                    sp.dma_start(segmask[:, k, :],
                                 keep_d[:, bass.ds((i + 1) * BODY + k * BE, BE)].partition_broadcast(P))\
                      .then_inc(e1.mask_loaded[k], DMA)
                store_rows(e1, i, i)
            for k in range(SLOTS):
                sp.wait_ge(e1.mask_loaded[k], DMA * (NB + 1))
                sp.wait_ge(attr_loaded[k], DMA * (NB + 1))
            sp.wait_ge(y_ready, 1)
            sp.dma_start(out, xres[:, :, :]).then_inc(y_stored, DMA)
            sp.wait_ge(y_stored, DMA)

        @block.gpsimd
        def _(pool):
            pool.memset(ident[:, :], 0.0).then_inc(consts, 1)
            pool.memset(neg_ident[:, :], 0.0).then_inc(consts, 1)
            pool.memset(zero1[:, :], 0.0).then_inc(consts, 1)
            pool.iota(end_idx[:, :], [[1, J]], base=0, channel_multiplier=J).then_inc(ids_ready, 1)
            pool.wait_ge(consts, 3)
            pool.affine_select(out=ident[:, :], in_=ident[:, :], compare_op=ALU.not_equal, fill=1.0,
                               base=0, pattern=[[-1, P]], channel_multiplier=1).then_inc(consts, 1)
            pool.affine_select(out=neg_ident[:, :], in_=neg_ident[:, :], compare_op=ALU.not_equal, fill=-1.0,
                               base=0, pattern=[[-1, D]], channel_multiplier=1).then_inc(consts, 1)

            pool.wait_ge(tile_known, 1)
            for j in range(J):
                pool.indirect_dma_start(wide[:, j, :].bitcast(I32), None, dst_tiles,
                                        bass.IndirectOffsetOnAxis(ap=end_idx[:, j:j + 1].bitcast(U32), axis=0))\
                    .then_inc(tile_fetched, DMA)

            def gather(e, c, i, table, width):
                for k in range(SLOTS):
                    pool.wait_ge(e.xt_done, SLOTS * c + k + 1)
                    pool.tensor_copy(idx[:, k, :], src_all[:, bass.ds(i * (SLOTS * TB) + k * TB, TB)])\
                        .then_inc(e.idx_ready, 1)
                    pool.wait_ge(e.idx_ready, SLOTS * c + k + 1)
                    pool.sem_inc(alone["pool"], 1)
                    for t in range(TB):
                        pool.indirect_dma_start(rows[:, k, t, 0:width], None, table,
                                                bass.IndirectOffsetOnAxis(ap=idx[:, k, t:t + 1].bitcast(U32), axis=0))\
                            .then_inc(e.gathered[k], DMA)

            def fetch_ends(e):
                for j in range(J):
                    pool.indirect_dma_start(ends[:, j, :], None, scan_rows,
                                            bass.IndirectOffsetOnAxis(ap=end_idx[:, j:j + 1].bitcast(U32), axis=0))\
                        .then_inc(e.ends_fetched, DMA)

            pool.wait_ge(loaded, LOADS * DMA)
            pool.wait_ge(ends_known, 1)
            with pool.Fori(0, LAYERS) as l:
                pool.wait_ge(h_stored, DMA * (l + 1))
                pool.sem_inc(alone["pool"], 1)
                with pool.Fori(0, NB) as i:
                    gather(e0, l * NB + i, i, h_tab, D)
                pool.wait_ge(e0.out_free, NB * (l + 1) + 1)
                pool.sem_inc(alone["pool"], 1)
                fetch_ends(e0)
            pool.wait_ge(p_stored, DMA)
            with pool.Fori(0, NB) as i:
                gather(e1, i, i, p_tab, HID)
            pool.wait_ge(e1.out_free, NB + 1)
            fetch_ends(e1)

        @block.tensor
        def _(pe):
            def node_group(s, n, steps, width, products):
                pe.wait_ge(s.staged, n * steps)
                pe.sem_inc(alone["pe"], 1)
                for t in range(GT):
                    last = pe.transpose(ps[0:width, t // TB, (t % TB) * P:(t % TB + 1) * P], stage[:, t, 0:width],
                                        ident[:, :])
                last.then_inc(s.turned, 1)
                pe.wait_ge(s.copied, n)
                for w, cols, bank in products:
                    per = 512 // cols
                    for t in range(GT):
                        last = pe.matmul(ps[:, bank + t // per, (t % per) * cols:(t % per + 1) * cols],
                                         stageT[0:width, t * P:(t + 1) * P], w, start=True, stop=True)
                last.then_inc(s.product, 1)

            pe.sem_inc(e0.xt_done, SLOTS)
            pe.sem_inc(e0.back_done, SLOTS)
            pe.sem_inc(e1.xt_done, SLOTS)
            pe.sem_inc(e1.back_done, SLOTS)
            pe.wait_ge(loaded, LOADS * DMA)
            pe.wait_ge(consts, 5)
            with pe.Fori(0, NG) as g:
                node_group(n_in, g + 1, 1, D, [(W("w_in"), D, 2)])
            with pe.Fori(0, LAYERS) as l:
                with pe.Fori(0, NB) as i:
                    c = l * NB + i
                    b = c * SLOTS
                    for k in range(SLOTS):
                        pe.wait_ge(e0.gathered[k], TB * DMA * (c + 1))
                        pe.wait_ge(e0.term_done, b + k + 1)
                        for t in range(TB):
                            last = pe.matmul(xT[k][0:D, t * P:(t + 1) * P], rows[:, k, t, 0:D], ident[:, :],
                                             start=(t == 0), stop=(t == TB - 1), skip_group_check=True)
                        last.then_inc(e0.xt_done, 1)
                    for k in range(SLOTS):
                        pe.wait_ge(e0.top_done, b + k + 1)
                        pe.sem_inc(alone["pe"], 1)
                        pe.matmul(xT[k][0:D, :], neg_ident[:, :], top[:, k * BE + 1:(k + 1) * BE + 1],
                                  start=False, stop=True, skip_group_check=True).then_inc(e0.shift_done, 1)
                    for k in range(SLOTS):
                        pe.wait_ge(e0.scan_done, b + k + 1 + SLOTS)
                        pe.wait_ge(e0.out_ready, b + k + 1)
                        pe.sem_inc(alone["pe"], 1)
                        for t in range(TB):
                            o = k * BE + t * P + 1
                            pe.transpose(back[k][:, t * P:t * P + D], top[:, o:o + P], ident[0:D, 0:D])
                            last = pe.transpose(back[k][:, t * P + D:(t + 1) * P], scan[0:D, o:o + P], ident[0:D, 0:D])
                        last.then_inc(e0.back_done, 1)
                with pe.Fori(0, NG) as g:
                    node_group(n_l, l * NG + g + 1, 2, 2 * D,
                               [(weights[:, bass.ds(l * D + W_COLS["w_l"][0], D)], D, 2)])
            with pe.Fori(0, NG) as g:
                node_group(n_p, g + 1, 1, D, [(W("W1x"), HID, 2)])
            with pe.Fori(0, NB) as i:
                b = i * SLOTS
                for k in range(SLOTS):
                    pe.wait_ge(attr_loaded[k], DMA * (i + 1))
                    pe.wait_ge(e1.silu2_done, b + k + 1)
                    pe.matmul(xT[k], W("W1e"), attrT[:, k, :], start=True, stop=False, skip_group_check=True)
                    pe.wait_ge(e1.gathered[k], TB * DMA * (i + 1))
                    for t in range(TB):
                        last = pe.matmul(xT[k][:, t * P:(t + 1) * P], rows[:, k, t, :], ident[:, :],
                                         start=False, stop=(t == TB - 1), skip_group_check=True)
                    last.then_inc(e1.xt_done, 1)
                for k in range(SLOTS):
                    pe.wait_ge(e1.silu1_done, b + k + 1)
                    pe.matmul(xT[k], W("W2"), bufA[:, k, :], start=True, stop=True).then_inc(e1.w2_done, 1)
                for k in range(SLOTS):
                    pe.wait_ge(e1.scan_done, b + k + 1 + SLOTS)
                    pe.wait_ge(e1.out_ready, b + k + 1)
                    for t in range(TB):
                        o = k * BE + t * P + 1
                        last = pe.transpose(back[k][:, t * P:(t + 1) * P], scan[:, o:o + P], ident[:, :])
                    last.then_inc(e1.back_done, 1)
            with pe.Fori(0, NG) as g:
                node_group(n_s, g + 1, 1, HID, [(W("W3"), D, 2)])
            with pe.Fori(0, NG) as g:
                node_group(n_u, g + 1, 2, 2 * D, [(W("U1"), HID, 2), (W("G"), D, 4)])
            with pe.Fori(0, NG) as g:
                node_group(n_o, g + 1, 1, HID, [(W("U2"), D, 2)])

        @block.scalar
        def _(act):
            def copy_turned(s, n, width):
                act.wait_ge(s.turned, n)
                act.activation(stageT[0:width, :], ps[0:width, 0:2, :].rearrange("p b c -> p (b c)")[:, 0:GT * P],
                               ACT.Copy).then_inc(s.copied, 1)

            def sqrt(tag, n):
                act.wait_ge(var_ready[tag], n)
                act.activation(rstd[:, :], var[:, :], ACT.Sqrt).then_inc(sd_ready[tag], 1)

            def copy_out(e, c):
                act.wait_ge(e.out_free, c + 1)
                for k in range(SLOTS):
                    act.wait_ge(e.back_done, c * SLOTS + k + 1 + SLOTS)
                    act.activation(outrow[:, k, :, :].rearrange("p t f -> p (t f)"), back[k], ACT.Copy)\
                        .then_inc(e.out_ready, 1)

            act.sem_inc(e0.term_done, SLOTS)
            act.sem_inc(e0.out_ready, SLOTS)
            act.sem_inc(e1.silu2_done, SLOTS)
            act.sem_inc(e1.out_ready, SLOTS)
            sqrt("in", 1)
            with act.Fori(0, NG) as g:
                copy_turned(n_in, g + 1, D)
            with act.Fori(0, LAYERS) as l:
                with act.Fori(0, NB) as i:
                    c = l * NB + i
                    b = c * SLOTS
                    for k in range(SLOTS):
                        act.wait_ge(e0.fall_done, b + k + 1)
                        act.activation(bufA[0:D, k, :], bufA[0:D, k, :], ACT.Exp).then_inc(e0.decay_done, 1)
                        act.wait_ge(e0.shift_done, b + k + 1)
                        act.wait_ge(e0.scan_done, b + k + 1)
                        act.activation(bufB[0:D, k, :], xT[k][0:D, :], ACT.Exp).then_inc(e0.term_done, 1)
                    copy_out(e0, c)
                act.wait_ge(e0.floored, l + 1)
                act.activation(ends[:, :, D:P], ends[:, :, D:P], ACT.Ln).then_inc(e0.ln_done, 1)
                with act.Fori(0, NG) as g:
                    copy_turned(n_l, l * NG + g + 1, 2 * D)
                sqrt("l", l + 1)
            sqrt("p", 1)
            with act.Fori(0, NG) as g:
                copy_turned(n_p, g + 1, D)
            with act.Fori(0, NB) as i:
                b = i * SLOTS
                for k in range(SLOTS):
                    act.wait_ge(e1.xt_done, b + k + 1 + SLOTS)
                    act.activation(bufA[:, k, :], xT[k], ACT.Silu).then_inc(e1.silu1_done, 1)
                for k in range(SLOTS):
                    act.wait_ge(e1.w2_done, b + k + 1)
                    act.wait_ge(e1.scan_done, b + k + 1)
                    act.activation(bufB[:, k, :], xT[k], ACT.Silu, bias=W("b2")).then_inc(e1.silu2_done, 1)
                copy_out(e1, i)
            with act.Fori(0, NG) as g:
                copy_turned(n_s, g + 1, HID)
            with act.Fori(0, NG) as g:
                copy_turned(n_u, g + 1, 2 * D)
            sqrt("u", 1)
            act.wait_ge(gate_in, 1)
            act.activation(ybuf[:, :, :], ybuf[:, :, :], ACT.Sigmoid).then_inc(gate_done, 1)
            act.wait_ge(u_in, 1)
            act.activation(wide[:, :, :], wide[:, :, :], ACT.Silu).then_inc(u_done, 1)
            with act.Fori(0, NG) as g:
                copy_turned(n_o, g + 1, HID)
            sqrt("o", 1)

        @block.vector
        def _(dve):
            class Chain:
                def __init__(self, s, base=0):
                    self.s, self.base, self.n = s, base, 0

                def __call__(self, ins):
                    self.n += 1
                    ins.then_inc(self.s, 1)
                    dve.wait_ge(self.s, self.base + self.n)

            def per_node(a, n):
                return a.unsqueeze(2).to_broadcast([P, a.shape[1], n])

            def per_feature(a, reps):
                return a.unsqueeze(1).to_broadcast([P, reps, a.shape[1]])

            def layernorm(link, tag, n, v, tmp, width):
                link(dve.tensor_reduce(mean[:, :], v, AX.X, ALU.add))
                link(dve.tensor_scalar(mean[:, :], mean[:, :], 1.0 / width, None, ALU.mult))
                link(dve.tensor_tensor(v, v, per_node(mean[:, :], width), ALU.subtract))
                link(dve.tensor_tensor(tmp, v, v, ALU.mult))
                link(dve.tensor_reduce(var[:, :], tmp, AX.X, ALU.add))
                dve.tensor_scalar(var[:, :], var[:, :], 1.0 / width, LN_EPS, ALU.mult, ALU.add).then_inc(var_ready[tag], 1)
                dve.wait_ge(sd_ready[tag], n)
                link(dve.reciprocal(rstd[:, :], rstd[:, :]))
                link(dve.tensor_tensor(v, v, per_node(rstd[:, :], width), ALU.mult))

            def group(buf, g):
                return buf[:, bass.ds(g * GT, GT), :]

            def product(bank, cols):
                return ps[:, bank:bank + 2, :].rearrange("p b c -> p (b c)")[:, 0:GT * cols]\
                    .rearrange("p (t c) -> p t c", c=cols)

            link = Chain(setup)
            dve.sem_inc(e0.scan_done, SLOTS)
            dve.sem_inc(e1.scan_done, SLOTS)
            dve.sem_inc(e1.scan_carried, 1)
            dve.memset(top[:, 0:1], 0.0).then_inc(e0.top_carried, 1)
            dve.memset(scan[:, 0:1], 0.0).then_inc(e0.scan_carried, 1)
            dve.wait_ge(loaded, LOADS * DMA)
            starts = wide[:, :, :].rearrange("p j f -> p (j f)")[:, 0:ET]
            junk = ends[:, :, :].rearrange("p j f -> p (j f)")[:, 0:ET]
            link(dve.tensor_tensor(starts, edge_list(bufA).bitcast(I32), edge_list(bufB).bitcast(I32), ALU.not_equal))
            dve.tensor_scalar(edge_list(bufA), starts, -BIG, None, ALU.mult).then_inc(masks_ready, 1)
            dve.tensor_scalar(edge_list(bufB), starts, -1.0, 1.0, ALU.mult, ALU.add).then_inc(masks_ready, 1)
            dve.wait_ge(masks_ready, 2)

            dve.wait_ge(ids_ready, 1)
            link(dve.tensor_copy(start_f[:, :], end_idx[:, :]))
            for j in range(J):
                link(dve.tensor_scalar(junk, firsts, start_f[:, j:j + 1], 0.0, ALU.is_le, ALU.add,
                                       accum_out=mean[:, j:j + 1]))
            link(dve.tensor_scalar(mean[:, :], mean[:, :], -1.0, 0.0, ALU.add, ALU.max))
            dve.tensor_copy(end_idx[:, :], mean[:, :]).then_inc(tile_known, 1)
            dve.wait_ge(tile_fetched, J * DMA)
            link(dve.tensor_tensor(ends[:, :, :], wide[:, :, :].bitcast(I32), per_node(start_f[:, :], P), ALU.is_le))
            link(dve.tensor_reduce(var[:, :], ends[:, :, :], AX.X, ALU.add))
            link(dve.scalar_tensor_tensor(end_f[:, :], mean[:, :], float(P), var[:, :], ALU.mult, ALU.add))
            dve.tensor_scalar(var[:, :], end_f[:, :], -1.0, 0.0, ALU.add, ALU.max).then_inc(end_known, 1)
            dve.wait_ge(end_known, 1)
            dve.tensor_copy(end_idx[:, :], var[:, :]).then_inc(ends_known, 1)
            dve.wait_ge(ends_known, 1)
            dve.wait_ge(start_loaded, DMA)
            link(dve.tensor_tensor(degree[:, :], end_f[:, :], start_f[:, :], ALU.subtract))
            link(dve.tensor_scalar(has[:, :], degree[:, :], 1.0, None, ALU.min))

            link = Chain(chain["in"])
            link(dve.tensor_copy(ybuf[:, :, :], xres[:, :, :]))
            layernorm(link, "in", 1, ybuf[:, :, :], wide[:, :, 0:D], D)
            link(dve.tensor_scalar(ybuf[:, :, :], ybuf[:, :, :], 0.0, None, ALU.max))
            with dve.Fori(0, NG) as g:
                dve.tensor_copy(stage[:, :, 0:D], group(ybuf, g)).then_inc(n_in.staged, 1)
                dve.wait_ge(n_in.product, g + 1)
                dve.tensor_tensor(group(hbuf, g), product(2, D), per_feature(V("b_in"), GT), ALU.add).then_inc(n_in.used, 1)
                dve.wait_ge(n_in.used, g + 1)
                dve.sem_inc(alone["dve"], 1)
            dve.sem_inc(h_ready, 1)

            with dve.Fori(0, LAYERS) as l:
                with dve.Fori(0, NB) as i:
                    c = l * NB + i
                    b = c * SLOTS
                    for k in range(SLOTS):
                        lo, hi = k * BE, (k + 1) * BE
                        mask, fall = segmask[0:D, k, :], bufA[0:D, k, :]
                        dve.wait_ge(e0.xt_done, b + k + 1 + SLOTS)
                        dve.wait_ge(e0.mask_loaded[k], DMA * (c + 1))
                        dve.wait_ge(e0.back_done, b + k + 1)
                        if k == 0:
                            dve.wait_ge(e0.top_carried, c + 1)
                        else:
                            dve.wait_ge(e0.top_done, b + k)
                        dve.tensor_tensor_scan(top[:, lo + 1:hi + 1], mask, xT[k][0:D, :], top[:, lo:lo + 1],
                                               ALU.add, ALU.max).then_inc(e0.top_done, 1)
                        dve.wait_ge(e0.top_done, b + k + 1)
                        dve.wait_ge(e0.scan_done, b + k + 1)
                        dve.tensor_tensor(fall, top[:, lo:hi], top[:, lo + 1:hi + 1], ALU.subtract).then_inc(e0.diff_done, 1)
                        dve.wait_ge(e0.diff_done, b + k + 1)
                        dve.tensor_tensor(fall, fall, mask, ALU.add).then_inc(e0.fall_done, 1)
                    dve.tensor_copy(top[:, 0:1], top[:, BODY:BODY + 1]).then_inc(e0.top_carried, 1)
                    for k in range(SLOTS):
                        lo, hi = k * BE, (k + 1) * BE
                        dve.wait_ge(e0.decay_done, b + k + 1)
                        dve.wait_ge(e0.term_done, b + k + 1 + SLOTS)
                        if k == 0:
                            dve.wait_ge(e0.scan_carried, c + 1)
                        else:
                            dve.wait_ge(e0.scan_done, b + k + SLOTS)
                        dve.tensor_tensor_scan(scan[0:D, lo + 1:hi + 1], bufA[0:D, k, :], bufB[0:D, k, :],
                                               scan[0:D, lo:lo + 1], ALU.mult, ALU.add).then_inc(e0.scan_done, 1)
                    dve.wait_ge(e0.scan_done, b + SLOTS + SLOTS)
                    dve.tensor_copy(scan[0:D, 0:1], scan[0:D, BODY:BODY + 1]).then_inc(e0.scan_carried, 1)

                link = Chain(chain["l"], l * LAYER_LINKS)
                dve.wait_ge(e0.ends_fetched, (l + 1) * (J * DMA))
                dve.tensor_scalar(ends[:, :, D:P], ends[:, :, D:P], SUM_EPS, None, ALU.max).then_inc(e0.floored, 1)
                dve.wait_ge(e0.ln_done, l + 1)
                link(dve.tensor_tensor(ends[:, :, 0:D], ends[:, :, 0:D], ends[:, :, D:P], ALU.add))
                link(dve.tensor_tensor(ends[:, :, 0:D], ends[:, :, 0:D], per_node(has[:, :], D), ALU.mult))
                dve.sem_inc(alone["dve"], 1)
                with dve.Fori(0, NG) as g:
                    n = l * NG + g + 1
                    dve.tensor_copy(stage[:, :, 0:D], group(hbuf, g)).then_inc(n_l.staged, 1)
                    dve.tensor_copy(stage[:, :, D:2 * D], group(ends, g)[:, :, 0:D]).then_inc(n_l.staged, 1)
                    dve.wait_ge(n_l.product, n)
                    bias = rowvec[:, bass.ds(l * D + V_COLS["b_l"][0], D)]
                    dve.tensor_tensor(group(ybuf, g), product(2, D), per_feature(bias, GT), ALU.add).then_inc(n_l.used, 1)
                    dve.wait_ge(n_l.used, n)
                    dve.sem_inc(alone["dve"], 1)
                layernorm(link, "l", l + 1, ybuf[:, :, :], wide[:, :, 0:D], D)
                for name, op in (("gamma", ALU.mult), ("beta", ALU.add)):
                    row = rowvec[:, bass.ds(l * D + V_COLS[name][0], D)]
                    link(dve.tensor_tensor(ybuf[:, :, :], ybuf[:, :, :], per_feature(row, J), op))
                link(dve.tensor_scalar(ybuf[:, :, :], ybuf[:, :, :], 0.0, 0.5, ALU.max, ALU.mult))
                dve.scalar_tensor_tensor(hbuf[:, :, :], hbuf[:, :, :], 0.5, ybuf[:, :, :], ALU.mult, ALU.add)\
                    .then_inc(h_ready, 1)
                dve.wait_ge(h_ready, l + 2)
                dve.sem_inc(alone["dve"], 1)
                assert link.n == LAYER_LINKS

            link = Chain(chain["p"])
            link(dve.tensor_tensor(xres[:, :, :], xres[:, :, :], hbuf[:, :, :], ALU.add))
            link(dve.tensor_copy(ybuf[:, :, :], xres[:, :, :]))
            layernorm(link, "p", 1, ybuf[:, :, :], wide[:, :, 0:D], D)
            dve.wait_ge(h_stored, DMA * (LAYERS + 1))
            link(dve.tensor_scalar(hbuf[:, :, :], ybuf[:, :, :], 0.0, None, ALU.max))
            with dve.Fori(0, NG) as g:
                dve.tensor_copy(stage[:, :, 0:D], group(hbuf, g)).then_inc(n_p.staged, 1)
                dve.wait_ge(n_p.product, g + 1)
                dve.tensor_tensor(group(wide, g), product(2, HID), per_feature(V("b1"), GT), ALU.add).then_inc(n_p.used, 1)
                dve.wait_ge(n_p.used, g + 1)
                dve.sem_inc(alone["dve"], 1)
            dve.sem_inc(p_ready, 1)

            with dve.Fori(0, NB) as i:
                b = i * SLOTS
                for k in range(SLOTS):
                    lo, hi = k * BE, (k + 1) * BE
                    dve.wait_ge(e1.mask_loaded[k], DMA * (i + 1))
                    dve.wait_ge(e1.silu2_done, b + k + 1 + SLOTS)
                    dve.wait_ge(e1.back_done, b + k + 1)
                    if k == 0:
                        dve.wait_ge(e1.scan_carried, i + 1)
                    else:
                        dve.wait_ge(e1.scan_done, b + k + SLOTS)
                    dve.tensor_tensor_scan(scan[:, lo + 1:hi + 1], segmask[:, k, :], bufB[:, k, :], scan[:, lo:lo + 1],
                                           ALU.mult, ALU.add).then_inc(e1.scan_done, 1)
                dve.wait_ge(e1.scan_done, b + SLOTS + SLOTS)
                dve.tensor_copy(scan[:, 0:1], scan[:, BODY:BODY + 1]).then_inc(e1.scan_carried, 1)

            link = Chain(chain["s"])
            link(dve.tensor_tensor(ybuf[:, :, :], per_node(degree[:, :], D), per_feature(V("b3"), J), ALU.mult))
            dve.wait_ge(e1.ends_fetched, J * DMA)
            with dve.Fori(0, NG) as g:
                dve.tensor_tensor(stage[:, :, :], group(ends, g), per_node(has[:, bass.ds(g * GT, GT)], P), ALU.mult)\
                    .then_inc(n_s.staged, 1)
                dve.wait_ge(n_s.product, g + 1)
                dve.tensor_tensor(group(ybuf, g), product(2, D), group(ybuf, g), ALU.add).then_inc(n_s.used, 1)
                dve.wait_ge(n_s.used, g + 1)
                dve.sem_inc(alone["dve"], 1)
            with dve.Fori(0, NG) as g:
                dve.tensor_copy(stage[:, :, 0:D], group(hbuf, g)).then_inc(n_u.staged, 1)
                dve.tensor_copy(stage[:, :, D:2 * D], group(ybuf, g)).then_inc(n_u.staged, 1)
                dve.wait_ge(n_u.product, g + 1)
                dve.tensor_tensor(group(wide, g), product(2, HID), per_feature(V("ub1"), GT), ALU.add).then_inc(n_u.used, 1)
                dve.tensor_tensor(group(ybuf, g), product(4, D), per_feature(V("gb"), GT), ALU.add).then_inc(n_u.used, 1)
                dve.wait_ge(n_u.used, 2 * (g + 1))
                dve.sem_inc(alone["dve"], 1)
            dve.sem_inc(gate_in, 1)
            link = Chain(chain["u"])
            layernorm(link, "u", 1, wide[:, :, :], ends[:, :, :], HID)
            link(dve.tensor_tensor(wide[:, :, :], wide[:, :, :], per_feature(V("ln1_g"), J), ALU.mult))
            dve.tensor_tensor(wide[:, :, :], wide[:, :, :], per_feature(V("ln1_b"), J), ALU.add).then_inc(u_in, 1)
            dve.wait_ge(u_done, 1)
            with dve.Fori(0, NG) as g:
                dve.tensor_copy(stage[:, :, :], group(wide, g)).then_inc(n_o.staged, 1)
                dve.wait_ge(n_o.product, g + 1)
                dve.tensor_tensor(group(ends, g)[:, :, 0:D], product(2, D), per_feature(V("ub2"), GT), ALU.add)\
                    .then_inc(n_o.used, 1)
                dve.wait_ge(n_o.used, g + 1)
                dve.sem_inc(alone["dve"], 1)
            link = Chain(chain["o"])
            upd = ends[:, :, 0:D]
            layernorm(link, "o", 1, upd, ends[:, :, D:P], D)
            link(dve.tensor_tensor(upd, upd, per_feature(V("ln2_g"), J), ALU.mult))
            link(dve.tensor_tensor(upd, upd, per_feature(V("ln2_b"), J), ALU.add))
            dve.wait_ge(gate_done, 1)
            link(dve.tensor_tensor(upd, upd, ybuf[:, :, :], ALU.mult))
            link(dve.tensor_tensor(upd, upd, hbuf[:, :, :], ALU.add))
            dve.tensor_tensor(xres[:, :, :], xres[:, :, :], upd, ALU.add).then_inc(y_ready, 1)


LAYER_LINKS = 12


def kernel(**inputs):
    import numpy as np
    import concourse.bacc as bacc
    from concourse.bass_utils import run_bass_kernel_spmd

    a = {k: np.asarray(v) for k, v in inputs.items()}
    f32, i32 = np.float32, np.int32
    x = np.zeros((NPAD, D), f32)
    x[:N_NODES] = a["x"]
    src = np.zeros(EPAD, i32)
    src[:N_EDGES] = a["src"]
    dst = np.full(EPAD, NPAD - 1, i32)
    dst[:N_EDGES] = a["dst"]
    prev = np.full(EPAD, -1, i32)
    prev[1:] = dst[:-1]
    attr = np.zeros((N_ATTR, EPAD + BODY), f32)
    attr[:9, :N_EDGES] = a["edge_attr_9"].T
    attr[9:, :N_EDGES] = a["edge_attr_8"].T
    g1, g0 = "L1_gnn_", "L0_gnn_"
    parts = {"w_l": np.concatenate([a[g0 + "W_l"][l].T for l in range(LAYERS)], axis=1), "w_in": a[g0 + "W_in"].T,
             "W1x": a[g1 + "W1"][:D], "W1e": a[g1 + "W1"][D:], "W2": a[g1 + "W2"], "W3": a[g1 + "W3"],
             "U1": a[g1 + "U1"], "U2": a[g1 + "U2"], "G": a[g1 + "G"], "b2": a[g1 + "b2"].reshape(HID, 1)}
    w = np.zeros((P, W_TOTAL), f32)
    for name, (at, r, c) in W_COLS.items():
        w[:r, at:at + c] = parts[name]
    rowsv = {"b_in": a[g0 + "b_in"], "b_l": a[g0 + "b_l"], "gamma": a[g0 + "gamma_l"], "beta": a[g0 + "beta_l"]}
    rowsv.update({n: a[g1 + n] for n in ("b1", "b3", "ub1", "ln1_g", "ln1_b", "ub2", "ln2_g", "ln2_b", "gb")})
    v = np.concatenate([rowsv[n].reshape(-1) for n in V_COLS]).reshape(1, V_TOTAL)
    arrays = {"x_in": x.reshape(P, J, D), "dst_in": dst.reshape(1, EPAD), "prev_in": prev.reshape(1, EPAD),
              "first_in": np.ascontiguousarray(dst[::P]).reshape(1, ET),
              "src_in": np.ascontiguousarray(src.reshape(ET, P).T), "attr_in": attr, "w_in": w, "v_in": v}

    nc = bacc.Bacc("TRN2", target_bir_lowering=False, num_devices=1)
    args = [nc.dram_tensor(n, t.shape, mybir.dt.from_np(t.dtype), kind="ExternalInput").ap() for n, t in arrays.items()]
    out = nc.dram_tensor("out", (P, J, D), F32, kind="ExternalOutput").ap()
    build(nc, *args, out)
    r = run_bass_kernel_spmd(nc, [arrays], core_ids=[0])
    return r.results[0]["out"].reshape(NPAD, D)[:N_NODES]
```

```python
from contextlib import ExitStack

import concourse.bass as bass
from concourse import mybir

F32 = mybir.dt.float32
BF16 = mybir.dt.bfloat16
FP16 = mybir.dt.float16
I32 = mybir.dt.int32
U32 = mybir.dt.uint32
ALU = mybir.AluOpType
ACT = mybir.ActivationFunctionType
AX = mybir.AxisListType

P = 128
N_NODES, D, HID = 6250, 64, 128
N_EDGES, N_ATTR, LAYERS = 200000, 17, 3
J = -(-N_NODES // P)
NPAD = P * J
GT = 7
NG = J // GT
TB = 4
BE = TB * P
SLOTS = 4
BODY = SLOTS * BE
NB = -(-N_EDGES // BODY)
EPAD = NB * BODY
ET = EPAD // P

WD = 8
NW = NPAD // WD
WB = P // WD
WT = 3
WE = WT * P
GE = 32
WG = 7
WQ = NW // WG
WCOLS = WD * J
WSLOTS = 4
RING = 4
BODIES = J // RING
PARTS = 3
MAX_DEGREE = 256
MAX_WINDOW = WE - GE + 1
MAX_RANGE = 40.0
NORM_MAX = 8.0

LN_EPS = 1e-5
SUM_EPS = 1e-30
BIG = 1e30
DMA = 16

W_COLS, _at = {}, 0
for _name, _rows, _cols in [("w_l", 2 * D, LAYERS * D), ("w_in", D, D), ("W1x", D, HID), ("W1e", N_ATTR, HID),
                            ("W2", HID, HID), ("W3", HID, D), ("U1", 2 * D, HID), ("U2", HID, D), ("G", 2 * D, D),
                            ("b2", HID, 1)]:
    W_COLS[_name] = (_at, _rows, _cols)
    _at += _cols
W_TOTAL = _at
V_COLS, _at = {}, 0
for _name, _cols in [("b_in", D), ("b_l", LAYERS * D), ("gamma", LAYERS * D), ("beta", LAYERS * D), ("b1", HID),
                     ("b3", D), ("ub1", HID), ("ln1_g", HID), ("ln1_b", HID), ("ub2", D), ("ln2_g", D),
                     ("ln2_b", D), ("gb", D)]:
    V_COLS[_name] = (_at, _cols)
    _at += _cols
V_TOTAL = _at


def build(nc, x_in, dst_in, prev_in, first_in, src_in, srcl_in, attr_in, w_in, v_in, out):
    with ExitStack() as ctx:
        def sb(name, shape, dt=F32):
            return ctx.enter_context(nc.sbuf_tensor(name, shape, dt))

        def sem(name):
            return ctx.enter_context(nc.semaphore(name))

        h_tab = nc.dram_tensor("h_tab", (NPAD, D), F32).ap()
        p_tab = nc.dram_tensor("p_tab", (NPAD, HID), F32).ap()
        scan_rows = nc.dram_tensor("scan_rows", (EPAD, P), F32).ap()
        drop_d = nc.dram_tensor("drop_d", (1, EPAD + BODY), F32).ap()
        keep_d = nc.dram_tensor("keep_d", (1, EPAD + BODY), F32).ap()
        edge_d = nc.dram_tensor("edge_d", (EPAD // GE, GE), I32).ap()
        win_d = nc.dram_tensor("win_d", (2 * WB, J), F32).ap()
        count_d = nc.dram_tensor("count_d", (J, P, J * P), BF16).ap()

        weights = sb("weights", [P, W_TOTAL])
        rowvec = sb("rowvec", [P, V_TOTAL])
        ident = sb("ident", [P, P])
        neg_ident = sb("neg_ident", [D, D])
        ones = sb("ones", [P, P])
        shift = sb("shift", [P, P])
        wrap = sb("wrap", [P, P])
        src_all = sb("src_all", [P, ET], I32)
        xres = sb("xres", [P, J, D])
        hbuf = sb("hbuf", [P, J, D])
        ybuf = sb("ybuf", [P, J, D])
        wide = sb("wide", [P, J, P])
        ends = sb("ends", [P, J, P])
        mean, var, rstd, end_f, start_f, has, degree = (sb(n, [P, J]) for n in (
            "mean", "var", "rstd", "end_f", "start_f", "has", "degree"))
        end_idx = sb("end_idx", [P, J], I32)
        stage = sb("stage", [P, GT, P])
        stageT = sb("stageT", [P, GT * P])
        idx = sb("idx", [P, SLOTS, TB], I32)
        win_first, win_end, win_base = (sb(n, [P, WG]) for n in ("win_first", "win_end", "win_base"))
        win_int, win_no = sb("win_int", [P, WG], I32), sb("win_no", [P, WG], I32)
        gran_f, gran = sb("gran_f", [P, WG, WE // GE]), sb("gran", [P, WG, WE // GE], I32)
        step_i, step_f = sb("step_i", [P, WE // GE], I32), sb("step_f", [P, WE // GE])
        iota_w, iota_p = sb("iota_w", [P, WCOLS], FP16), sb("iota_p", [P, P], FP16)
        iota_i = sb("iota_i", [P, WCOLS], I32)
        extreme = sb("extreme", [P, 2 * D])
        diag = sb("diag", [P, 2 * D])
        bound = sb("bound", [P, LAYERS * D])
        peak = sb("peak", [P, 4])
        shift_c = sb("shift_c", [P, D])
        use_counts = sb("use_counts", [P, 1], I32)

        arena = sb("arena", [P, 20480])

        def carve(at, n, parts=P):
            return arena[0:parts, at:at + n]

        rows = carve(0, BODY).rearrange("p (k t f) -> p k t f", k=SLOTS, t=TB)
        outrow = carve(2048, BODY).rearrange("p (k t f) -> p k t f", k=SLOTS, t=TB)
        segmask = carve(4096, BODY).rearrange("p (k e) -> p k e", k=SLOTS)
        scan = carve(6144, BODY + 1)
        top = carve(8208, BODY + 1, D)
        bufA = carve(10272, BODY).rearrange("p (k e) -> p k e", k=SLOTS)
        bufB = carve(12320, BODY).rearrange("p (k e) -> p k e", k=SLOTS)
        attrT = carve(14368, BODY, N_ATTR).rearrange("p (k e) -> p k e", k=SLOTS)
        dst_l, prev_l, src_l = (carve(at, ET).bitcast(I32) for at in (10272, 12320, 14368))
        drop_l, keep_l, starts, pack = carve(0, ET), carve(2048, ET), carve(4096, ET), carve(6144, ET).bitcast(I32)
        firsts = carve(8208, ET).bitcast(I32)
        NE = WG * WE
        win_edges = carve(16416, NE, WQ).bitcast(I32)
        key_a, key_b = carve(0, NE, WQ), carve(NE, NE, WQ)
        BLK = J * P
        blocks = carve(0, RING * BLK // 2).bitcast(BF16).rearrange("p (r a d) -> p r a d", r=RING, a=J)
        at = RING * BLK // 2
        keyT_a = carve(at, WT * NW).rearrange("p (i w) -> p i w", i=WT)
        keyT_b = carve(at + WT * NW, WT * NW).rearrange("p (i w) -> p i w", i=WT)
        hot_a = carve(at + 2 * WT * NW, WSLOTS * WT * WCOLS // 2).bitcast(BF16)\
            .rearrange("p (s i c) -> p s i c", s=WSLOTS, i=WT)
        hot_b = carve(at + 2 * WT * NW + WSLOTS * WT * WCOLS // 2, WSLOTS * WT * P // 2).bitcast(BF16)\
            .rearrange("p (s i c) -> p s i c", s=WSLOTS, i=WT)
        parts = carve(at, J * PARTS * D // 2).bitcast(BF16).rearrange("p (a c) -> p a c", a=J)

        ps = ctx.enter_context(nc.psum_tensor("ps", [P, 8, 512], F32))
        xT = [ps[:, k, :] for k in range(SLOTS)]
        back = [ps[:, SLOTS + k, :] for k in range(SLOTS)]

        def W(name):
            a, r, c = W_COLS[name]
            return weights[0:r, a:a + c]

        def V(name, a=0, n=None):
            s, c = V_COLS[name]
            return rowvec[:, s + a:s + a + (c if n is None else n)]

        dst_tiles = dst_in.rearrange("o (t e) -> (o t) e", e=P)

        loaded = sem("loaded")
        consts = sem("consts")
        ids_ready = sem("ids_ready")
        setup = sem("setup")
        masks_ready, masks_stored = sem("masks_ready"), sem("masks_stored")
        tile_known, tile_fetched = sem("tile_known"), sem("tile_fetched")
        end_known, start_summed, ends_known = (sem(n) for n in ("end_known", "start_summed", "ends_known"))
        pack_ready, pack_stored = sem("pack_ready"), sem("pack_stored")
        win_ready, win_stored, win_loaded = sem("win_ready"), sem("win_stored"), sem("win_loaded")
        gran_known, gran_fetched = sem("gran_known"), sem("gran_fetched")
        ext_ready, ext_turned, diag_ready, ext_spread, way_known = (sem(n) for n in (
            "ext_ready", "ext_turned", "diag_ready", "ext_spread", "way_known"))
        keys_ready, keys_turned, keys_copied = sem("keys_ready"), sem("keys_turned"), sem("keys_copied")
        hot_ready, win_counted, block_part, block_free, bank_free = (sem(n) for n in (
            "hot_ready", "win_counted", "block_part", "block_free", "bank_free"))
        block_stored = [sem(f"block_stored{r}") for r in range(2)]
        block_loaded = [sem(f"block_loaded{r}") for r in range(RING)]
        exp_in, exp_done, parts_ready, block_used, sums_read = (sem(n) for n in (
            "exp_in", "exp_done", "parts_ready", "block_used", "sums_read"))
        floored, ln_done = sem("floored"), sem("ln_done")
        h_ready, h_stored, p_ready, p_stored = (sem(n) for n in ("h_ready", "h_stored", "p_ready", "p_stored"))
        x_ready, y_ready, y_stored = sem("x_ready"), sem("y_ready"), sem("y_stored")
        attr_loaded = [sem(f"attr_loaded{k}") for k in range(SLOTS)]

        class PassSems:
            def __init__(self, tag):
                self.idx_ready = sem(tag + "idx_ready")
                self.xt_done = sem(tag + "xt_done")
                self.scan_done = sem(tag + "scan_done")
                self.scan_carried = sem(tag + "scan_carried")
                self.back_done = sem(tag + "back_done")
                self.out_ready = sem(tag + "out_ready")
                self.out_free = sem(tag + "out_free")
                self.ends_fetched = sem(tag + "ends_fetched")
                self.gathered = [sem(f"{tag}gathered{k}") for k in range(SLOTS)]
                self.mask_loaded = [sem(f"{tag}mask_loaded{k}") for k in range(SLOTS)]
                self.stored = [sem(f"{tag}stored{k}") for k in range(SLOTS)]

        class LayerPassSems(PassSems):
            def __init__(self, tag):
                super().__init__(tag)
                self.top_done = sem(tag + "top_done")
                self.diff_done = sem(tag + "diff_done")
                self.fall_done = sem(tag + "fall_done")
                self.shift_done = sem(tag + "shift_done")
                self.decay_done = sem(tag + "decay_done")
                self.term_done = sem(tag + "term_done")
                self.top_carried = sem(tag + "top_carried")

        class MessagePassSems(PassSems):
            def __init__(self, tag):
                super().__init__(tag)
                self.silu1_done = sem(tag + "silu1_done")
                self.w2_done = sem(tag + "w2_done")
                self.silu2_done = sem(tag + "silu2_done")

        class NodeSems:
            def __init__(self, tag):
                self.staged = sem(tag + "staged")
                self.turned = sem(tag + "turned")
                self.copied = sem(tag + "copied")
                self.product = sem(tag + "product")
                self.used = sem(tag + "used")

        e0, e1 = LayerPassSems("l0_"), MessagePassSems("l1_")
        n_in, n_l, n_p, n_s, n_u, n_o = (NodeSems(t) for t in ("nin_", "nl_", "np_", "ns_", "nu_", "no_"))
        chain = {t: sem("chain_" + t) for t in ("in", "l", "p", "u", "o", "s", "agg", "exp", "sum", "way")}
        var_ready, sd_ready = sem("var_ready"), sem("sd_ready")
        NORM_IN, NORM_L, NORM_P, NORM_U, NORM_O = 1, 2, 2 + LAYERS, 3 + LAYERS, 4 + LAYERS
        gate_in, gate_done, u_in, u_done = (sem(n) for n in ("gate_in", "gate_done", "u_in", "u_done"))

        alone = {e: sem("alone_" + e) for e in ("sp", "act", "pe", "pool", "dve")}

        block = ctx.enter_context(nc.Block())
        LOADS = 8

        @block.sync
        def _(sp):
            sp.sem_inc(e0.out_free, 1)
            sp.sem_inc(e1.out_free, 1)
            for t, d in ((dst_l, dst_in), (prev_l, prev_in), (src_l, srcl_in)):
                sp.dma_start(t, d.rearrange("o (p e) -> (o p) e", p=P)).then_inc(loaded, DMA)
            sp.dma_start(firsts, first_in.partition_broadcast(P)).then_inc(loaded, DMA)
            sp.dma_start(xres[:, :, :], x_in).then_inc(loaded, DMA)
            sp.dma_start(weights[:, :], w_in).then_inc(loaded, DMA)
            sp.dma_start(rowvec[:, :], v_in.partition_broadcast(P)).then_inc(loaded, DMA)
            sp.dma_start(src_all[:, :], src_in).then_inc(loaded, DMA)

            sp.wait_ge(pack_ready, 1)
            sp.dma_start(edge_d.rearrange("(p g) e -> p (g e)", p=P), pack).then_inc(pack_stored, DMA)
            sp.wait_ge(masks_ready, 2)
            for m, t in ((drop_d, drop_l), (keep_d, keep_l)):
                sp.dma_start(m[:, 0:EPAD].rearrange("o (p e) -> (o p) e", p=P), t).then_inc(masks_stored, DMA)
                sp.dma_start(m[:, EPAD:EPAD + ET], t[0:1, :]).then_inc(masks_stored, DMA)
                sp.dma_start(m[:, EPAD + ET:EPAD + BODY], t[1:2, 0:BODY - ET]).then_inc(masks_stored, DMA)
            sp.wait_ge(win_ready, 1)
            sp.dma_start(win_d[0:WB, :], start_f[0:P:WD, :]).then_inc(win_stored, DMA)
            sp.dma_start(win_d[WB:2 * WB, :], end_f[WD - 1:P:WD, :]).then_inc(win_stored, DMA)
            sp.wait_ge(win_stored, 2 * DMA)
            JG = J // WG
            with nc.allow_non_contiguous_dma(reason="784 values, once"):
                for t, r in ((win_first, 0), (win_end, WB)):
                    for q in range(JG):
                        sp.dma_start(t[q * WB:(q + 1) * WB, :], win_d[r:r + WB, q:J:JG]).then_inc(win_loaded, DMA)
            sp.wait_ge(masks_stored, 6 * DMA)

            def store_h():
                sp.dma_start(h_tab.rearrange("(j p) d -> p j d", p=P), hbuf[:, :, :])\
                  .then_inc(h_stored, DMA)

            def store_rows(e, c, i):
                for k in range(SLOTS):
                    sp.wait_ge(e.out_ready, SLOTS * c + k + 1 + SLOTS)
                    sp.dma_start(scan_rows[bass.ds(i * BODY + k * BE, BE), :].rearrange("(t p) f -> p t f", p=P),
                                 outrow[:, k, :, :]).then_inc(e.stored[k], DMA)
                for k in range(SLOTS):
                    sp.wait_ge(e.stored[k], DMA * (c + 1))
                sp.sem_inc(e.out_free, 1)

            def by_edges():
                for k in range(SLOTS):
                    sp.dma_start(segmask[0:D, k, :], drop_d[:, k * BE:(k + 1) * BE].partition_broadcast(D))\
                      .then_inc(e0.mask_loaded[k], DMA)
                sp.wait_ge(h_ready, 1)
                store_h()
                with sp.Fori(0, LAYERS) as l:
                    with sp.Fori(0, NB) as i:
                        c = l * NB + i
                        for k in range(SLOTS):
                            sp.wait_ge(e0.fall_done, SLOTS * c + k + 1)
                            sp.dma_start(segmask[0:D, k, :],
                                         drop_d[:, bass.ds((i + 1) * BODY + k * BE, BE)].partition_broadcast(D))\
                              .then_inc(e0.mask_loaded[k], DMA)
                        store_rows(e0, c, i)
                    sp.wait_ge(h_ready, l + 2)
                    store_h()
                for k in range(SLOTS):
                    sp.wait_ge(e0.mask_loaded[k], DMA * (LAYERS * NB + 1))

            def by_counts():
                def store_block(j, r, n):
                    sp.wait_ge(block_part, (WB // 2) * (j + 1))
                    sp.dma_start(count_d[bass.ds(j, 1), :, :].rearrange("o p c -> (o p) c"),
                                 blocks[:, r, :, :].rearrange("p a d -> p (a d)")).then_inc(block_stored[r], DMA)
                    sp.wait_ge(block_stored[r], DMA * n)
                    sp.sem_inc(block_free, 1)

                with sp.Fori(0, J // 2) as i:
                    for r in range(2):
                        store_block(2 * i + r, r, i + 1)
                store_block(J - 1, 0, J // 2 + 1)

                def load_block(l, j, r):
                    sp.wait_ge(block_used, l * J + j + 1)
                    sp.dma_start(blocks[:, r, :, :].rearrange("p a d -> p (a d)"),
                                 count_d[bass.ds(j, 1), :, :].rearrange("o p c -> (o p) c"))\
                      .then_inc(block_loaded[r], DMA)

                with sp.Fori(0, LAYERS) as l:
                    sp.wait_ge(block_used, l * J + RING)
                    sp.sem_inc(alone["sp"], 1)
                    with sp.Fori(0, BODIES) as i:
                        for r in range(RING):
                            load_block(l, RING * i + r, r)
                    load_block(l, J - 1, 0)

            sp.wait_ge(way_known, 1)
            counts = sp.to_reg(sp.value_load(use_counts[0:1, 0:1], min_val=0, max_val=1))
            with sp.If_ne(counts, 0):
                by_counts()
            with sp.Else():
                by_edges()

            sp.wait_ge(x_ready, 1)
            for k in range(SLOTS):
                sp.dma_start(segmask[:, k, :], keep_d[:, k * BE:(k + 1) * BE].partition_broadcast(P))\
                  .then_inc(e1.mask_loaded[k], DMA)
                sp.dma_start(attrT[:, k, :], attr_in[:, k * BE:(k + 1) * BE]).then_inc(attr_loaded[k], DMA)
            sp.wait_ge(p_ready, 1)
            sp.dma_start(p_tab.rearrange("(j p) d -> p j d", p=P), wide[:, :, :])\
              .then_inc(p_stored, DMA)
            with sp.Fori(0, NB) as i:
                for k in range(SLOTS):
                    sp.wait_ge(e1.xt_done, SLOTS * i + k + 1 + SLOTS)
                    sp.dma_start(attrT[:, k, :], attr_in[:, bass.ds((i + 1) * BODY + k * BE, BE)])\
                      .then_inc(attr_loaded[k], DMA)
                for k in range(SLOTS):
                    sp.wait_ge(e1.scan_done, SLOTS * i + k + 1 + SLOTS)
                    sp.dma_start(segmask[:, k, :],
                                 keep_d[:, bass.ds((i + 1) * BODY + k * BE, BE)].partition_broadcast(P))\
                      .then_inc(e1.mask_loaded[k], DMA)
                store_rows(e1, i, i)
            for k in range(SLOTS):
                sp.wait_ge(e1.mask_loaded[k], DMA * (NB + 1))
                sp.wait_ge(attr_loaded[k], DMA * (NB + 1))
            sp.wait_ge(y_ready, 1)
            sp.dma_start(out, xres[:, :, :]).then_inc(y_stored, DMA)
            sp.wait_ge(y_stored, DMA)

        @block.gpsimd
        def _(pool):
            for t in (ident, neg_ident, shift, wrap):
                pool.memset(t[:, :], 0.0).then_inc(consts, 1)
            pool.memset(ones[:, :], 1.0).then_inc(consts, 1)
            pool.iota(end_idx[:, :], [[P, J]], base=0, channel_multiplier=1).then_inc(ids_ready, 1)
            pool.iota(win_no[:, :], [[WQ, WG]], base=0, channel_multiplier=1).then_inc(ids_ready, 1)
            pool.iota(step_i[:, :], [[1, WE // GE]], base=0, channel_multiplier=0).then_inc(ids_ready, 1)
            pool.iota(iota_i[:, :], [[1, WCOLS]], base=0, channel_multiplier=0).then_inc(ids_ready, 1)
            pool.wait_ge(consts, 5)
            for t, fill, base, pattern in ((ident, 1.0, 0, [[-1, P]]), (neg_ident, -1.0, 0, [[-1, D]]),
                                           (shift, 1.0, 1, [[-1, P]]), (wrap, 1.0, 1 - P, [[P, P]])):
                pool.affine_select(out=t[:, :], in_=t[:, :], compare_op=ALU.not_equal, fill=fill,
                                   base=base, pattern=pattern, channel_multiplier=1).then_inc(consts, 1)

            pool.wait_ge(tile_known, 1)
            for j in range(J):
                pool.indirect_dma_start(wide[:, j, :].bitcast(I32), None, dst_tiles,
                                        bass.IndirectOffsetOnAxis(ap=end_idx[:, j:j + 1].bitcast(U32), axis=0))\
                    .then_inc(tile_fetched, DMA)

            pool.wait_ge(gran_known, 1)
            pool.wait_ge(pack_stored, DMA)
            for g in range(WG):
                for n in range(WE // GE):
                    to = g * WE + n * GE
                    pool.indirect_dma_start(win_edges[:, to:to + GE], None, edge_d,
                                            bass.IndirectOffsetOnAxis(ap=gran[0:WQ, g, n:n + 1].bitcast(U32), axis=0))\
                        .then_inc(gran_fetched, DMA)
            pool.wait_ge(gran_fetched, WG * (WE // GE) * DMA)

            def gather(e, c, i, table, width):
                for k in range(SLOTS):
                    pool.wait_ge(e.xt_done, SLOTS * c + k + 1)
                    pool.tensor_copy(idx[:, k, :], src_all[:, bass.ds(i * (SLOTS * TB) + k * TB, TB)])\
                        .then_inc(e.idx_ready, 1)
                    pool.wait_ge(e.idx_ready, SLOTS * c + k + 1)
                    pool.sem_inc(alone["pool"], 1)
                    for t in range(TB):
                        pool.indirect_dma_start(rows[:, k, t, 0:width], None, table,
                                                bass.IndirectOffsetOnAxis(ap=idx[:, k, t:t + 1].bitcast(U32), axis=0))\
                            .then_inc(e.gathered[k], DMA)

            def fetch_ends(e):
                for j in range(J):
                    pool.indirect_dma_start(ends[:, j, :], None, scan_rows,
                                            bass.IndirectOffsetOnAxis(ap=end_idx[:, j:j + 1].bitcast(U32), axis=0))\
                        .then_inc(e.ends_fetched, DMA)

            pool.wait_ge(loaded, LOADS * DMA)
            pool.wait_ge(ends_known, 1)

            pool.wait_ge(way_known, 1)
            counts = pool.to_reg(pool.value_load(use_counts[0:1, 0:1], min_val=0, max_val=1))
            with pool.If_eq(counts, 0):
                with pool.Fori(0, LAYERS) as l:
                    pool.wait_ge(h_stored, DMA * (l + 1))
                    pool.sem_inc(alone["pool"], 1)
                    with pool.Fori(0, NB) as i:
                        gather(e0, l * NB + i, i, h_tab, D)
                    pool.wait_ge(e0.out_free, NB * (l + 1) + 1)
                    pool.sem_inc(alone["pool"], 1)
                    fetch_ends(e0)
            pool.wait_ge(p_stored, DMA)
            with pool.Fori(0, NB) as i:
                gather(e1, i, i, p_tab, HID)
            pool.wait_ge(e1.out_free, NB + 1)
            fetch_ends(e1)

        @block.tensor
        def _(pe):
            def node_group(s, n, steps, width, products):
                pe.wait_ge(s.staged, n * steps)
                pe.sem_inc(alone["pe"], 1)
                for t in range(GT):
                    last = pe.transpose(ps[0:width, t // TB, (t % TB) * P:(t % TB + 1) * P], stage[:, t, 0:width],
                                        ident[:, :])
                last.then_inc(s.turned, 1)
                pe.wait_ge(s.copied, n)
                for w, cols, bank in products:
                    per = 512 // cols
                    for t in range(GT):
                        last = pe.matmul(ps[:, bank + t // per, (t % per) * cols:(t % per + 1) * cols],
                                         stageT[0:width, t * P:(t + 1) * P], w, start=True, stop=True)
                last.then_inc(s.product, 1)

            pe.sem_inc(e0.xt_done, SLOTS)
            pe.sem_inc(e0.back_done, SLOTS)
            pe.sem_inc(e1.xt_done, SLOTS)
            pe.sem_inc(e1.back_done, SLOTS)
            pe.wait_ge(loaded, LOADS * DMA)
            pe.wait_ge(consts, 9)
            pe.wait_ge(end_known, 1)
            pe.matmul(ps[:, 7, 0:J], shift[:, :], end_f[:, :], start=True, stop=False, skip_group_check=True)
            pe.matmul(ps[:, 7, 1:J], wrap[:, :], end_f[:, 0:J - 1], start=False, stop=True, skip_group_check=True)\
              .then_inc(start_summed, 1)
            with pe.Fori(0, NG) as g:
                node_group(n_in, g + 1, 1, D, [(W("w_in"), D, 2)])
            pe.wait_ge(ext_ready, 1)
            pe.transpose(ps[:, 0, 0:P], extreme[:, :], ident[:, :]).then_inc(ext_turned, 1)
            pe.wait_ge(diag_ready, 2)
            pe.matmul(ps[:, 1, 0:P], ones[:, :], diag[:, :], start=True, stop=True).then_inc(ext_spread, 1)
            pe.matmul(ps[:, 2, 0:1], ones[:, :], peak[:, 3:4], start=True, stop=True).then_inc(ext_spread, 1)

            def layer_product(l):
                with pe.Fori(0, NG) as g:
                    node_group(n_l, l * NG + g + 1, 2, 2 * D,
                               [(weights[:, bass.ds(l * D + W_COLS["w_l"][0], D)], D, 2)])

            def by_edges():
                with pe.Fori(0, LAYERS) as l:
                    with pe.Fori(0, NB) as i:
                        c = l * NB + i
                        b = c * SLOTS
                        for k in range(SLOTS):
                            pe.wait_ge(e0.gathered[k], TB * DMA * (c + 1))
                            pe.wait_ge(e0.term_done, b + k + 1)
                            for t in range(TB):
                                last = pe.matmul(xT[k][0:D, t * P:(t + 1) * P], rows[:, k, t, 0:D], ident[:, :],
                                                 start=(t == 0), stop=(t == TB - 1), skip_group_check=True)
                            last.then_inc(e0.xt_done, 1)
                        for k in range(SLOTS):
                            pe.wait_ge(e0.top_done, b + k + 1)
                            pe.sem_inc(alone["pe"], 1)
                            pe.matmul(xT[k][0:D, :], neg_ident[:, :], top[:, k * BE + 1:(k + 1) * BE + 1],
                                      start=False, stop=True, skip_group_check=True).then_inc(e0.shift_done, 1)
                        for k in range(SLOTS):
                            pe.wait_ge(e0.scan_done, b + k + 1 + SLOTS)
                            pe.wait_ge(e0.out_ready, b + k + 1)
                            pe.sem_inc(alone["pe"], 1)
                            for t in range(TB):
                                o = k * BE + t * P + 1
                                pe.transpose(back[k][:, t * P:t * P + D], top[:, o:o + P], ident[0:D, 0:D])
                                last = pe.transpose(back[k][:, t * P + D:(t + 1) * P], scan[0:D, o:o + P], ident[0:D, 0:D])
                            last.then_inc(e0.back_done, 1)
                    layer_product(l)

            def by_counts():
                pe.wait_ge(keys_ready, 2)
                for n, (key, i) in enumerate((key, i) for key in (key_a, key_b) for i in range(WT)):
                    if n >= 2:
                        pe.wait_ge(keys_copied, 2 * (n - 1))
                    for g in range(WG):
                        last = pe.transpose(ps[:, 2 * (n % 2) + g // 4, (g % 4) * WQ:(g % 4 + 1) * WQ],
                                            key[:, g * WE + i * P:g * WE + (i + 1) * P], ident[0:WQ, 0:WQ])
                    last.then_inc(keys_turned, 1)

                def count_window(n, s):
                    for i in range(WT):
                        last = pe.matmul(ps[:, 4 + s, 0:WCOLS], hot_b[:, s, i, :], hot_a[:, s, i, :],
                                         start=(i == 0), stop=(i == WT - 1))
                    last.then_inc(win_counted, 1)

                pe.sem_inc(block_used, RING)
                pe.sem_inc(win_counted, WSLOTS)
                with pe.Fori(0, NW // WSLOTS) as i:
                    for s in range(WSLOTS):
                        if s % 2 == 0:
                            pe.wait_ge(bank_free, (WSLOTS // 2) * i + s // 2 + 1)
                        pe.wait_ge(hot_ready, 2 * WT * (WSLOTS * i + s + 1))
                        count_window(WSLOTS * i + s, s)

                def block_sums(l, j, r, n):
                    pe.wait_ge(sums_read, l * J + j + 1)
                    pe.wait_ge(block_loaded[r], DMA * n)
                    for a in range(J):
                        last = pe.matmul(ps[:, 5 + r % 2, 0:PARTS * D], blocks[:, r, a, :], parts[:, a, :],
                                         start=(a == 0), stop=(a == J - 1))
                    last.then_inc(block_used, 1)

                with pe.Fori(0, LAYERS) as l:
                    pe.wait_ge(parts_ready, PARTS * (l + 1))
                    pe.sem_inc(alone["pe"], 1)
                    with pe.Fori(0, BODIES) as i:
                        for r in range(RING):
                            block_sums(l, RING * i + r, r, (BODIES + (r == 0)) * l + i + 1)
                    block_sums(l, J - 1, 0, (BODIES + 1) * (l + 1))
                    layer_product(l)

            pe.wait_ge(way_known, 1)
            counts = pe.to_reg(pe.value_load(use_counts[0:1, 0:1], min_val=0, max_val=1))
            with pe.If_ne(counts, 0):
                by_counts()
            with pe.Else():
                by_edges()
            with pe.Fori(0, NG) as g:
                node_group(n_p, g + 1, 1, D, [(W("W1x"), HID, 2)])
            with pe.Fori(0, NB) as i:
                b = i * SLOTS
                for k in range(SLOTS):
                    pe.wait_ge(attr_loaded[k], DMA * (i + 1))
                    pe.wait_ge(e1.silu2_done, b + k + 1)
                    pe.matmul(xT[k], W("W1e"), attrT[:, k, :], start=True, stop=False, skip_group_check=True)
                    pe.wait_ge(e1.gathered[k], TB * DMA * (i + 1))
                    for t in range(TB):
                        last = pe.matmul(xT[k][:, t * P:(t + 1) * P], rows[:, k, t, :], ident[:, :],
                                         start=False, stop=(t == TB - 1), skip_group_check=True)
                    last.then_inc(e1.xt_done, 1)
                for k in range(SLOTS):
                    pe.wait_ge(e1.silu1_done, b + k + 1)
                    pe.matmul(xT[k], W("W2"), bufA[:, k, :], start=True, stop=True).then_inc(e1.w2_done, 1)
                for k in range(SLOTS):
                    pe.wait_ge(e1.scan_done, b + k + 1 + SLOTS)
                    pe.wait_ge(e1.out_ready, b + k + 1)
                    for t in range(TB):
                        o = k * BE + t * P + 1
                        last = pe.transpose(back[k][:, t * P:(t + 1) * P], scan[:, o:o + P], ident[:, :])
                    last.then_inc(e1.back_done, 1)
            with pe.Fori(0, NG) as g:
                node_group(n_s, g + 1, 1, HID, [(W("W3"), D, 2)])
            with pe.Fori(0, NG) as g:
                node_group(n_u, g + 1, 2, 2 * D, [(W("U1"), HID, 2), (W("G"), D, 4)])
            with pe.Fori(0, NG) as g:
                node_group(n_o, g + 1, 1, HID, [(W("U2"), D, 2)])

        @block.scalar
        def _(act):
            def copy_turned(s, n, width):
                act.wait_ge(s.turned, n)
                act.activation(stageT[0:width, :], ps[0:width, 0:2, :].rearrange("p b c -> p (b c)")[:, 0:GT * P],
                               ACT.Copy).then_inc(s.copied, 1)

            def sqrt(n):
                act.wait_ge(var_ready, n)
                act.activation(rstd[:, :], var[:, :], ACT.Sqrt).then_inc(sd_ready, 1)

            def copy_out(e, c):
                act.wait_ge(e.out_free, c + 1)
                for k in range(SLOTS):
                    act.wait_ge(e.back_done, c * SLOTS + k + 1 + SLOTS)
                    act.activation(outrow[:, k, :, :].rearrange("p t f -> p (t f)"), back[k], ACT.Copy)\
                        .then_inc(e.out_ready, 1)

            act.sem_inc(e0.term_done, SLOTS)
            act.sem_inc(e0.out_ready, SLOTS)
            act.sem_inc(e1.silu2_done, SLOTS)
            act.sem_inc(e1.out_ready, SLOTS)
            sqrt(NORM_IN)
            with act.Fori(0, NG) as g:
                copy_turned(n_in, g + 1, D)
            def layer_product(l):
                act.wait_ge(floored, l + 1)
                act.activation(ends[:, :, D:P], ends[:, :, D:P], ACT.Ln).then_inc(ln_done, 1)
                with act.Fori(0, NG) as g:
                    copy_turned(n_l, l * NG + g + 1, 2 * D)
                sqrt(NORM_L + l)

            def by_edges():
                with act.Fori(0, LAYERS) as l:
                    with act.Fori(0, NB) as i:
                        c = l * NB + i
                        b = c * SLOTS
                        for k in range(SLOTS):
                            act.wait_ge(e0.fall_done, b + k + 1)
                            act.activation(bufA[0:D, k, :], bufA[0:D, k, :], ACT.Exp).then_inc(e0.decay_done, 1)
                            act.wait_ge(e0.shift_done, b + k + 1)
                            act.wait_ge(e0.scan_done, b + k + 1)
                            act.activation(bufB[0:D, k, :], xT[k][0:D, :], ACT.Exp).then_inc(e0.term_done, 1)
                        copy_out(e0, c)
                    layer_product(l)

            def by_counts():
                for n, (key, i) in enumerate((key, i) for key in (keyT_a, keyT_b) for i in range(WT)):
                    act.wait_ge(keys_turned, n + 1)
                    for h, (g0, g1) in enumerate(((0, 4), (4, WG))):
                        act.activation(key[:, i, g0 * WQ:g1 * WQ], ps[:, 2 * (n % 2) + h, 0:(g1 - g0) * WQ], ACT.Copy)\
                            .then_inc(keys_copied, 1)

                act.sem_inc(block_free, 2)
                act.sem_inc(bank_free, WSLOTS // 2)

                def fill_block(j, r):
                    act.wait_ge(block_free, j + 1)
                    for m in range(WB // 2):
                        two = 4 + 2 * (m % 2)
                        act.wait_ge(win_counted, WB * j + 2 * (m + 1) + WSLOTS)
                        act.activation(blocks[:, r, :, 2 * m * WD:2 * (m + 1) * WD].rearrange("p a (w d) -> p a w d", w=2),
                                       ps[:, two:two + 2, 0:WCOLS].rearrange("p w (d a) -> p a w d", a=J), ACT.Copy)\
                            .then_inc(block_part, 1)
                        act.wait_ge(block_part, (WB // 2) * j + m + 1)
                        act.sem_inc(bank_free, 1)

                with act.Fori(0, J // 2) as i:
                    for r in range(2):
                        fill_block(2 * i + r, r)
                fill_block(J - 1, 0)
                with act.Fori(0, LAYERS) as l:
                    act.wait_ge(exp_in, l + 1)
                    act.activation(ybuf[:, :, :], ybuf[:, :, :], ACT.Exp).then_inc(exp_done, 1)
                    layer_product(l)

            act.wait_ge(way_known, 1)
            counts = act.to_reg(act.value_load(use_counts[0:1, 0:1], min_val=0, max_val=1))
            with act.If_ne(counts, 0):
                by_counts()
            with act.Else():
                by_edges()
            sqrt(NORM_P)
            with act.Fori(0, NG) as g:
                copy_turned(n_p, g + 1, D)
            with act.Fori(0, NB) as i:
                b = i * SLOTS
                for k in range(SLOTS):
                    act.wait_ge(e1.xt_done, b + k + 1 + SLOTS)
                    act.activation(bufA[:, k, :], xT[k], ACT.Silu).then_inc(e1.silu1_done, 1)
                for k in range(SLOTS):
                    act.wait_ge(e1.w2_done, b + k + 1)
                    act.wait_ge(e1.scan_done, b + k + 1)
                    act.activation(bufB[:, k, :], xT[k], ACT.Silu, bias=W("b2")).then_inc(e1.silu2_done, 1)
                copy_out(e1, i)
            with act.Fori(0, NG) as g:
                copy_turned(n_s, g + 1, HID)
            with act.Fori(0, NG) as g:
                copy_turned(n_u, g + 1, 2 * D)
            sqrt(NORM_U)
            act.wait_ge(gate_in, 1)
            act.activation(ybuf[:, :, :], ybuf[:, :, :], ACT.Sigmoid).then_inc(gate_done, 1)
            act.wait_ge(u_in, 1)
            act.activation(wide[:, :, :], wide[:, :, :], ACT.Silu).then_inc(u_done, 1)
            with act.Fori(0, NG) as g:
                copy_turned(n_o, g + 1, HID)
            sqrt(NORM_O)

        @block.vector
        def _(dve):
            class Chain:
                def __init__(self, s, base=0):
                    self.s, self.base, self.n = s, base, 0

                def __call__(self, ins):
                    self.n += 1
                    ins.then_inc(self.s, 1)
                    dve.wait_ge(self.s, self.base + self.n)

            def per_node(a, n):
                return a.unsqueeze(2).to_broadcast([P, a.shape[1], n])

            def per_feature(a, reps):
                return a.unsqueeze(1).to_broadcast([P, reps, a.shape[1]])

            def layernorm(link, n, v, tmp, width):
                link(dve.tensor_reduce(mean[:, :], v, AX.X, ALU.add))
                link(dve.tensor_scalar(mean[:, :], mean[:, :], 1.0 / width, None, ALU.mult))
                link(dve.tensor_tensor(v, v, per_node(mean[:, :], width), ALU.subtract))
                link(dve.tensor_tensor(tmp, v, v, ALU.mult))
                link(dve.tensor_reduce(var[:, :], tmp, AX.X, ALU.add))
                dve.tensor_scalar(var[:, :], var[:, :], 1.0 / width, LN_EPS, ALU.mult, ALU.add).then_inc(var_ready, 1)
                dve.wait_ge(sd_ready, n)
                link(dve.reciprocal(rstd[:, :], rstd[:, :]))
                link(dve.tensor_tensor(v, v, per_node(rstd[:, :], width), ALU.mult))

            def group(buf, g):
                return buf[:, bass.ds(g * GT, GT), :]

            def product(bank, cols):
                return ps[:, bank:bank + 2, :].rearrange("p b c -> p (b c)")[:, 0:GT * cols]\
                    .rearrange("p (t c) -> p t c", c=cols)

            link = Chain(setup)
            dve.sem_inc(e0.scan_done, SLOTS)
            dve.sem_inc(e1.scan_done, SLOTS)
            dve.wait_ge(loaded, LOADS * DMA)
            hi = starts.bitcast(I32)
            link(dve.tensor_scalar(hi, src_l, 7, None, ALU.logical_shift_right))
            link(dve.scalar_tensor_tensor(pack, dst_l, float(J), hi, ALU.mult, ALU.add))
            link(dve.tensor_scalar(pack, pack, 7, None, ALU.logical_shift_left))
            link(dve.tensor_scalar(hi, src_l, P - 1, None, ALU.bitwise_and))
            dve.tensor_tensor(pack, pack, hi, ALU.bitwise_or).then_inc(pack_ready, 1)
            dve.wait_ge(pack_ready, 1)
            link(dve.tensor_tensor(starts, dst_l, prev_l, ALU.not_equal))
            dve.tensor_scalar(drop_l, starts, -BIG, None, ALU.mult).then_inc(masks_ready, 1)
            dve.tensor_scalar(keep_l, starts, -1.0, 1.0, ALU.mult, ALU.add).then_inc(masks_ready, 1)

            dve.wait_ge(ids_ready, 4)
            link(dve.tensor_copy(start_f[:, :], end_idx[:, :]))
            junk = ends[:, :, :].rearrange("p j f -> p (j f)")[:, 0:ET]
            for j in range(J):
                link(dve.tensor_scalar(junk, firsts, start_f[:, j:j + 1], 0.0, ALU.is_le, ALU.add,
                                       accum_out=mean[:, j:j + 1]))
            link(dve.tensor_scalar(mean[:, :], mean[:, :], -1.0, 0.0, ALU.add, ALU.max))
            dve.tensor_copy(end_idx[:, :], mean[:, :]).then_inc(tile_known, 1)
            link(dve.tensor_copy(win_base[:, :], win_no[:, :]))
            link(dve.tensor_scalar(win_base[:, :], win_base[:, :], float(WCOLS), None, ALU.mult))
            link(dve.tensor_copy(step_f[:, :], step_i[:, :]))
            link(dve.tensor_copy(iota_w[:, :], iota_i[:, :]))
            link(dve.tensor_copy(iota_p[:, :], iota_i[:, 0:P]))
            link(dve.scalar_tensor_tensor(bound[:, :], V("gamma"), -1.0, V("gamma"), ALU.mult, ALU.max))
            babs = ends[:, 0:LAYERS, 0:D]
            beta = V("beta").rearrange("p (l d) -> p l d", l=LAYERS)
            by_layer = bound[:, :].rearrange("p (l d) -> p l d", l=LAYERS)
            link(dve.scalar_tensor_tensor(babs, beta, -1.0, beta, ALU.mult, ALU.max))
            link(dve.scalar_tensor_tensor(by_layer, by_layer, NORM_MAX, babs, ALU.mult, ALU.add))
            link(dve.tensor_scalar(bound[:, :], bound[:, :], 0.5, None, ALU.mult))
            dve.wait_ge(tile_fetched, J * DMA)
            link(dve.tensor_tensor(ends[:, :, :], wide[:, :, :].bitcast(I32), per_node(start_f[:, :], P), ALU.is_le))
            link(dve.tensor_reduce(var[:, :], ends[:, :, :], AX.X, ALU.add))
            dve.scalar_tensor_tensor(end_f[:, :], mean[:, :], float(P), var[:, :], ALU.mult, ALU.add).then_inc(end_known, 1)
            dve.wait_ge(end_known, 1)
            link(dve.tensor_scalar(var[:, :], end_f[:, :], -1.0, 0.0, ALU.add, ALU.max))
            dve.tensor_copy(end_idx[:, :], var[:, :]).then_inc(ends_known, 1)
            dve.wait_ge(ends_known, 1)
            dve.wait_ge(start_summed, 1)
            dve.tensor_copy(start_f[:, :], ps[:, 7, 0:J]).then_inc(win_ready, 1)
            dve.wait_ge(win_ready, 1)
            link(dve.tensor_tensor(degree[:, :], end_f[:, :], start_f[:, :], ALU.subtract))
            link(dve.tensor_scalar(has[:, :], degree[:, :], 1.0, None, ALU.min))

            link(dve.memset(peak[:, :], 0.0))
            dve.wait_ge(win_loaded, 2 * (J // WG) * DMA)
            link(dve.tensor_copy(win_int[0:WQ, :], win_first[0:WQ, :]))
            link(dve.tensor_scalar(win_int[0:WQ, :], win_int[0:WQ, :], 5, None, ALU.logical_shift_right))
            link(dve.tensor_copy(rstd[0:WQ, 0:WG], win_int[0:WQ, :]))
            link(dve.tensor_tensor(gran_f[0:WQ, :, :], rstd[0:WQ, 0:WG].unsqueeze(2).to_broadcast([WQ, WG, WE // GE]),
                                   step_f[0:WQ, :].unsqueeze(1).to_broadcast([WQ, WG, WE // GE]), ALU.add))
            dve.tensor_copy(gran[0:WQ, :, :], gran_f[0:WQ, :, :]).then_inc(gran_known, 1)
            link(dve.tensor_tensor(win_end[0:WQ, :], win_end[0:WQ, :], win_first[0:WQ, :], ALU.subtract))
            link(dve.tensor_reduce(peak[0:WQ, 0:1], win_end[0:WQ, :], AX.X, ALU.max))
            link(dve.tensor_reduce(peak[:, 1:2], degree[:, :], AX.X, ALU.max))
            link(dve.tensor_reduce(peak[:, 2:3], bound[:, :], AX.X, ALU.max))
            link(dve.tensor_scalar(peak[:, 0:1], peak[:, 0:1], float(MAX_WINDOW), None, ALU.is_gt))
            link(dve.tensor_scalar(peak[:, 1:2], peak[:, 1:2], float(MAX_DEGREE), None, ALU.is_gt))
            link(dve.tensor_scalar(peak[:, 2:3], peak[:, 2:3], 0.5 * MAX_RANGE, None, ALU.is_gt))
            link(dve.tensor_reduce(peak[:, 3:4], peak[:, 0:3], AX.X, ALU.add))

            link = Chain(chain["in"])
            link(dve.tensor_copy(ybuf[:, :, :], xres[:, :, :]))
            layernorm(link, NORM_IN, ybuf[:, :, :], wide[:, :, 0:D], D)
            link(dve.tensor_scalar(ybuf[:, :, :], ybuf[:, :, :], 0.0, None, ALU.max))
            with dve.Fori(0, NG) as g:
                dve.tensor_copy(stage[:, :, 0:D], group(ybuf, g)).then_inc(n_in.staged, 1)
                dve.wait_ge(n_in.product, g + 1)
                dve.tensor_tensor(group(hbuf, g), product(2, D), per_feature(V("b_in"), GT), ALU.add).then_inc(n_in.used, 1)
                dve.wait_ge(n_in.used, g + 1)
                dve.sem_inc(alone["dve"], 1)
            dve.sem_inc(h_ready, 1)

            link = Chain(chain["way"])
            byf = hbuf[:, :, :].rearrange("p j d -> p d j")
            link(dve.tensor_reduce(extreme[:, 0:D], byf, AX.X, ALU.max))
            link(dve.tensor_reduce(extreme[:, D:2 * D], byf, AX.X, ALU.min))
            dve.tensor_scalar(extreme[:, D:2 * D], extreme[:, D:2 * D], -1.0, None, ALU.mult).then_inc(ext_ready, 1)
            dve.wait_ge(ext_turned, 1)
            link(dve.tensor_reduce(rstd[:, 0:1], ps[:, 0, 0:P], AX.X, ALU.max))
            dve.tensor_scalar(diag[:, :], ident[:, :], rstd[:, 0:1], None, ALU.mult).then_inc(diag_ready, 2)
            dve.wait_ge(ext_spread, 2)
            link(dve.tensor_copy(diag[:, :], ps[:, 1, 0:2 * D]))
            link(dve.tensor_copy(shift_c[:, :], diag[:, 0:D]))
            link(dve.tensor_tensor(diag[:, 0:D], diag[:, 0:D], diag[:, D:2 * D], ALU.add))
            link(dve.tensor_reduce(rstd[:, 0:1], diag[:, 0:D], AX.X, ALU.max))
            link(dve.tensor_scalar(rstd[:, 0:1], rstd[:, 0:1], MAX_RANGE, None, ALU.is_le))
            link(dve.tensor_scalar(rstd[:, 1:2], ps[:, 2, 0:1], 0.0, None, ALU.is_equal))
            link(dve.tensor_tensor(rstd[:, 0:1], rstd[:, 0:1], rstd[:, 1:2], ALU.mult))
            dve.tensor_copy(use_counts[:, :], rstd[:, 0:1]).then_inc(way_known, 1)
            dve.wait_ge(way_known, 1)

            def layer_tail(l):
                link = Chain(chain["l"], l * LAYER_LINKS)
                with dve.Fori(0, NG) as g:
                    n = l * NG + g + 1
                    dve.tensor_copy(stage[:, :, 0:D], group(hbuf, g)).then_inc(n_l.staged, 1)
                    dve.tensor_copy(stage[:, :, D:2 * D], group(ends, g)[:, :, 0:D]).then_inc(n_l.staged, 1)
                    dve.wait_ge(n_l.product, n)
                    bias = rowvec[:, bass.ds(l * D + V_COLS["b_l"][0], D)]
                    dve.tensor_tensor(group(ybuf, g), product(2, D), per_feature(bias, GT), ALU.add).then_inc(n_l.used, 1)
                    dve.wait_ge(n_l.used, n)
                    dve.sem_inc(alone["dve"], 1)
                layernorm(link, NORM_L + l, ybuf[:, :, :], wide[:, :, 0:D], D)
                for name, op in (("gamma", ALU.mult), ("beta", ALU.add)):
                    row = rowvec[:, bass.ds(l * D + V_COLS[name][0], D)]
                    link(dve.tensor_tensor(ybuf[:, :, :], ybuf[:, :, :], per_feature(row, J), op))
                link(dve.tensor_scalar(ybuf[:, :, :], ybuf[:, :, :], 0.0, 0.5, ALU.max, ALU.mult))
                dve.scalar_tensor_tensor(hbuf[:, :, :], hbuf[:, :, :], 0.5, ybuf[:, :, :], ALU.mult, ALU.add)\
                    .then_inc(h_ready, 1)
                dve.wait_ge(h_ready, l + 2)
                dve.sem_inc(alone["dve"], 1)
                assert link.n == LAYER_LINKS

            def by_edges():
                dve.memset(top[:, 0:1], 0.0).then_inc(e0.top_carried, 1)
                dve.memset(scan[:, 0:1], 0.0).then_inc(e0.scan_carried, 1)
                with dve.Fori(0, LAYERS) as l:
                    with dve.Fori(0, NB) as i:
                        c = l * NB + i
                        b = c * SLOTS
                        for k in range(SLOTS):
                            lo, hi = k * BE, (k + 1) * BE
                            mask, fall = segmask[0:D, k, :], bufA[0:D, k, :]
                            dve.wait_ge(e0.xt_done, b + k + 1 + SLOTS)
                            dve.wait_ge(e0.mask_loaded[k], DMA * (c + 1))
                            dve.wait_ge(e0.back_done, b + k + 1)
                            if k == 0:
                                dve.wait_ge(e0.top_carried, c + 1)
                            else:
                                dve.wait_ge(e0.top_done, b + k)
                            dve.tensor_tensor_scan(top[:, lo + 1:hi + 1], mask, xT[k][0:D, :], top[:, lo:lo + 1],
                                                   ALU.add, ALU.max).then_inc(e0.top_done, 1)
                            dve.wait_ge(e0.top_done, b + k + 1)
                            dve.wait_ge(e0.scan_done, b + k + 1)
                            dve.tensor_tensor(fall, top[:, lo:hi], top[:, lo + 1:hi + 1], ALU.subtract).then_inc(e0.diff_done, 1)
                            dve.wait_ge(e0.diff_done, b + k + 1)
                            dve.tensor_tensor(fall, fall, mask, ALU.add).then_inc(e0.fall_done, 1)
                        dve.tensor_copy(top[:, 0:1], top[:, BODY:BODY + 1]).then_inc(e0.top_carried, 1)
                        for k in range(SLOTS):
                            lo, hi = k * BE, (k + 1) * BE
                            dve.wait_ge(e0.decay_done, b + k + 1)
                            dve.wait_ge(e0.term_done, b + k + 1 + SLOTS)
                            if k == 0:
                                dve.wait_ge(e0.scan_carried, c + 1)
                            else:
                                dve.wait_ge(e0.scan_done, b + k + SLOTS)
                            dve.tensor_tensor_scan(scan[0:D, lo + 1:hi + 1], bufA[0:D, k, :], bufB[0:D, k, :],
                                                   scan[0:D, lo:lo + 1], ALU.mult, ALU.add).then_inc(e0.scan_done, 1)
                        dve.wait_ge(e0.scan_done, b + SLOTS + SLOTS)
                        dve.tensor_copy(scan[0:D, 0:1], scan[0:D, BODY:BODY + 1]).then_inc(e0.scan_carried, 1)

                    link = Chain(chain["agg"], 2 * l)
                    dve.wait_ge(e0.ends_fetched, (l + 1) * (J * DMA))
                    dve.tensor_scalar(ends[:, :, D:P], ends[:, :, D:P], SUM_EPS, None, ALU.max).then_inc(floored, 1)
                    dve.wait_ge(ln_done, l + 1)
                    link(dve.tensor_tensor(ends[:, :, 0:D], ends[:, :, 0:D], ends[:, :, D:P], ALU.add))
                    link(dve.tensor_tensor(ends[:, :, 0:D], ends[:, :, 0:D], per_node(has[:, :], D), ALU.mult))
                    dve.sem_inc(alone["dve"], 1)
                    layer_tail(l)
                dve.wait_ge(h_stored, DMA * (LAYERS + 1))

            def by_counts():
                dve.wait_ge(gran_fetched, WG * (WE // GE) * DMA)
                link = Chain(chain["way"], WAY_LINKS)
                ka, kb = key_a.bitcast(I32), key_b.bitcast(I32)
                link(dve.tensor_scalar(ka, win_edges, 7, None, ALU.logical_shift_right))
                link(dve.tensor_scalar(kb, win_edges, P - 1, None, ALU.bitwise_and))
                by_window = key_a.rearrange("p (g e) -> p g e", g=WG)
                dve.tensor_tensor(by_window, ka.rearrange("p (g e) -> p g e", g=WG),
                                  win_base[0:WQ, :].unsqueeze(2).to_broadcast([WQ, WG, WE]), ALU.subtract)\
                    .then_inc(keys_ready, 1)
                dve.tensor_copy(key_b, kb).then_inc(keys_ready, 1)
                dve.wait_ge(keys_copied, 4 * WT)
                with dve.Fori(0, NW // WSLOTS) as i:
                    for s in range(WSLOTS):
                        w = WSLOTS * i + s
                        dve.wait_ge(win_counted, w + 1)
                        for t in range(WT):
                            dve.tensor_scalar(hot_a[:, s, t, :], iota_w[:, :], keyT_a[:, t, bass.ds(w, 1)], None, ALU.is_equal)\
                                .then_inc(hot_ready, 1)
                            dve.tensor_scalar(hot_b[:, s, t, :], iota_p[:, :], keyT_b[:, t, bass.ds(w, 1)], None, ALU.is_equal)\
                                .then_inc(hot_ready, 1)

                dve.sem_inc(sums_read, 2)
                with dve.Fori(0, LAYERS) as l:
                    link = Chain(chain["exp"], 2 * l)
                    dve.tensor_tensor(ybuf[:, :, :], hbuf[:, :, :], per_feature(shift_c[:, :], J), ALU.subtract).then_inc(exp_in, 1)
                    dve.wait_ge(exp_done, l + 1)
                    for n in range(PARTS):
                        part = parts[:, :, n * D:(n + 1) * D]
                        dve.tensor_copy(part, ybuf[:, :, :]).then_inc(parts_ready, 1)
                        if n < PARTS - 1:
                            dve.wait_ge(parts_ready, PARTS * l + n + 1)
                            link(dve.tensor_tensor(ybuf[:, :, :], ybuf[:, :, :], part, ALU.subtract))

                    def read_sums(j, r):
                        dve.wait_ge(block_used, l * J + j + 1 + RING)
                        dve.tensor_reduce(ends[:, bass.ds(j, 1), D:P].rearrange("p o d -> p (o d)"),
                                          ps[:, 5 + r % 2, 0:PARTS * D].rearrange("p (n d) -> p d n", n=PARTS), AX.X, ALU.add)\
                            .then_inc(sums_read, 1)

                    with dve.Fori(0, BODIES) as i:
                        for r in range(RING):
                            read_sums(RING * i + r, r)
                    read_sums(J - 1, 0)
                    link = Chain(chain["sum"], 3 * l)
                    dve.wait_ge(sums_read, J * (l + 1) + 2)
                    dve.tensor_scalar(ends[:, :, D:P], ends[:, :, D:P], SUM_EPS, None, ALU.max).then_inc(floored, 1)
                    dve.wait_ge(ln_done, l + 1)
                    link(dve.tensor_tensor(ends[:, :, 0:D], ends[:, :, D:P], per_feature(shift_c[:, :], J), ALU.add))
                    link(dve.tensor_tensor(ends[:, :, 0:D], ends[:, :, 0:D], per_node(has[:, :], D), ALU.mult))
                    link(dve.scalar_tensor_tensor(shift_c[:, :], shift_c[:, :], 0.5, bound[:, bass.ds(l * D, D)], ALU.mult, ALU.add))
                    dve.sem_inc(alone["dve"], 1)
                    layer_tail(l)

            assert link.n == WAY_LINKS
            counts = dve.to_reg(dve.value_load(use_counts[0:1, 0:1], min_val=0, max_val=1))
            with dve.If_ne(counts, 0):
                by_counts()
            with dve.Else():
                by_edges()

            link = Chain(chain["p"])
            dve.tensor_tensor(xres[:, :, :], xres[:, :, :], hbuf[:, :, :], ALU.add).then_inc(x_ready, 1)
            dve.wait_ge(x_ready, 1)
            link(dve.tensor_copy(ybuf[:, :, :], xres[:, :, :]))
            layernorm(link, NORM_P, ybuf[:, :, :], wide[:, :, 0:D], D)
            dve.memset(scan[:, 0:1], 0.0).then_inc(e1.scan_carried, 1)
            link(dve.tensor_scalar(hbuf[:, :, :], ybuf[:, :, :], 0.0, None, ALU.max))
            with dve.Fori(0, NG) as g:
                dve.tensor_copy(stage[:, :, 0:D], group(hbuf, g)).then_inc(n_p.staged, 1)
                dve.wait_ge(n_p.product, g + 1)
                dve.tensor_tensor(group(wide, g), product(2, HID), per_feature(V("b1"), GT), ALU.add).then_inc(n_p.used, 1)
                dve.wait_ge(n_p.used, g + 1)
                dve.sem_inc(alone["dve"], 1)
            dve.sem_inc(p_ready, 1)

            with dve.Fori(0, NB) as i:
                b = i * SLOTS
                for k in range(SLOTS):
                    lo, hi = k * BE, (k + 1) * BE
                    dve.wait_ge(e1.mask_loaded[k], DMA * (i + 1))
                    dve.wait_ge(e1.silu2_done, b + k + 1 + SLOTS)
                    dve.wait_ge(e1.back_done, b + k + 1)
                    if k == 0:
                        dve.wait_ge(e1.scan_carried, i + 1)
                    else:
                        dve.wait_ge(e1.scan_done, b + k + SLOTS)
                    dve.tensor_tensor_scan(scan[:, lo + 1:hi + 1], segmask[:, k, :], bufB[:, k, :], scan[:, lo:lo + 1],
                                           ALU.mult, ALU.add).then_inc(e1.scan_done, 1)
                dve.wait_ge(e1.scan_done, b + SLOTS + SLOTS)
                dve.tensor_copy(scan[:, 0:1], scan[:, BODY:BODY + 1]).then_inc(e1.scan_carried, 1)

            link = Chain(chain["s"])
            link(dve.tensor_tensor(ybuf[:, :, :], per_node(degree[:, :], D), per_feature(V("b3"), J), ALU.mult))
            dve.wait_ge(e1.ends_fetched, J * DMA)
            with dve.Fori(0, NG) as g:
                dve.tensor_tensor(stage[:, :, :], group(ends, g), per_node(has[:, bass.ds(g * GT, GT)], P), ALU.mult)\
                    .then_inc(n_s.staged, 1)
                dve.wait_ge(n_s.product, g + 1)
                dve.tensor_tensor(group(ybuf, g), product(2, D), group(ybuf, g), ALU.add).then_inc(n_s.used, 1)
                dve.wait_ge(n_s.used, g + 1)
                dve.sem_inc(alone["dve"], 1)
            with dve.Fori(0, NG) as g:
                dve.tensor_copy(stage[:, :, 0:D], group(hbuf, g)).then_inc(n_u.staged, 1)
                dve.tensor_copy(stage[:, :, D:2 * D], group(ybuf, g)).then_inc(n_u.staged, 1)
                dve.wait_ge(n_u.product, g + 1)
                dve.tensor_tensor(group(wide, g), product(2, HID), per_feature(V("ub1"), GT), ALU.add).then_inc(n_u.used, 1)
                dve.tensor_tensor(group(ybuf, g), product(4, D), per_feature(V("gb"), GT), ALU.add).then_inc(n_u.used, 1)
                dve.wait_ge(n_u.used, 2 * (g + 1))
                dve.sem_inc(alone["dve"], 1)
            dve.sem_inc(gate_in, 1)
            link = Chain(chain["u"])
            layernorm(link, NORM_U, wide[:, :, :], ends[:, :, :], HID)
            link(dve.tensor_tensor(wide[:, :, :], wide[:, :, :], per_feature(V("ln1_g"), J), ALU.mult))
            dve.tensor_tensor(wide[:, :, :], wide[:, :, :], per_feature(V("ln1_b"), J), ALU.add).then_inc(u_in, 1)
            dve.wait_ge(u_done, 1)
            with dve.Fori(0, NG) as g:
                dve.tensor_copy(stage[:, :, :], group(wide, g)).then_inc(n_o.staged, 1)
                dve.wait_ge(n_o.product, g + 1)
                dve.tensor_tensor(group(ends, g)[:, :, 0:D], product(2, D), per_feature(V("ub2"), GT), ALU.add)\
                    .then_inc(n_o.used, 1)
                dve.wait_ge(n_o.used, g + 1)
                dve.sem_inc(alone["dve"], 1)
            link = Chain(chain["o"])
            upd = ends[:, :, 0:D]
            layernorm(link, NORM_O, upd, ends[:, :, D:P], D)
            link(dve.tensor_tensor(upd, upd, per_feature(V("ln2_g"), J), ALU.mult))
            link(dve.tensor_tensor(upd, upd, per_feature(V("ln2_b"), J), ALU.add))
            dve.wait_ge(gate_done, 1)
            link(dve.tensor_tensor(upd, upd, ybuf[:, :, :], ALU.mult))
            link(dve.tensor_tensor(upd, upd, hbuf[:, :, :], ALU.add))
            dve.tensor_tensor(xres[:, :, :], xres[:, :, :], upd, ALU.add).then_inc(y_ready, 1)


LAYER_LINKS = 10
WAY_LINKS = 10


def kernel(**inputs):
    import numpy as np
    import concourse.bacc as bacc
    from concourse.bass_utils import run_bass_kernel_spmd

    a = {k: np.asarray(v) for k, v in inputs.items()}
    f32, i32 = np.float32, np.int32
    x = np.zeros((NPAD, D), f32)
    x[:N_NODES] = a["x"]
    src = np.zeros(EPAD, i32)
    src[:N_EDGES] = a["src"]
    dst = np.full(EPAD, NPAD, i32)
    dst[:N_EDGES] = a["dst"]
    prev = np.full(EPAD, -1, i32)
    prev[1:] = dst[:-1]
    attr = np.zeros((N_ATTR, EPAD + BODY), f32)
    attr[:9, :N_EDGES] = a["edge_attr_9"].T
    attr[9:, :N_EDGES] = a["edge_attr_8"].T
    g1, g0 = "L1_gnn_", "L0_gnn_"
    parts = {"w_l": np.concatenate([a[g0 + "W_l"][l].T for l in range(LAYERS)], axis=1), "w_in": a[g0 + "W_in"].T,
             "W1x": a[g1 + "W1"][:D], "W1e": a[g1 + "W1"][D:], "W2": a[g1 + "W2"], "W3": a[g1 + "W3"],
             "U1": a[g1 + "U1"], "U2": a[g1 + "U2"], "G": a[g1 + "G"], "b2": a[g1 + "b2"].reshape(HID, 1)}
    w = np.zeros((P, W_TOTAL), f32)
    for name, (at, r, c) in W_COLS.items():
        w[:r, at:at + c] = parts[name]
    rowsv = {"b_in": a[g0 + "b_in"], "b_l": a[g0 + "b_l"], "gamma": a[g0 + "gamma_l"], "beta": a[g0 + "beta_l"]}
    rowsv.update({n: a[g1 + n] for n in ("b1", "b3", "ub1", "ln1_g", "ln1_b", "ub2", "ln2_g", "ln2_b", "gb")})
    v = np.concatenate([rowsv[n].reshape(-1) for n in V_COLS]).reshape(1, V_TOTAL)
    arrays = {"x_in": np.ascontiguousarray(x.reshape(J, P, D).transpose(1, 0, 2)), "dst_in": dst.reshape(1, EPAD), "prev_in": prev.reshape(1, EPAD),
              "first_in": np.ascontiguousarray(dst[::P]).reshape(1, ET),
              "src_in": np.ascontiguousarray(src.reshape(ET, P).T), "srcl_in": src.reshape(1, EPAD), "attr_in": attr, "w_in": w, "v_in": v}

    nc = bacc.Bacc("TRN2", target_bir_lowering=False, num_devices=1)
    args = [nc.dram_tensor(n, t.shape, mybir.dt.from_np(t.dtype), kind="ExternalInput").ap() for n, t in arrays.items()]
    out = nc.dram_tensor("out", (P, J, D), F32, kind="ExternalOutput").ap()
    build(nc, *args, out)
    r = run_bass_kernel_spmd(nc, [arrays], core_ids=[0])
    return r.results[0]["out"].transpose(1, 0, 2).reshape(NPAD, D)[:N_NODES]
```

```python
from contextlib import ExitStack

import concourse.bass as bass
from concourse import mybir

F32 = mybir.dt.float32
BF16 = mybir.dt.bfloat16
FP16 = mybir.dt.float16
I32 = mybir.dt.int32
U32 = mybir.dt.uint32
ALU = mybir.AluOpType
ACT = mybir.ActivationFunctionType
AX = mybir.AxisListType

P = 128
N_NODES, D, HID = 6250, 64, 128
N_EDGES, N_ATTR, LAYERS = 200000, 17, 3
J = -(-N_NODES // P)
NPAD = P * J
GT = 7
NG = J // GT
TB = 4
BE = TB * P
SLOTS = 4
BODY = SLOTS * BE
NB = -(-N_EDGES // BODY)
EPAD = NB * BODY
ET = EPAD // P

WD = 8
NW = NPAD // WD
WB = P // WD
WT = 3
WE = WT * P
GE = 32
EROWS = EPAD // GE - P // GE + 1
WG = 7
WQ = NW // WG
WCOLS = WD * J
WSLOTS = 4
QUAD = WSLOTS * WT
DVE_HOTS = QUAD - 1
QUADS = WB // WSLOTS
RING = 6
ARENA_SLOTS = 4
BODIES = J // RING
PARTS = 3
HALVES = (0, (J + 1) // 2), ((J + 1) // 2, J)
MAX_WINDOW = WE - GE + 1
MAX_RANGE = 40.0
NORM_MAX = 8.0

LN_EPS = 1e-5
SUM_EPS = 1e-30
LEAST_SUM = 1e-18
BIG = 1e30
DMA = 16

W_COLS, _at = {}, 0
for _name, _rows, _cols in [("w_l", 2 * D, LAYERS * D), ("w_in", D, D), ("W1x", D, HID), ("W1e", N_ATTR, HID),
                            ("W2", HID, HID), ("W3", HID, D), ("U1", 2 * D, HID), ("U2", HID, D), ("G", 2 * D, D),
                            ("b2", HID, 1), ("ln1_g", HID, 1), ("ln1_b", HID, 1)]:
    W_COLS[_name] = (_at, _rows, _cols)
    _at += _cols
W_TOTAL = _at
V_COLS, _at = {}, 0
for _name, _cols in [("b_in", D), ("b_l", LAYERS * D), ("gamma", LAYERS * D), ("beta", LAYERS * D), ("b1", HID),
                     ("b3", D), ("ub1", HID), ("ub2", D), ("ln2_g", D),
                     ("ln2_b", D), ("gb", D)]:
    V_COLS[_name] = (_at, _cols)
    _at += _cols
V_TOTAL = _at


def build(nc, x_in, dst_in, prev_in, first_in, src_in, srcl_in, attr_in, w_in, v_in, out):
    with ExitStack() as ctx:
        def sb(name, shape, dt=F32):
            return ctx.enter_context(nc.sbuf_tensor(name, shape, dt))

        def sem(name):
            return ctx.enter_context(nc.semaphore(name))

        h_tab = nc.dram_tensor("h_tab", (NPAD, D), F32).ap()
        p_tab = nc.dram_tensor("p_tab", (NPAD, HID), F32).ap()
        scan_rows = nc.dram_tensor("scan_rows", (EPAD, P), F32).ap()
        drop_d = nc.dram_tensor("drop_d", (1, EPAD + BODY), F32).ap()
        keep_d = nc.dram_tensor("keep_d", (1, EPAD + BODY), F32).ap()
        edge_d = nc.dram_tensor("edge_d", (EPAD // GE, GE), I32).ap()
        edge_w = nc.dram_tensor("edge_w", (EROWS, P), I32).ap()
        count_d = nc.dram_tensor("count_d", (J, P, J * P), FP16).ap()

        weights = sb("weights", [P, W_TOTAL])
        rowvec = sb("rowvec", [P, V_TOTAL])
        ident = sb("ident", [P, P])
        neg_ident = sb("neg_ident", [D, D])
        ones = sb("ones", [P, P])
        shift = sb("shift", [P, P])
        wrap = sb("wrap", [P, P])
        src_all = sb("src_all", [P, ET + SLOTS * TB], I32)
        xres = sb("xres", [P, J, D])
        hbuf = sb("hbuf", [P, J, D])
        ybuf = sb("ybuf", [P, J, D])
        wide = sb("wide", [P, J, P])
        ends = sb("ends", [P, J, P])
        mean, var, rstd, end_tile, end_f, start_f, has, degree = (sb(n, [P, J]) for n in (
            "mean", "var", "rstd", "end_tile", "end_f", "start_f", "has", "degree"))
        end_idx = sb("end_idx", [P, J], I32)
        stage = sb("stage", [P, 2, GT, P])
        stageT = sb("stageT", [P, 2, GT * P])
        idx = sb("idx", [P, SLOTS, TB], I32)
        win_no, win_base = sb("win_no", [P, WG], I32), sb("win_base", [P, WG])
        win_last, win_tile, win_edge = (sb(n, [P, 2 * WG]) for n in ("win_last", "win_tile", "win_edge"))
        win_int = sb("win_int", [P, 2 * WG], I32)
        gran_f, gran = sb("gran_f", [P, WG, WT]), sb("gran", [P, WG, WT], I32)
        step_i, step_f = sb("step_i", [P, WT], I32), sb("step_f", [P, WT])
        node_no, after_node, sign_sum = (sb(n, [P, J]) for n in ("node_no", "after_node", "sign_sum"))
        iota_w, iota_s = sb("iota_w", [P, WCOLS], FP16), sb("iota_s", [P, P, QUAD], BF16)
        extreme = sb("extreme", [P, 2 * D])
        diag = sb("diag", [P, 2 * D])
        bound = sb("bound", [P, LAYERS * D])
        peak = sb("peak", [P, 4])
        shift_c = sb("shift_c", [P, D])
        use_counts = sb("use_counts", [P, 1], I32)

        arena = sb("arena", [P, 20400])

        def carve(at, n, parts=P):
            return arena[0:parts, at:at + n]

        rows = carve(0, BODY).rearrange("p (k t f) -> p k t f", k=SLOTS, t=TB)
        outrow = carve(2048, BODY).rearrange("p (k t f) -> p k t f", k=SLOTS, t=TB)
        segmask = carve(4096, BODY).rearrange("p (k e) -> p k e", k=SLOTS)
        scan = carve(6144, BODY + 1)
        top = carve(8208, BODY + 1, D)
        bufA = carve(10272, BODY).rearrange("p (k e) -> p k e", k=SLOTS)
        bufB = carve(12320, BODY).rearrange("p (k e) -> p k e", k=SLOTS)
        attrT = carve(14368, BODY, N_ATTR).rearrange("p (k e) -> p k e", k=SLOTS)
        dst_l, prev_l, src_l = (carve(at, ET).bitcast(I32) for at in (10272, 12320, 14368))
        drop_l, keep_l, starts, pack = carve(0, ET), carve(2048, ET), carve(4096, ET), carve(6144, ET).bitcast(I32)
        firsts = carve(8208, ET).bitcast(I32)
        NE = WG * WE
        win_edges = carve(16416, NE, WQ).bitcast(I32)
        iota_i = carve(16416 + NE, WCOLS).bitcast(I32)
        win_rows, win_end_rows = (carve(at, WG * P, WQ).bitcast(I32).rearrange("p (c e) -> p c e", c=WG)
                                  for at in (16416, 16416 + NE + WCOLS))
        win_upto = carve(0, WG * P, WQ).rearrange("p (c e) -> p c e", c=WG)
        key_a, key_b = carve(0, NE, WQ), carve(NE, NE, WQ)
        BLK = J * P
        at = ARENA_SLOTS * BLK // 2
        over_wide = wide[:, :, :].rearrange("p j f -> p (j f)")
        blocks = [(carve(r * BLK // 2, BLK // 2) if r < ARENA_SLOTS else
                   over_wide[:, (r - ARENA_SLOTS) * BLK // 2:(r - ARENA_SLOTS + 1) * BLK // 2])
                  .bitcast(FP16).rearrange("p (a d) -> p a d", a=J) for r in range(RING)]
        keyT_a = carve(at, WT * NW).rearrange("p (i w) -> p i w", i=WT)
        keyT_b = carve(at + WT * NW, WT * (NW + WSLOTS) // 2).bitcast(BF16).rearrange("p (w i) -> p w i", i=WT)
        hot_a = carve(at + 2 * WT * NW, WSLOTS * WT * WCOLS // 2).bitcast(BF16)\
            .rearrange("p (s i c) -> p s i c", s=WSLOTS, i=WT)
        hot_b = carve(at + 2 * WT * NW + WSLOTS * WT * WCOLS // 2, QUAD * P // 2).bitcast(BF16)\
            .rearrange("p (c n) -> p c n", n=QUAD), \
            carve(at + WT * NW + WT * (NW + WSLOTS) // 2, QUAD * P // 2).bitcast(BF16).rearrange("p (c n) -> p c n", n=QUAD)
        squares = stage[:, :, :, :].rearrange("p s t f -> p (s t f)")[:, 0:WCOLS // 2].bitcast(BF16)
        first_parts = carve(2 * BLK // 2, J * PARTS * D // 2).bitcast(BF16).rearrange("p (a c) -> p a c", a=J)
        parts = carve(at, J * PARTS * D // 2).bitcast(BF16).rearrange("p (a c) -> p a c", a=J)

        ps = ctx.enter_context(nc.psum_tensor("ps", [P, 8, 512], F32))
        xT = [ps[:, k, :] for k in range(SLOTS)]
        back = [ps[:, SLOTS + k, :] for k in range(SLOTS)]

        def W(name):
            a, r, c = W_COLS[name]
            return weights[0:r, a:a + c]

        def V(name, a=0, n=None):
            s, c = V_COLS[name]
            return rowvec[:, s + a:s + a + (c if n is None else n)]

        dst_tiles = dst_in.rearrange("o (t e) -> (o t) e", e=P)

        loaded = sem("loaded")
        consts = sem("consts")
        ids_ready = sem("ids_ready")
        setup = sem("setup")
        masks_ready, masks_stored = sem("masks_ready"), sem("masks_stored")
        tile_known, tile_fetched = sem("tile_known"), sem("tile_fetched")
        end_known, start_summed, ends_known = (sem(n) for n in ("end_known", "start_summed", "ends_known"))
        pack_ready, pack_stored = sem("pack_ready"), sem("pack_stored")
        rows_stored = sem("rows_stored")
        edges_loaded = sem("edges_loaded")
        win_tile_known, win_fetched = sem("win_tile_known"), sem("win_fetched")
        win_end_known, win_end_fetched, win_searched = (sem(n) for n in ("win_end_known", "win_end_fetched", "win_searched"))
        gate_scaled = sem("gate_scaled")
        nodes_ready, nodes_searched, degrees_ready = sem("nodes_ready"), sem("nodes_searched"), sem("degrees_ready")
        node_tiles, starts_read, centered = sem("node_tiles"), sem("starts_read"), sem("centered")
        gran_known, gran_fetched = sem("gran_known"), sem("gran_fetched")
        ext_ready, ext_turned, diag_ready, ext_spread, way_known = (sem(n) for n in (
            "ext_ready", "ext_turned", "diag_ready", "ext_spread", "way_known"))
        keys_ready, keys_turned, keys_copied = sem("keys_ready"), sem("keys_turned"), sem("keys_copied")
        hot_ready, win_counted, block_part, block_free, bank_free = (sem(n) for n in (
            "hot_ready", "win_counted", "block_part", "block_free", "bank_free"))
        src_hot_ready, act_hot_ready, square_ready = (sem(n) for n in ("src_hot_ready", "act_hot_ready", "square_ready"))
        block_stored = [sem(f"block_stored{r}") for r in range(2)]
        block_loaded = [sem(f"block_loaded{r}") for r in range(RING)]
        exp_in, exp_done, rest_ready, part_done, parts_ready, block_used, sums_read = (sem(n) for n in (
            "exp_in", "exp_done", "rest_ready", "part_done", "parts_ready", "block_used", "sums_read"))
        floored, ln_done = sem("floored"), sem("ln_done")
        h_ready, h_stored, p_stored = (sem(n) for n in ("h_ready", "h_stored", "p_stored"))
        x_ready, y_ready, y_stored = sem("x_ready"), sem("y_ready"), sem("y_stored")
        attr_loaded = [sem(f"attr_loaded{k}") for k in range(SLOTS)]

        class PassSems:
            def __init__(self, tag):
                self.idx_ready = sem(tag + "idx_ready")
                self.xt_done = sem(tag + "xt_done")
                self.scan_done = sem(tag + "scan_done")
                self.scan_carried = sem(tag + "scan_carried")
                self.back_done = sem(tag + "back_done")
                self.out_ready = sem(tag + "out_ready")
                self.out_free = sem(tag + "out_free")
                self.gathered = [sem(f"{tag}gathered{k}") for k in range(SLOTS)]
                self.mask_loaded = [sem(f"{tag}mask_loaded{k}") for k in range(SLOTS)]
                self.stored = [sem(f"{tag}stored{k}") for k in range(SLOTS)]

        class LayerPassSems(PassSems):
            def __init__(self, tag):
                super().__init__(tag)
                self.top_done = sem(tag + "top_done")
                self.diff_done = sem(tag + "diff_done")
                self.fall_done = sem(tag + "fall_done")
                self.shift_done = sem(tag + "shift_done")
                self.decay_done = sem(tag + "decay_done")
                self.term_done = sem(tag + "term_done")
                self.top_carried = sem(tag + "top_carried")
                self.ends_fetched = sem(tag + "ends_fetched")

        class MessagePassSems(PassSems):
            def __init__(self, tag):
                super().__init__(tag)
                self.silu1_done = sem(tag + "silu1_done")
                self.w2_done = sem(tag + "w2_done")
                self.silu2_done = sem(tag + "silu2_done")
                self.ends_fetched = [sem(f"{tag}ends_fetched{n}") for n in range(2)]
                self.ends_ready = sem(tag + "ends_ready")

        squares_summed = sem("squares_summed")
        node_staged, node_turned, node_copied, node_product, node_used = (sem(n) for n in (
            "node_staged", "node_turned", "node_copied", "node_product", "node_used"))
        G_IN, G_LAYER = 0, NG
        G_TABLE, G_SUM, G_UPDATE, G_OUT = (NG * (1 + LAYERS + n) for n in range(4))

        e0, e1 = LayerPassSems("l0_"), MessagePassSems("l1_")
        chain = {t: sem("chain_" + t) for t in ("in", "l", "p", "u", "o", "s", "agg", "way")}
        var_ready, sd_ready = sem("var_ready"), sem("sd_ready")
        NORM_IN, NORM_L, NORM_P, NORM_U, NORM_O = 1, 2, 2 + LAYERS, 3 + LAYERS, 4 + LAYERS
        gate_in, gate_done, x_summed = (sem(n) for n in ("gate_in", "gate_done", "x_summed"))

        alone = {e: sem("alone_" + e) for e in ("sp", "act", "pe", "pool", "dve")}

        block = ctx.enter_context(nc.Block())
        LOADS = 5

        @block.sync
        def _(sp):
            sp.sem_inc(e0.out_free, 1)
            sp.sem_inc(e1.out_free, 1)
            for t, d in ((dst_l, dst_in), (src_l, srcl_in)):
                sp.dma_start(t, d.rearrange("o (p e) -> (o p) e", p=P)).then_inc(edges_loaded, DMA)
            sp.dma_start(firsts, first_in.partition_broadcast(P)).then_inc(edges_loaded, DMA)
            sp.dma_start(prev_l, prev_in.rearrange("o (p e) -> (o p) e", p=P)).then_inc(loaded, DMA)
            sp.dma_start(xres[:, :, :], x_in).then_inc(loaded, DMA)
            sp.dma_start(weights[:, :], w_in).then_inc(loaded, DMA)
            sp.dma_start(rowvec[:, :], v_in.partition_broadcast(P)).then_inc(loaded, DMA)
            sp.dma_start(src_all[:, :], src_in).then_inc(loaded, DMA)

            sp.wait_ge(pack_ready, 1)
            sp.dma_start(edge_d.rearrange("(p g) e -> p (g e)", p=P), pack).then_inc(pack_stored, DMA)
            sp.wait_ge(pack_stored, DMA)
            sp.dma_start(edge_w, bass.AP(edge_d.tensor, 0, [[GE, EROWS], [1, P]])).then_inc(rows_stored, DMA)
            sp.wait_ge(masks_ready, 2)
            for m, t in ((drop_d, drop_l), (keep_d, keep_l)):
                sp.dma_start(m[:, 0:EPAD].rearrange("o (p e) -> (o p) e", p=P), t).then_inc(masks_stored, DMA)
                sp.dma_start(m[:, EPAD:EPAD + ET], t[0:1, :]).then_inc(masks_stored, DMA)
                sp.dma_start(m[:, EPAD + ET:EPAD + BODY], t[1:2, 0:BODY - ET]).then_inc(masks_stored, DMA)
            sp.wait_ge(masks_stored, 6 * DMA)

            def store_h():
                sp.dma_start(h_tab.rearrange("(j p) d -> p j d", p=P), hbuf[:, :, :])\
                  .then_inc(h_stored, DMA)

            def store_rows(e, c, i):
                for k in range(SLOTS):
                    sp.wait_ge(e.out_ready, SLOTS * c + k + 1 + SLOTS)
                    sp.dma_start(scan_rows[bass.ds(i * BODY + k * BE, BE), :].rearrange("(t p) f -> p t f", p=P),
                                 outrow[:, k, :, :]).then_inc(e.stored[k], DMA)
                for k in range(SLOTS):
                    sp.wait_ge(e.stored[k], DMA * (c + 1))
                sp.sem_inc(e.out_free, 1)

            def by_edges():
                for k in range(SLOTS):
                    sp.dma_start(segmask[0:D, k, :], drop_d[:, k * BE:(k + 1) * BE].partition_broadcast(D))\
                      .then_inc(e0.mask_loaded[k], DMA)
                sp.wait_ge(h_ready, 1)
                store_h()
                with sp.Fori(0, LAYERS) as l:
                    with sp.Fori(0, NB) as i:
                        c = l * NB + i
                        for k in range(SLOTS):
                            sp.wait_ge(e0.fall_done, SLOTS * c + k + 1)
                            sp.dma_start(segmask[0:D, k, :],
                                         drop_d[:, bass.ds((i + 1) * BODY + k * BE, BE)].partition_broadcast(D))\
                              .then_inc(e0.mask_loaded[k], DMA)
                        store_rows(e0, c, i)
                    sp.wait_ge(h_ready, l + 2)
                    store_h()
                for k in range(SLOTS):
                    sp.wait_ge(e0.mask_loaded[k], DMA * (LAYERS * NB + 1))

            def by_counts():
                def store_block(j, r, n):
                    sp.wait_ge(block_part, (WB // 2) * (j + 1))
                    sp.dma_start(count_d[bass.ds(j, 1), :, :].rearrange("o p c -> (o p) c"),
                                 blocks[r].rearrange("p a d -> p (a d)")).then_inc(block_stored[r], DMA)
                    sp.wait_ge(block_stored[r], DMA * n)
                    sp.sem_inc(block_free, 1)

                with sp.Fori(0, J // 2) as i:
                    for r in range(2):
                        store_block(2 * i + r, r, i + 1)
                store_block(J - 1, 0, J // 2 + 1)

                def load_block(l, j, r):
                    sp.wait_ge(block_used, l * J + j + 1)
                    sp.dma_start(blocks[r].rearrange("p a d -> p (a d)"),
                                 count_d[bass.ds(j, 1), :, :].rearrange("o p c -> (o p) c"))\
                      .then_inc(block_loaded[r], DMA)

                sp.wait_ge(end_known, 1)
                with sp.Fori(0, LAYERS - 1) as m:
                    l = m + 1
                    sp.wait_ge(block_used, l * J + RING)
                    sp.sem_inc(alone["sp"], 1)
                    with sp.Fori(0, BODIES) as i:
                        for r in range(RING):
                            load_block(l, RING * i + r, r)
                    load_block(l, J - 1, 0)

            sp.wait_ge(way_known, 1)
            counts = sp.to_reg(sp.value_load(use_counts[0:1, 0:1], min_val=0, max_val=1))
            with sp.If_ne(counts, 0):
                by_counts()
            with sp.Else():
                by_edges()

            sp.wait_ge(x_ready, 1)
            for k in range(SLOTS):
                sp.dma_start(segmask[:, k, :], keep_d[:, k * BE:(k + 1) * BE].partition_broadcast(P))\
                  .then_inc(e1.mask_loaded[k], DMA)
                sp.dma_start(attrT[:, k, :], attr_in[:, k * BE:(k + 1) * BE]).then_inc(attr_loaded[k], DMA)
            with sp.Fori(0, NG) as g:
                sp.wait_ge(node_used, G_TABLE + g + 3)
                sp.dma_start(p_tab.rearrange("(j p) d -> p j d", p=P)[:, bass.ds(g * GT, GT), :], wide[:, bass.ds(g * GT, GT), :])\
                  .then_inc(p_stored, DMA)
            with sp.Fori(0, NB) as i:
                for k in range(SLOTS):
                    sp.wait_ge(e1.xt_done, SLOTS * i + k + 1 + SLOTS)
                    sp.dma_start(attrT[:, k, :], attr_in[:, bass.ds((i + 1) * BODY + k * BE, BE)])\
                      .then_inc(attr_loaded[k], DMA)
                for k in range(SLOTS):
                    sp.wait_ge(e1.scan_done, SLOTS * i + k + 1 + SLOTS)
                    sp.dma_start(segmask[:, k, :],
                                 keep_d[:, bass.ds((i + 1) * BODY + k * BE, BE)].partition_broadcast(P))\
                      .then_inc(e1.mask_loaded[k], DMA)
                store_rows(e1, i, i)
            for k in range(SLOTS):
                sp.wait_ge(e1.mask_loaded[k], DMA * (NB + 1))
                sp.wait_ge(attr_loaded[k], DMA * (NB + 1))
            sp.wait_ge(y_ready, 1)
            sp.dma_start(out, xres[:, :, :]).then_inc(y_stored, DMA)
            sp.wait_ge(y_stored, DMA)

        @block.gpsimd
        def _(pool):
            for t in (ident, neg_ident, shift, wrap):
                pool.memset(t[:, :], 0.0).then_inc(consts, 1)
            pool.memset(ones[:, :], 1.0).then_inc(consts, 1)
            pool.iota(end_idx[:, :], [[P, J]], base=0, channel_multiplier=1).then_inc(ids_ready, 1)
            pool.iota(win_no[:, :], [[WQ, WG]], base=0, channel_multiplier=1).then_inc(ids_ready, 1)
            pool.iota(step_i[:, :], [[P // GE, WT]], base=0, channel_multiplier=0).then_inc(ids_ready, 1)
            pool.iota(iota_i[:, :], [[1, WCOLS]], base=0, channel_multiplier=0).then_inc(ids_ready, 1)
            pool.wait_ge(consts, 5)
            for t, fill, base, pattern in ((ident, 1.0, 0, [[-1, P]]), (neg_ident, -1.0, 0, [[-1, D]]),
                                           (shift, 1.0, 1, [[-1, P]]), (wrap, 1.0, 1 - P, [[P, P]])):
                pool.affine_select(out=t[:, :], in_=t[:, :], compare_op=ALU.not_equal, fill=fill,
                                   base=base, pattern=pattern, channel_multiplier=1).then_inc(consts, 1)

            pool.wait_ge(win_tile_known, 1)
            for c in range(WG):
                pool.indirect_dma_start(win_rows[:, c, :], None, dst_tiles,
                                        bass.IndirectOffsetOnAxis(ap=win_int[0:WQ, c:c + 1].bitcast(U32), axis=0))\
                    .then_inc(win_fetched, DMA)
            pool.wait_ge(gran_known, 1)
            pool.wait_ge(rows_stored, DMA)
            for g in range(WG):
                for n in range(WT):
                    to = g * WE + n * P
                    pool.indirect_dma_start(win_edges[:, to:to + P], None, edge_w,
                                            bass.IndirectOffsetOnAxis(ap=gran[0:WQ, g, n:n + 1].bitcast(U32), axis=0))\
                        .then_inc(gran_fetched, DMA)
            pool.wait_ge(win_end_known, 1)
            for c in range(WG):
                pool.indirect_dma_start(win_end_rows[:, c, :], None, dst_tiles,
                                        bass.IndirectOffsetOnAxis(ap=win_int[0:WQ, WG + c:WG + c + 1].bitcast(U32), axis=0))\
                    .then_inc(win_end_fetched, DMA)
            pool.wait_ge(tile_known, 1)
            for j in range(J):
                pool.indirect_dma_start(wide[:, j, :].bitcast(I32), None, dst_tiles,
                                        bass.IndirectOffsetOnAxis(ap=end_idx[:, j:j + 1].bitcast(U32), axis=0))\
                    .then_inc(tile_fetched, DMA)
            pool.wait_ge(gran_fetched, WG * WT * DMA)
            pool.wait_ge(tile_fetched, J * DMA)

            def gather(e, c, i, table, width):
                for k in range(SLOTS):
                    pool.wait_ge(e.xt_done, SLOTS * c + k + 1)
                    pool.tensor_copy(idx[:, k, :], src_all[:, bass.ds(i * (SLOTS * TB) + k * TB, TB)])\
                        .then_inc(e.idx_ready, 1)
                    pool.wait_ge(e.idx_ready, SLOTS * c + k + 1)
                    pool.sem_inc(alone["pool"], 1)
                    for t in range(TB):
                        pool.indirect_dma_start(rows[:, k, t, 0:width], None, table,
                                                bass.IndirectOffsetOnAxis(ap=idx[:, k, t:t + 1].bitcast(U32), axis=0))\
                            .then_inc(e.gathered[k], DMA)

            def fetch_end(j, fetched):
                pool.indirect_dma_start(ends[:, j, :], None, scan_rows,
                                        bass.IndirectOffsetOnAxis(ap=end_idx[:, j:j + 1].bitcast(U32), axis=0))\
                    .then_inc(fetched, DMA)

            pool.wait_ge(loaded, LOADS * DMA)
            pool.wait_ge(way_known, 1)
            counts = pool.to_reg(pool.value_load(use_counts[0:1, 0:1], min_val=0, max_val=1))
            with pool.If_eq(counts, 0):
                pool.wait_ge(ends_known, 1)
                with pool.Fori(0, LAYERS) as l:
                    pool.wait_ge(h_stored, DMA * (l + 1))
                    pool.sem_inc(alone["pool"], 1)
                    with pool.Fori(0, NB) as i:
                        gather(e0, l * NB + i, i, h_tab, D)
                    pool.wait_ge(e0.out_free, NB * (l + 1) + 1)
                    pool.sem_inc(alone["pool"], 1)
                    for j in range(J):
                        fetch_end(j, e0.ends_fetched)
            pool.wait_ge(ends_known, 1)
            pool.wait_ge(p_stored, NG * DMA)
            with pool.Fori(0, NB) as i:
                for k in range(SLOTS):
                    pool.wait_ge(e1.idx_ready, SLOTS * i + k + 1)
                    pool.sem_inc(alone["pool"], 1)
                    for t in range(TB):
                        pool.indirect_dma_start(rows[:, k, t, :], None, p_tab,
                                                bass.IndirectOffsetOnAxis(ap=idx[:, k, t:t + 1].bitcast(U32), axis=0))\
                            .then_inc(e1.gathered[k], DMA)
            pool.wait_ge(e1.out_free, NB + 1)
            for g in range(NG):
                for j in range(g * GT, (g + 1) * GT):
                    fetch_end(j, e1.ends_fetched[g % 2])
                if g >= 1:
                    pool.wait_ge(e1.ends_fetched[(g - 1) % 2], ((g - 1) // 2 + 1) * (GT * DMA))
                    pool.sem_inc(e1.ends_ready, 1)
            pool.wait_ge(e1.ends_fetched[(NG - 1) % 2], ((NG - 1) // 2 + 1) * (GT * DMA))
            pool.sem_inc(e1.ends_ready, 1)
            pool.wait_ge(x_summed, 1)
            pool.wait_ge(gate_done, 1)
            gain, bias = (V(n).unsqueeze(1).to_broadcast([P, J, D]) for n in ("ln2_g", "ln2_b"))
            pool.tensor_tensor(hbuf[:, :, :], ybuf[:, :, :], bias, ALU.mult).then_inc(gate_scaled, 1)
            pool.wait_ge(gate_scaled, 1)
            pool.tensor_tensor(ybuf[:, :, :], ybuf[:, :, :], gain, ALU.mult).then_inc(gate_scaled, 1)
            pool.tensor_tensor(hbuf[:, :, :], hbuf[:, :, :], xres[:, :, :], ALU.add).then_inc(gate_scaled, 1)

        @block.tensor
        def _(pe):
            def turn(n, s, width):
                pe.wait_ge(node_staged, n + 1)
                pe.wait_ge(node_copied, n + 1)
                pe.sem_inc(alone["pe"], 1)
                for t in range(GT):
                    last = pe.transpose(ps[0:width, 2 * s + t // TB, (t % TB) * P:(t % TB + 1) * P],
                                        stage[:, s, t, 0:width], ident[:, :])
                last.then_inc(node_turned, 1)

            def multiply(n, s, width, products, slots):
                pe.wait_ge(node_copied, n + 3)
                pe.wait_ge(node_used, n + 3 - slots)
                bank = 4 + 2 * s if slots == 2 else 4
                for w, cols in products:
                    per = 512 // cols
                    for t in range(GT):
                        last = pe.matmul(ps[:, bank + t // per, (t % per) * cols:(t % per + 1) * cols],
                                         stageT[0:width, s, t * P:(t + 1) * P], w, start=True, stop=True)
                    bank += 2
                last.then_inc(node_product, 1)

            def node_phase(n0, width, products, slots=2):
                turn(n0, 0, width)
                with pe.Fori(0, NG // 2) as i:
                    for s in range(2):
                        turn(n0 + 2 * i + s + 1, 1 - s, width)
                        multiply(n0 + 2 * i + s, s, width, products, slots)
                multiply(n0 + NG - 1, 0, width, products, slots)

            pe.sem_inc(node_product, 2)
            pe.sem_inc(e0.xt_done, SLOTS)
            pe.sem_inc(e0.back_done, SLOTS)
            pe.sem_inc(e1.xt_done, SLOTS)
            pe.sem_inc(e1.back_done, SLOTS)
            pe.wait_ge(loaded, LOADS * DMA)
            pe.wait_ge(consts, 9)
            def node_starts():
                pe.wait_ge(end_known, 1)
                pe.matmul(ps[:, 2, 0:J], shift[:, :], end_f[:, :], start=True, stop=False, skip_group_check=True)
                pe.matmul(ps[:, 2, 1:J], wrap[:, :], end_f[:, 0:J - 1], start=False, stop=True, skip_group_check=True)\
                  .then_inc(start_summed, 1)

            node_phase(G_IN, D, [(W("w_in"), D)])
            pe.wait_ge(ext_ready, 1)
            pe.transpose(ps[:, 0, 0:P], extreme[:, :], ident[:, :]).then_inc(ext_turned, 1)
            pe.wait_ge(diag_ready, 2)
            pe.matmul(ps[:, 1, 0:P], ones[:, :], diag[:, :], start=True, stop=True).then_inc(ext_spread, 1)
            pe.matmul(ps[:, 2, 0:1], ones[:, :], peak[:, 3:4], start=True, stop=True).then_inc(ext_spread, 1)

            def layer_product(l):
                node_phase(l * NG + G_LAYER, 2 * D, [(weights[:, bass.ds(l * D + W_COLS["w_l"][0], D)], D)])

            def by_edges():
                node_starts()
                pe.wait_ge(starts_read, 1)
                with pe.Fori(0, LAYERS) as l:
                    with pe.Fori(0, NB) as i:
                        c = l * NB + i
                        b = c * SLOTS
                        for k in range(SLOTS):
                            pe.wait_ge(e0.gathered[k], TB * DMA * (c + 1))
                            pe.wait_ge(e0.term_done, b + k + 1)
                            for t in range(TB):
                                last = pe.matmul(xT[k][0:D, t * P:(t + 1) * P], rows[:, k, t, 0:D], ident[:, :],
                                                 start=(t == 0), stop=(t == TB - 1), skip_group_check=True)
                            last.then_inc(e0.xt_done, 1)
                        for k in range(SLOTS):
                            pe.wait_ge(e0.top_done, b + k + 1)
                            pe.sem_inc(alone["pe"], 1)
                            pe.matmul(xT[k][0:D, :], neg_ident[:, :], top[:, k * BE + 1:(k + 1) * BE + 1],
                                      start=False, stop=True, skip_group_check=True).then_inc(e0.shift_done, 1)
                        for k in range(SLOTS):
                            pe.wait_ge(e0.scan_done, b + k + 1 + SLOTS)
                            pe.wait_ge(e0.out_ready, b + k + 1)
                            pe.sem_inc(alone["pe"], 1)
                            for t in range(TB):
                                o = k * BE + t * P + 1
                                pe.transpose(back[k][:, t * P:t * P + D], top[:, o:o + P], ident[0:D, 0:D])
                                last = pe.transpose(back[k][:, t * P + D:(t + 1) * P], scan[0:D, o:o + P], ident[0:D, 0:D])
                            last.then_inc(e0.back_done, 1)
                    layer_product(l)

            def by_counts():
                pe.wait_ge(keys_ready, 2)
                for n, (key, i) in enumerate((key, i) for key in (key_a, key_b) for i in range(WT)):
                    if n >= 2:
                        pe.wait_ge(keys_copied, 2 * (n - 1))
                    for g in range(WG):
                        last = pe.transpose(ps[:, 2 * (n % 2) + g // 4, (g % 4) * WQ:(g % 4 + 1) * WQ],
                                            key[:, g * WE + i * P:g * WE + (i + 1) * P], ident[0:WQ, 0:WQ])
                    last.then_inc(keys_turned, 1)

                def block_sums(j, r, rhs, a0=0, a1=J):
                    for a in range(a0, a1):
                        last = pe.matmul(ps[:, r % 2, 0:PARTS * D], blocks[r][:, a, :], rhs[:, a, :],
                                         start=(a == 0), stop=(a == J - 1), skip_group_check=True)
                    if a1 == J:
                        last.then_inc(block_used, 1)

                def count_windows(j, q):
                    pe.wait_ge(src_hot_ready, QUADS * j + q + 1)
                    for s in range(WSLOTS):
                        w = WB * j + WSLOTS * q + s
                        if s % 2 == 0:
                            pe.wait_ge(bank_free, (WB // 2) * j + (WSLOTS // 2) * q + s // 2 + 1)
                        pe.wait_ge(hot_ready, DVE_HOTS * (QUADS * j + q) + min(WT * (s + 1), DVE_HOTS))
                        if s == WSLOTS - 1:
                            pe.wait_ge(act_hot_ready, QUADS * j + q + 1)
                        for i in range(WT):
                            last = pe.matmul(ps[:, 4 + s, 0:WCOLS], hot_b[q % 2][:, :, s * WT + i], hot_a[:, s, i, :],
                                             start=(i == 0), stop=(i == WT - 1))
                        last.then_inc(win_counted, 1)

                def first_sums_ready(j):
                    pe.wait_ge(block_part, (WB // 2) * (j + 1))
                    pe.wait_ge(sums_read, j + 1)

                def later_sums(l, j, r, n):
                    pe.wait_ge(sums_read, l * J + j + 1)
                    pe.wait_ge(block_loaded[r], DMA * n)
                    block_sums(j, r, parts)

                pe.sem_inc(block_used, RING)
                pe.sem_inc(win_counted, WSLOTS)
                for q in range(QUADS):
                    count_windows(0, q)
                pe.wait_ge(parts_ready, 2)
                with pe.Fori(0, J // 2) as i:
                    for r in range(2):
                        j = 2 * i + r
                        for q in range(QUADS):
                            count_windows(j + 1, q)
                            if q == 0:
                                first_sums_ready(j)
                            if q < QUADS - 1:
                                block_sums(j, r, first_parts, q * J // (QUADS - 1), (q + 1) * J // (QUADS - 1))
                first_sums_ready(J - 1)
                block_sums(J - 1, 0, first_parts)
                node_starts()
                layer_product(0)
                with pe.Fori(0, LAYERS - 1) as m:
                    l = m + 1
                    pe.wait_ge(parts_ready, 2 * (l + 1))
                    pe.sem_inc(alone["pe"], 1)
                    with pe.Fori(0, BODIES) as i:
                        for r in range(RING):
                            later_sums(l, RING * i + r, r, (BODIES + (r == 0)) * m + i + 1)
                    later_sums(l, J - 1, 0, (BODIES + 1) * (m + 1))
                    layer_product(l)

            pe.wait_ge(way_known, 1)
            counts = pe.to_reg(pe.value_load(use_counts[0:1, 0:1], min_val=0, max_val=1))
            with pe.If_ne(counts, 0):
                by_counts()
            with pe.Else():
                by_edges()
            node_phase(G_TABLE, D, [(W("W1x"), HID)])
            with pe.Fori(0, NB) as i:
                b = i * SLOTS
                for k in range(SLOTS):
                    pe.wait_ge(attr_loaded[k], DMA * (i + 1))
                    pe.wait_ge(e1.silu2_done, b + k + 1)
                    pe.matmul(xT[k], W("W1e"), attrT[:, k, :], start=True, stop=False, skip_group_check=True)
                    pe.wait_ge(e1.gathered[k], TB * DMA * (i + 1))
                    for t in range(TB):
                        last = pe.matmul(xT[k][:, t * P:(t + 1) * P], rows[:, k, t, :], ident[:, :],
                                         start=False, stop=(t == TB - 1), skip_group_check=True)
                    last.then_inc(e1.xt_done, 1)
                for k in range(SLOTS):
                    pe.wait_ge(e1.silu1_done, b + k + 1)
                    pe.matmul(xT[k], W("W2"), bufA[:, k, :], start=True, stop=True).then_inc(e1.w2_done, 1)
                for k in range(SLOTS):
                    pe.wait_ge(e1.scan_done, b + k + 1 + SLOTS)
                    pe.wait_ge(e1.out_ready, b + k + 1)
                    for t in range(TB):
                        o = k * BE + t * P + 1
                        last = pe.transpose(back[k][:, t * P:(t + 1) * P], scan[:, o:o + P], ident[:, :])
                    last.then_inc(e1.back_done, 1)
            node_phase(G_SUM, HID, [(W("W3"), D)])
            node_phase(G_UPDATE, 2 * D, [(W("U1"), HID), (W("G"), D)], slots=1)
            node_phase(G_OUT, HID, [(W("U2"), D)])

        @block.scalar
        def _(act):
            def copy_turned(n, s, width, **func):
                act.wait_ge(node_turned, n + 1)
                act.wait_ge(node_product, n + 1)
                act.activation(stageT[0:width, s, :], ps[0:width, 2 * s:2 * s + 2, :].rearrange("p b c -> p (b c)")[:, 0:GT * P],
                               **(func or {"func": ACT.Copy})).then_inc(node_copied, 1)

            def node_phase(n0, width, **func):
                with act.Fori(0, NG // 2) as i:
                    for s in range(2):
                        copy_turned(n0 + 2 * i + s, s, width, **func)
                copy_turned(n0 + NG - 1, 0, width, **func)

            def sqrt(n):
                act.wait_ge(var_ready, n)
                act.activation(rstd[:, :], var[:, :], ACT.Sqrt).then_inc(sd_ready, 1)

            def copy_out(e, c):
                act.wait_ge(e.out_free, c + 1)
                for k in range(SLOTS):
                    act.wait_ge(e.back_done, c * SLOTS + k + 1 + SLOTS)
                    act.activation(outrow[:, k, :, :].rearrange("p t f -> p (t f)"), back[k], ACT.Copy)\
                        .then_inc(e.out_ready, 1)

            act.sem_inc(node_copied, 2)
            act.sem_inc(e0.term_done, SLOTS)
            act.sem_inc(e0.out_ready, SLOTS)
            act.sem_inc(e1.silu2_done, SLOTS)
            act.sem_inc(e1.out_ready, SLOTS)
            act.wait_ge(nodes_ready, 1)
            act.wait_ge(edges_loaded, 3 * DMA)
            junk = ends[:, :, :].rearrange("p j f -> p (j f)")

            def search(j):
                if j >= 4:
                    act.wait_ge(nodes_searched, j - 3)
                act.activation(junk[:, (j % 4) * ET:(j % 4 + 1) * ET], firsts, ACT.Sign, bias=after_node[:, j:j + 1],
                               accum_out=sign_sum[:, j:j + 1]).then_inc(nodes_searched, 1)

            for g in range(WG):
                act.activation(junk[:, (g % 4) * ET:(g % 4 + 1) * ET], firsts, ACT.Sign, bias=win_last[:, WG + g:WG + g + 1],
                               accum_out=win_tile[:, WG + g:WG + g + 1]).then_inc(win_searched, 1)
                if g >= 3:
                    act.wait_ge(win_searched, g - 2)
            act.wait_ge(win_searched, WG)
            BEFORE = 28
            for j in range(BEFORE):
                search(j)
            sqrt(NORM_IN)
            node_phase(G_IN, D, func=ACT.Relu)
            for j in range(BEFORE, J):
                search(j)

            def layer_product(l):
                act.wait_ge(floored, l + 1)
                act.activation(ends[:, :, D:P], ends[:, :, D:P], ACT.Ln).then_inc(ln_done, 1)
                node_phase(l * NG + G_LAYER, 2 * D)
                sqrt(NORM_L + l)

            def by_edges():
                with act.Fori(0, LAYERS) as l:
                    with act.Fori(0, NB) as i:
                        c = l * NB + i
                        b = c * SLOTS
                        for k in range(SLOTS):
                            act.wait_ge(e0.fall_done, b + k + 1)
                            act.activation(bufA[0:D, k, :], bufA[0:D, k, :], ACT.Exp).then_inc(e0.decay_done, 1)
                            act.wait_ge(e0.shift_done, b + k + 1)
                            act.wait_ge(e0.scan_done, b + k + 1)
                            act.activation(bufB[0:D, k, :], xT[k][0:D, :], ACT.Exp).then_inc(e0.term_done, 1)
                        copy_out(e0, c)
                    layer_product(l)

            def by_counts():
                for n, (key, i) in enumerate((key, i) for key in (keyT_a, keyT_b.rearrange("p w i -> p i w")) for i in range(WT)):
                    act.wait_ge(keys_turned, n + 1)
                    for h, (g0, g1) in enumerate(((0, 4), (4, WG))):
                        act.activation(key[:, i, g0 * WQ:g1 * WQ], ps[:, 2 * (n % 2) + h, 0:(g1 - g0) * WQ], ACT.Copy)\
                            .then_inc(keys_copied, 1)

                act.sem_inc(block_free, 2)
                act.sem_inc(bank_free, WSLOTS // 2)

                def exponential(l, out):
                    for n, (a, b) in enumerate(HALVES):
                        act.wait_ge(exp_in, 2 * l + n + 1)
                        act.activation(ends[:, a:b, 0:D], ybuf[:, a:b, :], ACT.Exp)
                        act.activation(out[:, a:b, 0:D], ybuf[:, a:b, :], ACT.Exp).then_inc(exp_done, 1)
                    for n, (a, b) in enumerate(HALVES):
                        act.wait_ge(rest_ready, 2 * l + n + 1)
                        act.activation(out[:, a:b, D:2 * D], ybuf[:, a:b, :], ACT.Copy).then_inc(part_done, 1)

                def fill_block(j, r, last=False):
                    act.wait_ge(block_free, j + 1)
                    act.wait_ge(block_used, j + RING - 1)
                    for m in range(WB // 2):
                        two = 4 + 2 * (m % 2)
                        act.wait_ge(win_counted, WB * j + 2 * (m + 1) + WSLOTS)
                        act.activation(blocks[r][:, :, 2 * m * WD:2 * (m + 1) * WD].rearrange("p a (w d) -> p a w d", w=2),
                                       ps[:, two:two + 2, 0:WCOLS].rearrange("p w (d a) -> p a w d", a=J), ACT.Copy)\
                            .then_inc(block_part, 1)
                        act.wait_ge(block_part, (WB // 2) * j + m + 1)
                        act.sem_inc(bank_free, 1)
                        if m % 2 == 1 and not (last and m == WB // 2 - 1):
                            one_hot(QUADS * j + m // 2 + 1)

                def one_hot(n):
                    act.wait_ge(win_counted, WSLOTS * (n + 1))
                    act.activation(squares, iota_w[:, :], ACT.Square, scale=-1.0,
                                   bias=keyT_a[:, WT - 1, bass.ds(WSLOTS * n + WSLOTS - 1, 1)]).then_inc(square_ready, 1)
                    act.wait_ge(square_ready, n + 1)
                    act.activation(hot_a[:, WSLOTS - 1, WT - 1, :], squares, ACT.Relu, scale=-1.0, bias=ones[:, 0:1])\
                        .then_inc(act_hot_ready, 1)

                exponential(0, first_parts)
                one_hot(0)
                with act.Fori(0, J // 2) as i:
                    for r in range(2):
                        fill_block(2 * i + r, r)
                fill_block(J - 1, 0, last=True)
                layer_product(0)
                with act.Fori(0, LAYERS - 1) as m:
                    exponential(m + 1, parts)
                    layer_product(m + 1)

            act.wait_ge(way_known, 1)
            counts = act.to_reg(act.value_load(use_counts[0:1, 0:1], min_val=0, max_val=1))
            with act.If_ne(counts, 0):
                by_counts()
            with act.Else():
                by_edges()
            sqrt(NORM_P)
            node_phase(G_TABLE, D, func=ACT.Relu)
            with act.Fori(0, NB) as i:
                b = i * SLOTS
                for k in range(SLOTS):
                    act.wait_ge(e1.xt_done, b + k + 1 + SLOTS)
                    act.activation(bufA[:, k, :], xT[k], ACT.Silu).then_inc(e1.silu1_done, 1)
                for k in range(SLOTS):
                    act.wait_ge(e1.w2_done, b + k + 1)
                    act.wait_ge(e1.scan_done, b + k + 1)
                    act.activation(bufB[:, k, :], xT[k], ACT.Silu, bias=W("b2")).then_inc(e1.silu2_done, 1)
                copy_out(e1, i)
            node_phase(G_SUM, HID)
            node_phase(G_UPDATE, 2 * D)
            sqrt(NORM_U)
            act.wait_ge(gate_in, 1)
            act.activation(ybuf[:, :, :], ybuf[:, :, :], ACT.Sigmoid).then_inc(gate_done, 1)
            node_phase(G_OUT, HID, func=ACT.Silu, scale=W("ln1_g"), bias=W("ln1_b"))
            sqrt(NORM_O)

        @block.vector
        def _(dve):
            class Chain:
                def __init__(self, s, base=0):
                    self.s, self.base, self.n = s, base, 0

                def __call__(self, ins):
                    self.n += 1
                    ins.then_inc(self.s, 1)
                    dve.wait_ge(self.s, self.base + self.n)

            def per_node(a, n):
                return a.unsqueeze(2).to_broadcast([P, a.shape[1], n])

            def per_feature(a, reps):
                return a.unsqueeze(1).to_broadcast([P, reps, a.shape[1]])

            def center(link, a):
                r, n, width = a.shape
                m = var[0:r, 0:n]
                link(dve.tensor_reduce(m, a, AX.X, ALU.add))
                link(dve.tensor_scalar(m, m, 1.0 / width, None, ALU.mult))
                link(dve.tensor_tensor(a, a, m.unsqueeze(2).to_broadcast([r, n, width]), ALU.subtract))

            def subtract_mean(link, v, width):
                link(dve.tensor_reduce(mean[:, :], v, AX.X, ALU.add))
                link(dve.tensor_scalar(mean[:, :], mean[:, :], 1.0 / width, None, ALU.mult))
                link(dve.tensor_tensor(v, v, per_node(mean[:, :], width), ALU.subtract))

            def sum_squares(link, v, tmp):
                link(dve.tensor_tensor(tmp, v, v, ALU.mult))
                link(dve.tensor_reduce(var[:, :], tmp, AX.X, ALU.add))

            def inverse_deviation(link, n, width):
                dve.tensor_scalar(var[:, :], var[:, :], 1.0 / width, LN_EPS, ALU.mult, ALU.add).then_inc(var_ready, 1)
                dve.wait_ge(sd_ready, n)
                link(dve.reciprocal(rstd[:, :], rstd[:, :]))

            def scale_by_rstd(link, v, width):
                link(dve.tensor_tensor(v, v, per_node(rstd[:, :], width), ALU.mult))

            def group(buf, g):
                return buf[:, bass.ds(g * GT, GT), :]

            def product(bank, cols):
                return ps[:, bank:bank + 2, :].rearrange("p b c -> p (b c)")[:, 0:GT * cols]\
                    .rearrange("p (t c) -> p t c", c=cols)

            def node_phase(n0, stage_group, use_group, square=None):
                def restage(g, s):
                    dve.wait_ge(node_turned, n0 + g - 1)
                    stage_in(g, s)

                def use(g, s):
                    dve.wait_ge(node_product, n0 + g + 3)
                    use_group(g, s).then_inc(node_used, 1)
                    if square:
                        first, v, squared = square
                        dve.wait_ge(node_used, n0 + g + 3)
                        dve.tensor_tensor(group(squared, g), group(v, g), group(v, g), ALU.mult).then_inc(squares_summed, 1)
                        dve.wait_ge(squares_summed, 2 * (first + g) + 1)
                        dve.tensor_reduce(var[:, bass.ds(g * GT, GT)], group(squared, g), AX.X, ALU.add).then_inc(squares_summed, 1)

                def stage_in(g, s):
                    stage_group(g, s).then_inc(node_staged, 1)

                stage_in(0, 0)
                stage_in(1, 1)
                with dve.Fori(0, (NG - 3) // 2) as i:
                    for s in range(2):
                        restage(2 * i + s + 2, s)
                        use(2 * i + s, s)
                restage(NG - 1, 0)
                use(NG - 3, 0)
                use(NG - 2, 1)
                use(NG - 1, 0)
                dve.wait_ge(node_used, n0 + NG + 2)
                if square:
                    dve.wait_ge(squares_summed, 2 * (square[0] + NG))
                dve.sem_inc(alone["dve"], 1)

            dve.sem_inc(node_used, 2)
            link = Chain(setup)
            dve.sem_inc(e0.scan_done, SLOTS)
            dve.sem_inc(e1.scan_done, SLOTS)
            dve.wait_ge(ids_ready, 4)
            link(dve.tensor_copy(node_no[:, :], end_idx[:, :]))
            link(dve.tensor_copy(win_base[:, :], win_no[:, :]))
            link(dve.tensor_scalar(win_last[:, 0:WG], win_base[:, :], float(WD), -1.0, ALU.mult, ALU.add))
            link(dve.tensor_scalar(win_last[:, WG:2 * WG], win_base[:, :], -float(WD), -(WD - 0.5), ALU.mult, ALU.add))
            dve.tensor_scalar(after_node[:, :], node_no[:, :], -1.0, -0.5, ALU.mult, ALU.add).then_inc(nodes_ready, 1)
            dve.wait_ge(edges_loaded, 3 * DMA)
            hi = starts.bitcast(I32)
            link(dve.tensor_scalar(hi, src_l, 7, None, ALU.logical_shift_right))
            link(dve.scalar_tensor_tensor(pack, dst_l, float(J), hi, ALU.mult, ALU.add))
            link(dve.tensor_scalar(pack, pack, 7, None, ALU.logical_shift_left))
            link(dve.tensor_scalar(hi, src_l, P - 1, None, ALU.bitwise_and))
            dve.tensor_tensor(pack, pack, hi, ALU.bitwise_or).then_inc(pack_ready, 1)
            dve.wait_ge(pack_ready, 1)
            junk = hbuf[:, :, :].rearrange("p j d -> p (j d)")[:, 0:ET]

            for c in range(WG):
                link(dve.tensor_scalar(junk, firsts, win_last[:, c:c + 1], 0.0, ALU.is_le, ALU.add, accum_out=win_tile[:, c:c + 1]))
            link(dve.tensor_scalar(win_tile[:, 0:WG], win_tile[:, 0:WG], -1.0, 0.0, ALU.add, ALU.max))
            dve.tensor_copy(win_int[:, 0:WG], win_tile[:, 0:WG]).then_inc(win_tile_known, 1)

            def search_edges(a, tile_rows):
                to = win_edge[0:WQ, a:a + WG]
                link(dve.tensor_tensor(win_upto, tile_rows, win_last[0:WQ, a:a + WG].unsqueeze(2).to_broadcast([WQ, WG, P]), ALU.is_le))
                link(dve.tensor_reduce(to, win_upto, AX.X, ALU.add))
                link(dve.scalar_tensor_tensor(to, win_tile[0:WQ, a:a + WG], float(P), to, ALU.mult, ALU.add))

            link(dve.tensor_copy(step_f[:, :], step_i[:, :]))
            dve.wait_ge(win_tile_known, 1)
            dve.wait_ge(win_fetched, WG * DMA)
            search_edges(0, win_rows)
            link(dve.tensor_copy(win_int[0:WQ, 0:WG], win_edge[0:WQ, 0:WG]))
            link(dve.tensor_scalar(win_int[0:WQ, 0:WG], win_int[0:WQ, 0:WG], GE.bit_length() - 1, None, ALU.logical_shift_right))
            link(dve.tensor_copy(rstd[0:WQ, 0:WG], win_int[0:WQ, 0:WG]))
            link(dve.tensor_tensor(gran_f[0:WQ, :, :], rstd[0:WQ, 0:WG].unsqueeze(2).to_broadcast([WQ, WG, WT]),
                                   step_f[0:WQ, :].unsqueeze(1).to_broadcast([WQ, WG, WT]), ALU.add))
            dve.tensor_copy(gran[0:WQ, :, :], gran_f[0:WQ, :, :]).then_inc(gran_known, 1)
            last_tile = win_tile[:, WG:2 * WG]
            dve.wait_ge(win_searched, WG)
            link(dve.tensor_scalar(win_last[:, WG:2 * WG], win_last[:, WG:2 * WG], -1.0, -0.5, ALU.mult, ALU.add))
            link(dve.tensor_scalar(last_tile, last_tile, -0.5, ET / 2 - 1.0, ALU.mult, ALU.add))
            link(dve.tensor_scalar(last_tile, last_tile, 0.0, None, ALU.max))
            dve.tensor_copy(win_int[:, WG:2 * WG], last_tile).then_inc(win_end_known, 1)

            dve.wait_ge(loaded, LOADS * DMA)
            link(dve.tensor_tensor(starts, dst_l, prev_l, ALU.not_equal))
            dve.tensor_scalar(drop_l, starts, -BIG, None, ALU.mult).then_inc(masks_ready, 1)
            dve.tensor_scalar(keep_l, starts, -1.0, 1.0, ALU.mult, ALU.add).then_inc(masks_ready, 1)

            link(dve.tensor_scalar(win_base[:, :], win_base[:, :], float(WCOLS), None, ALU.mult))
            link(dve.tensor_copy(iota_w[:, :], iota_i[:, :]))
            link(dve.tensor_copy(iota_s[:, :, :], iota_i[:, 0:P].unsqueeze(2).to_broadcast([P, P, QUAD])))
            link(dve.scalar_tensor_tensor(bound[:, :], V("gamma"), -1.0, V("gamma"), ALU.mult, ALU.max))
            babs = stage[:, 0, 0:LAYERS, 0:D]
            beta = V("beta").rearrange("p (l d) -> p l d", l=LAYERS)
            by_layer = bound[:, :].rearrange("p (l d) -> p l d", l=LAYERS)
            link(dve.scalar_tensor_tensor(babs, beta, -1.0, beta, ALU.mult, ALU.max))
            link(dve.scalar_tensor_tensor(by_layer, by_layer, NORM_MAX, babs, ALU.mult, ALU.add))
            link(dve.tensor_scalar(bound[:, :], bound[:, :], 0.5, None, ALU.mult))
            link(dve.memset(peak[:, :], 0.0))
            link(dve.tensor_reduce(peak[:, 1:2], bound[:, :], AX.X, ALU.max))
            link(dve.tensor_scalar(peak[:, 1:2], peak[:, 1:2], 0.5 * MAX_RANGE, None, ALU.is_gt))

            in_link = Chain(chain["in"])
            dve.wait_ge(masks_stored, 6 * DMA)
            in_link(dve.tensor_copy(ybuf[:, :, :], xres[:, :, :]))
            subtract_mean(in_link, ybuf[:, :, :], D)
            sum_squares(in_link, ybuf[:, :, :], carve(0, J * D).rearrange("p (j d) -> p j d", j=J))
            inverse_deviation(in_link, NORM_IN, D)
            node_phase(G_IN, lambda g, s: dve.tensor_tensor(stage[:, s, :, 0:D], group(ybuf, g),
                                                            per_node(rstd[:, bass.ds(g * GT, GT)], D), ALU.mult),
                       lambda g, s: dve.tensor_tensor(group(hbuf, g), product(4 + 2 * s, D), per_feature(V("b_in"), GT), ALU.add))
            dve.sem_inc(h_ready, 1)

            dve.wait_ge(win_end_fetched, WG * DMA)
            search_edges(WG, win_end_rows)
            link(dve.tensor_tensor(win_edge[0:WQ, 0:WG], win_edge[0:WQ, WG:2 * WG], win_edge[0:WQ, 0:WG], ALU.subtract))
            link(dve.tensor_reduce(peak[0:WQ, 0:1], win_edge[0:WQ, 0:WG], AX.X, ALU.max))
            link(dve.tensor_scalar(peak[0:WQ, 0:1], peak[0:WQ, 0:1], float(MAX_WINDOW), None, ALU.is_gt))
            link(dve.tensor_tensor(peak[:, 3:4], peak[:, 0:1], peak[:, 1:2], ALU.add))

            def node_ends():
                link = Chain(degrees_ready)
                dve.wait_ge(tile_fetched, J * DMA)
                link(dve.tensor_tensor(wide[:, :, :], wide[:, :, :].bitcast(I32), per_node(node_no[:, :], P), ALU.is_le))
                link(dve.tensor_reduce(var[:, :], wide[:, :, :], AX.X, ALU.add))
                dve.scalar_tensor_tensor(end_f[:, :], end_tile[:, :], float(P), var[:, :], ALU.mult, ALU.add).then_inc(end_known, 1)
                dve.wait_ge(end_known, 1)
                link(dve.tensor_scalar(var[:, :], end_f[:, :], -1.0, 0.0, ALU.add, ALU.max))
                dve.tensor_copy(end_idx[:, :], var[:, :]).then_inc(ends_known, 1)
                dve.wait_ge(start_summed, 1)
                dve.tensor_copy(start_f[:, :], ps[:, 2, 0:J]).then_inc(starts_read, 1)
                dve.wait_ge(starts_read, 1)
                link(dve.tensor_tensor(degree[:, :], end_f[:, :], start_f[:, :], ALU.subtract))
                link(dve.tensor_scalar(has[:, :], degree[:, :], 1.0, None, ALU.min))

            link = Chain(chain["way"])
            byf = hbuf[:, :, :].rearrange("p j d -> p d j")
            link(dve.tensor_reduce(extreme[:, 0:D], byf, AX.X, ALU.max))
            link(dve.tensor_reduce(extreme[:, D:2 * D], byf, AX.X, ALU.min))
            dve.tensor_scalar(extreme[:, D:2 * D], extreme[:, D:2 * D], -1.0, None, ALU.mult).then_inc(ext_ready, 1)
            dve.wait_ge(ext_turned, 1)
            link(dve.tensor_reduce(rstd[:, 0:1], ps[:, 0, 0:P], AX.X, ALU.max))
            dve.tensor_scalar(diag[:, :], ident[:, :], rstd[:, 0:1], None, ALU.mult).then_inc(diag_ready, 2)
            dve.wait_ge(ext_spread, 2)
            link(dve.tensor_copy(diag[:, :], ps[:, 1, 0:2 * D]))
            link(dve.tensor_copy(shift_c[:, :], diag[:, 0:D]))
            link(dve.tensor_tensor(diag[:, 0:D], diag[:, 0:D], diag[:, D:2 * D], ALU.add))
            link(dve.tensor_reduce(rstd[:, 0:1], diag[:, 0:D], AX.X, ALU.max))
            link(dve.tensor_scalar(rstd[:, 0:1], rstd[:, 0:1], MAX_RANGE, None, ALU.is_le))
            link(dve.tensor_scalar(rstd[:, 1:2], ps[:, 2, 0:1], 0.0, None, ALU.is_equal))
            link(dve.tensor_tensor(rstd[:, 0:1], rstd[:, 0:1], rstd[:, 1:2], ALU.mult))
            dve.tensor_copy(use_counts[:, :], rstd[:, 0:1]).then_inc(way_known, 1)
            dve.wait_ge(way_known, 1)

            center_link = Chain(centered)
            for a in (W("w_l"), V("b_l")):
                center(center_link, a.rearrange("p (l c) -> p l c", l=LAYERS))

            def find_tiles():
                link = Chain(node_tiles)
                dve.wait_ge(nodes_searched, J)
                link(dve.tensor_scalar(mean[:, :], sign_sum[:, :], -0.5, ET / 2 - 1.0, ALU.mult, ALU.add))
                link(dve.tensor_scalar(mean[:, :], mean[:, :], 0.0, None, ALU.max))
                link(dve.tensor_copy(end_tile[:, :], mean[:, :]))
                dve.tensor_copy(end_idx[:, :], mean[:, :]).then_inc(tile_known, 1)

            def layer_tail(l):
                link = Chain(chain["l"], l * LAYER_LINKS)
                bias = rowvec[:, bass.ds(l * D + V_COLS["b_l"][0], D)]

                def stage_group(g, s):
                    dve.tensor_copy(stage[:, s, :, 0:D], group(hbuf, g))
                    return dve.tensor_tensor(stage[:, s, :, D:2 * D], group(ends, g)[:, :, 0:D],
                                             per_node(has[:, bass.ds(g * GT, GT)], D), ALU.mult)

                node_phase(l * NG + G_LAYER, stage_group,
                           lambda g, s: dve.tensor_tensor(group(ybuf, g), product(4 + 2 * s, D), per_feature(bias, GT), ALU.add),
                           square=(l * NG, ybuf, ends[:, :, D:P]))
                inverse_deviation(link, NORM_L + l, D)
                scale_by_rstd(link, ybuf[:, :, :], D)
                for name, op in (("gamma", ALU.mult), ("beta", ALU.add)):
                    row = rowvec[:, bass.ds(l * D + V_COLS[name][0], D)]
                    link(dve.tensor_tensor(ybuf[:, :, :], ybuf[:, :, :], per_feature(row, J), op))
                link(dve.tensor_scalar(ybuf[:, :, :], ybuf[:, :, :], 0.0, 0.5, ALU.max, ALU.mult))
                dve.scalar_tensor_tensor(hbuf[:, :, :], hbuf[:, :, :], 0.5, ybuf[:, :, :], ALU.mult, ALU.add)\
                    .then_inc(h_ready, 1)
                dve.wait_ge(h_ready, l + 2)
                dve.sem_inc(alone["dve"], 1)
                assert link.n == LAYER_LINKS

            def by_edges():
                find_tiles()
                node_ends()
                dve.memset(top[:, 0:1], 0.0).then_inc(e0.top_carried, 1)
                dve.memset(scan[:, 0:1], 0.0).then_inc(e0.scan_carried, 1)
                with dve.Fori(0, LAYERS) as l:
                    with dve.Fori(0, NB) as i:
                        c = l * NB + i
                        b = c * SLOTS
                        for k in range(SLOTS):
                            lo, hi = k * BE, (k + 1) * BE
                            mask, fall = segmask[0:D, k, :], bufA[0:D, k, :]
                            dve.wait_ge(e0.xt_done, b + k + 1 + SLOTS)
                            dve.wait_ge(e0.mask_loaded[k], DMA * (c + 1))
                            dve.wait_ge(e0.back_done, b + k + 1)
                            if k == 0:
                                dve.wait_ge(e0.top_carried, c + 1)
                            else:
                                dve.wait_ge(e0.top_done, b + k)
                            dve.tensor_tensor_scan(top[:, lo + 1:hi + 1], mask, xT[k][0:D, :], top[:, lo:lo + 1],
                                                   ALU.add, ALU.max).then_inc(e0.top_done, 1)
                            dve.wait_ge(e0.top_done, b + k + 1)
                            dve.wait_ge(e0.scan_done, b + k + 1)
                            dve.tensor_tensor(fall, top[:, lo:hi], top[:, lo + 1:hi + 1], ALU.subtract).then_inc(e0.diff_done, 1)
                            dve.wait_ge(e0.diff_done, b + k + 1)
                            dve.tensor_tensor(fall, fall, mask, ALU.add).then_inc(e0.fall_done, 1)
                        dve.tensor_copy(top[:, 0:1], top[:, BODY:BODY + 1]).then_inc(e0.top_carried, 1)
                        for k in range(SLOTS):
                            lo, hi = k * BE, (k + 1) * BE
                            dve.wait_ge(e0.decay_done, b + k + 1)
                            dve.wait_ge(e0.term_done, b + k + 1 + SLOTS)
                            if k == 0:
                                dve.wait_ge(e0.scan_carried, c + 1)
                            else:
                                dve.wait_ge(e0.scan_done, b + k + SLOTS)
                            dve.tensor_tensor_scan(scan[0:D, lo + 1:hi + 1], bufA[0:D, k, :], bufB[0:D, k, :],
                                                   scan[0:D, lo:lo + 1], ALU.mult, ALU.add).then_inc(e0.scan_done, 1)
                        dve.wait_ge(e0.scan_done, b + SLOTS + SLOTS)
                        dve.tensor_copy(scan[0:D, 0:1], scan[0:D, BODY:BODY + 1]).then_inc(e0.scan_carried, 1)

                    link = Chain(chain["agg"], l)
                    dve.wait_ge(e0.ends_fetched, (l + 1) * (J * DMA))
                    dve.tensor_scalar(ends[:, :, D:P], ends[:, :, D:P], SUM_EPS, None, ALU.max).then_inc(floored, 1)
                    dve.wait_ge(ln_done, l + 1)
                    link(dve.tensor_tensor(ends[:, :, 0:D], ends[:, :, 0:D], ends[:, :, D:P], ALU.add))
                    dve.sem_inc(alone["dve"], 1)
                    layer_tail(l)
                dve.wait_ge(h_stored, DMA * (LAYERS + 1))

            def by_counts():
                dve.wait_ge(gran_fetched, WG * WT * DMA)
                link = Chain(chain["way"], WAY_LINKS)
                ka, kb = key_a.bitcast(I32), key_b.bitcast(I32)
                link(dve.tensor_scalar(ka, win_edges, 7, None, ALU.logical_shift_right))
                link(dve.tensor_scalar(kb, win_edges, P - 1, None, ALU.bitwise_and))
                by_window = key_a.rearrange("p (g e) -> p g e", g=WG)
                dve.tensor_tensor(by_window, ka.rearrange("p (g e) -> p g e", g=WG),
                                  win_base[0:WQ, :].unsqueeze(2).to_broadcast([WQ, WG, WE]), ALU.subtract)\
                    .then_inc(keys_ready, 1)
                dve.tensor_copy(key_b, kb).then_inc(keys_ready, 1)
                def make_parts(l, out):
                    part = [out[:, :, n * D:(n + 1) * D] for n in range(PARTS)]
                    for a, b in HALVES:
                        dve.tensor_tensor(ybuf[:, a:b, :], hbuf[:, a:b, :], per_feature(shift_c[:, :], b - a), ALU.subtract)\
                            .then_inc(exp_in, 1)
                    for n, (a, b) in enumerate(HALVES):
                        dve.wait_ge(exp_done, 2 * l + n + 1)
                        dve.tensor_tensor(ybuf[:, a:b, :], ends[:, a:b, 0:D], part[0][:, a:b, :], ALU.subtract).then_inc(rest_ready, 1)
                    for n, (a, b) in enumerate(HALVES):
                        dve.wait_ge(part_done, 2 * l + n + 1)
                        dve.tensor_tensor(part[2][:, a:b, :], ybuf[:, a:b, :], part[1][:, a:b, :], ALU.subtract).then_inc(parts_ready, 1)

                def read_sums(l, j, r):
                    dve.wait_ge(block_used, l * J + j + 1 + RING)
                    dve.tensor_reduce(ends[:, bass.ds(j, 1), D:P].rearrange("p o d -> p (o d)"),
                                      ps[:, r % 2, 0:PARTS * D].rearrange("p (n d) -> p d n", n=PARTS), AX.X, ALU.add)\
                        .then_inc(sums_read, 1)

                def aggregate(l):
                    link = Chain(chain["agg"], 2 * l)
                    dve.wait_ge(sums_read, J * (l + 1) + 2)
                    dve.tensor_scalar(ends[:, :, D:P], ends[:, :, D:P], LEAST_SUM, None, ALU.max).then_inc(floored, 1)
                    dve.wait_ge(ln_done, l + 1)
                    link(dve.tensor_tensor(ends[:, :, 0:D], ends[:, :, D:P], per_feature(shift_c[:, :], J), ALU.add))
                    link(dve.scalar_tensor_tensor(shift_c[:, :], shift_c[:, :], 0.5, bound[:, bass.ds(l * D, D)], ALU.mult, ALU.add))
                    dve.sem_inc(alone["dve"], 1)

                def source_hots(w, slot):
                    keys = keyT_b[:, bass.ds(w, WSLOTS), :].rearrange("p w i -> p (w i)")
                    dve.tensor_tensor(hot_b[slot], iota_s[:, :, :], keys.unsqueeze(1).to_broadcast([P, P, QUAD]),
                                      ALU.is_equal).then_inc(src_hot_ready, 1)

                def one_hots(j):
                    for q in range(QUADS):
                        for s in range(WSLOTS):
                            w = WB * j + WSLOTS * q + s
                            if s % 2 == 0:
                                dve.wait_ge(win_counted, w + 2)
                            if s == 2:
                                source_hots(WB * j + WSLOTS * (q + 1), (q + 1) % 2)
                            for t in range(min(WT, DVE_HOTS - WT * s)):
                                dve.tensor_scalar(hot_a[:, s, t, :], iota_w[:, :], keyT_a[:, t, bass.ds(w, 1)], None, ALU.is_equal)\
                                    .then_inc(hot_ready, 1)

                dve.memset(keyT_b[:, NW:NW + WSLOTS, :], 0.0)
                dve.wait_ge(keys_copied, 4 * WT)
                make_parts(0, first_parts)
                find_tiles()
                dve.sem_inc(sums_read, 2)
                source_hots(0, 0)
                one_hots(0)
                with dve.Fori(0, J // 2) as i:
                    for r in range(2):
                        one_hots(2 * i + r + 1)
                        read_sums(0, 2 * i + r, r)
                node_ends()
                read_sums(0, J - 1, 0)
                aggregate(0)
                layer_tail(0)
                with dve.Fori(0, LAYERS - 1) as m:
                    l = m + 1
                    make_parts(l, parts)
                    with dve.Fori(0, BODIES) as i:
                        for r in range(RING):
                            read_sums(l, RING * i + r, r)
                    read_sums(l, J - 1, 0)
                    aggregate(l)
                    layer_tail(l)

            assert link.n == WAY_LINKS
            counts = dve.to_reg(dve.value_load(use_counts[0:1, 0:1], min_val=0, max_val=1))
            with dve.If_ne(counts, 0):
                by_counts()
            with dve.Else():
                by_edges()

            link = Chain(chain["p"])
            dve.tensor_tensor(ybuf[:, :, :], xres[:, :, :], hbuf[:, :, :], ALU.add).then_inc(x_ready, 1)
            dve.wait_ge(x_ready, 1)
            subtract_mean(link, ybuf[:, :, :], D)
            sum_squares(link, ybuf[:, :, :], wide[:, :, 0:D])
            inverse_deviation(link, NORM_P, D)
            dve.memset(scan[:, 0:1], 0.0).then_inc(e1.scan_carried, 1)
            node_phase(G_TABLE, lambda g, s: dve.tensor_tensor(stage[:, s, :, 0:D], group(ybuf, g),
                                                               per_node(rstd[:, bass.ds(g * GT, GT)], D), ALU.mult),
                       lambda g, s: dve.tensor_tensor(group(wide, g), product(4 + 2 * s, HID), per_feature(V("b1"), GT), ALU.add))
            link(dve.tensor_copy(idx[:, :, :].rearrange("p k t -> p (k t)"), src_all[:, 0:SLOTS * TB]))
            dve.sem_inc(e1.idx_ready, SLOTS)
            link(dve.tensor_tensor(xres[:, :, :], xres[:, :, :], hbuf[:, :, :], ALU.add))
            scale_by_rstd(link, ybuf[:, :, :], D)
            link(dve.tensor_scalar(hbuf[:, :, :], ybuf[:, :, :], 0.0, None, ALU.max))
            dve.tensor_tensor(xres[:, :, :], xres[:, :, :], hbuf[:, :, :], ALU.add).then_inc(x_summed, 1)
            for a in (W("U1"), V("ub1"), W("U2"), V("ub2")):
                center(center_link, a.unsqueeze(1))

            with dve.Fori(0, NB) as i:
                b = i * SLOTS
                for k in range(SLOTS):
                    dve.wait_ge(e1.xt_done, b + k + 1 + SLOTS)
                    dve.tensor_copy(idx[:, k, :], src_all[:, bass.ds((i + 1) * (SLOTS * TB) + k * TB, TB)])\
                        .then_inc(e1.idx_ready, 1)
                for k in range(SLOTS):
                    lo, hi = k * BE, (k + 1) * BE
                    dve.wait_ge(e1.mask_loaded[k], DMA * (i + 1))
                    dve.wait_ge(e1.silu2_done, b + k + 1 + SLOTS)
                    dve.wait_ge(e1.back_done, b + k + 1)
                    if k == 0:
                        dve.wait_ge(e1.scan_carried, i + 1)
                    else:
                        dve.wait_ge(e1.scan_done, b + k + SLOTS)
                    dve.tensor_tensor_scan(scan[:, lo + 1:hi + 1], segmask[:, k, :], bufB[:, k, :], scan[:, lo:lo + 1],
                                           ALU.mult, ALU.add).then_inc(e1.scan_done, 1)
                dve.wait_ge(e1.scan_done, b + SLOTS + SLOTS)
                dve.tensor_copy(scan[:, 0:1], scan[:, BODY:BODY + 1]).then_inc(e1.scan_carried, 1)

            link = Chain(chain["s"])
            link(dve.tensor_tensor(ybuf[:, :, :], per_node(degree[:, :], D), per_feature(V("b3"), J), ALU.mult))
            def stage_sums(g, s):
                dve.wait_ge(e1.ends_ready, g + 1)
                return dve.tensor_tensor(stage[:, s, :, :], group(ends, g), per_node(has[:, bass.ds(g * GT, GT)], P), ALU.mult)

            node_phase(G_SUM, stage_sums,
                       lambda g, s: dve.tensor_tensor(group(ybuf, g), product(4 + 2 * s, D), group(ybuf, g), ALU.add))
            def stage_group(g, s):
                dve.tensor_copy(stage[:, s, :, 0:D], group(hbuf, g))
                return dve.tensor_copy(stage[:, s, :, D:2 * D], group(ybuf, g))

            def use_group(g, s):
                dve.tensor_tensor(group(wide, g), product(4, HID), per_feature(V("ub1"), GT), ALU.add)
                return dve.tensor_tensor(group(ybuf, g), product(6, D), per_feature(V("gb"), GT), ALU.add)

            node_phase(G_UPDATE, stage_group, use_group, square=(LAYERS * NG, wide, ends))
            dve.sem_inc(gate_in, 1)
            link = Chain(chain["u"])
            inverse_deviation(link, NORM_U, HID)
            node_phase(G_OUT, lambda g, s: dve.tensor_tensor(stage[:, s, :, :], group(wide, g),
                                                             per_node(rstd[:, bass.ds(g * GT, GT)], HID), ALU.mult),
                       lambda g, s: dve.tensor_tensor(group(ends, g)[:, :, 0:D], product(4 + 2 * s, D), per_feature(V("ub2"), GT), ALU.add),
                       square=((LAYERS + 1) * NG, ends[:, :, 0:D], ends[:, :, D:P]))
            link = Chain(chain["o"])
            upd = ends[:, :, 0:D]
            inverse_deviation(link, NORM_O, D)
            scale_by_rstd(link, upd, D)
            dve.wait_ge(gate_scaled, 3)
            link(dve.tensor_tensor(upd, upd, ybuf[:, :, :], ALU.mult))
            dve.tensor_tensor(xres[:, :, :], upd, hbuf[:, :, :], ALU.add).then_inc(y_ready, 1)


LAYER_LINKS = 5
WAY_LINKS = 10


def kernel(**inputs):
    import numpy as np
    import concourse.bacc as bacc
    from concourse.bass_utils import run_bass_kernel_spmd

    a = {k: np.asarray(v) for k, v in inputs.items()}
    f32, i32 = np.float32, np.int32
    x = np.zeros((NPAD, D), f32)
    x[:N_NODES] = a["x"]
    src = np.zeros(EPAD, i32)
    src[:N_EDGES] = a["src"]
    dst = np.full(EPAD, NPAD, i32)
    dst[:N_EDGES] = a["dst"]
    prev = np.full(EPAD, -1, i32)
    prev[1:] = dst[:-1]
    attr = np.zeros((N_ATTR, EPAD + BODY), f32)
    attr[:9, :N_EDGES] = a["edge_attr_9"].T
    attr[9:, :N_EDGES] = a["edge_attr_8"].T
    g1, g0 = "L1_gnn_", "L0_gnn_"
    parts = {"w_l": np.concatenate([a[g0 + "W_l"][l].T for l in range(LAYERS)], axis=1), "w_in": a[g0 + "W_in"].T,
             "W1x": a[g1 + "W1"][:D], "W1e": a[g1 + "W1"][D:], "W2": a[g1 + "W2"], "W3": a[g1 + "W3"],
             "U1": a[g1 + "U1"], "U2": a[g1 + "U2"], "G": a[g1 + "G"], "b2": a[g1 + "b2"].reshape(HID, 1),
             "ln1_g": a[g1 + "ln1_g"].reshape(HID, 1), "ln1_b": a[g1 + "ln1_b"].reshape(HID, 1)}
    w = np.zeros((P, W_TOTAL), f32)
    for name, (at, r, c) in W_COLS.items():
        w[:r, at:at + c] = parts[name]
    rowsv = {"b_in": a[g0 + "b_in"], "b_l": a[g0 + "b_l"], "gamma": a[g0 + "gamma_l"], "beta": a[g0 + "beta_l"]}
    rowsv.update({n: a[g1 + n] for n in ("b1", "b3", "ub1", "ub2", "ln2_g", "ln2_b", "gb")})
    v = np.concatenate([rowsv[n].reshape(-1) for n in V_COLS]).reshape(1, V_TOTAL)
    arrays = {"x_in": np.ascontiguousarray(x.reshape(J, P, D).transpose(1, 0, 2)),
              "dst_in": dst.reshape(1, EPAD), "prev_in": prev.reshape(1, EPAD),
              "first_in": np.ascontiguousarray(dst[::P]).reshape(1, ET),
              "src_in": np.concatenate([src.reshape(ET, P).T, np.zeros((P, SLOTS * TB), i32)], axis=1),
              "srcl_in": src.reshape(1, EPAD), "attr_in": attr, "w_in": w, "v_in": v}

    nc = bacc.Bacc("TRN2", target_bir_lowering=False, num_devices=1)
    args = [nc.dram_tensor(n, t.shape, mybir.dt.from_np(t.dtype), kind="ExternalInput").ap() for n, t in arrays.items()]
    out = nc.dram_tensor("out", (P, J, D), F32, kind="ExternalOutput").ap()
    build(nc, *args, out)
    r = run_bass_kernel_spmd(nc, [arrays], core_ids=[0])
    return r.results[0]["out"].transpose(1, 0, 2).reshape(NPAD, D)[:N_NODES]
```
